# Optimizing a Trainium2 kernel written in Bass

```python
import numpy as np
import jax
import jax.numpy as jnp

def _softmax(x, axis=-1):
    return jax.nn.softmax(x, axis=axis)

def _gelu(x):
    return jax.nn.gelu(x, approximate=True)

def _silu(x):
    return jax.nn.silu(x)

def _sigmoid(x):
    return jax.nn.sigmoid(x)

def _layernorm(x, axis=-1, eps=1e-05):
    m = jnp.mean(x, axis=axis, keepdims=True)
    v = jnp.var(x, axis=axis, keepdims=True)
    return (x - m) / jnp.sqrt(v + eps)

def _scatter_add(tgt, idx, src, axis=0):
    return tgt.at[idx].add(src)

def _segment_sum(src, seg, n):
    return jax.ops.segment_sum(src, seg, n)
kernel_name = 'mk_xattn_seq_d4_seqx_r4_3203ae'

def setup_inputs(seed: int=0):
    np.random.seed(seed)
    _w = jnp.asarray

    def _rec_inputs():
        import jax
        import jax.numpy as jnp
        _rk = jax.random.key(seed)
        x = -0.0005207 + 1.001 * jax.random.normal(jax.random.fold_in(_rk, 1), (16, 128, 256), jnp.float32)
        _lenS = 128 - jax.random.randint(jax.random.fold_in(_rk, 7), (16,), 0, max(1, 128 // 4) + 1, jnp.int32)
        _lenS2 = 128 - jax.random.randint(jax.random.fold_in(_rk, 8), (16,), 0, max(1, 128 // 4) + 1, jnp.int32)
        _ctx_1024P = jax.random.normal(jax.random.fold_in(_rk, 11), (16, 16, 256), jnp.float32)
        _ctx_1024c = jax.random.dirichlet(jax.random.fold_in(_rk, 511), 0.3 * jnp.ones((16,), jnp.float32), (16, 128))
        _ctx_1024t = jnp.einsum('bsk,bkd->bsd', _ctx_1024c, _ctx_1024P)
        _ctx_1024t = _ctx_1024t * jax.lax.rsqrt(jnp.mean(jnp.square(_ctx_1024t)) + 1e-12) * 0.953939
        ctx_1024 = 4.13588e-05 + 0.999923 * (_ctx_1024t + 0.3 * jax.random.normal(jax.random.fold_in(_rk, 611), (16, 128, 256), jnp.float32))
        _validS = jnp.arange(128)[None, :] < _lenS[:, None]
        _validS2 = jnp.arange(128)[None, :] < _lenS2[:, None]
        _causal = jnp.tril(jnp.ones((128, 128), dtype=bool))
        mask_Bx1xSxS2_ff0 = jnp.where(jnp.ones((16, 1, 128, 128), dtype=bool), 0.0, -1000000000.0).astype(jnp.float32)
        return (x, ctx_1024, mask_Bx1xSxS2_ff0)
    x, ctx_1024, mask_Bx1xSxS2_ff0 = _rec_inputs()

    def _L0_xattn_setup():
        import jax, jax.numpy as jnp
        import numpy as np
        D, H, E, K, DFF = (256, 16, 8, 2, 1024)
        B, L, T = (4, 128, 512)
        EPS = 1e-05

        def _xavier(key, shape):
            fan_in, fan_out = (shape[-1], shape[-2])
            a = jnp.sqrt(6.0 / (fan_in + fan_out))
            return jax.random.uniform(key, shape, jnp.float32, -a, a)

        def _ln(x, g, b):
            m = x.mean(-1, keepdims=True)
            v = ((x - m) ** 2).mean(-1, keepdims=True)
            return (x - m) / jnp.sqrt(v + EPS) * g + b

        def _mha(q_in, kv_in, in_w, in_b, out_w, out_b):
            wq, wk, wv = jnp.split(in_w, 3, axis=0)
            bq, bk, bv = jnp.split(in_b, 3, axis=0)
            dh = D // H

            def heads(x, w, b):
                y = x @ w.T + b
                return y.reshape(x.shape[0], x.shape[1], H, dh).transpose(0, 2, 1, 3)
            q = heads(q_in, wq, bq)
            k = heads(kv_in, wk, bk)
            v = heads(kv_in, wv, bv)
            scores = jnp.einsum('bhqd,bhkd->bhqk', q, k) / jnp.sqrt(jnp.float32(dh))
            attn = jax.nn.softmax(scores, axis=-1)
            out = jnp.einsum('bhqk,bhkd->bhqd', attn, v)
            out = out.transpose(0, 2, 1, 3).reshape(q_in.shape[0], q_in.shape[1], D)
            return out @ out_w.T + out_b

        def _fuse_moe(x, ln_g, ln_b, rw, rb, fc1_w, fc1_b, fc2_w, fc2_b):
            h = _ln(x, ln_g, ln_b)
            logits = h @ rw.T + rb
            vals, idx = jax.lax.top_k(logits, K)
            gates = jax.nn.softmax(vals, axis=-1)
            N = x.shape[0] * x.shape[1]
            hf = h.reshape(N, D)
            h1 = jax.nn.gelu(jnp.einsum('nd,efd->enf', hf, fc1_w) + fc1_b[:, None, :], approximate=False)
            eo = jnp.einsum('enf,edf->end', h1, fc2_w) + fc2_b[:, None, :]
            idx_f = idx.reshape(N, K)
            gates_f = gates.reshape(N, K)
            gathered = eo[idx_f, jnp.arange(N)[:, None], :]
            mixed = (gathered * gates_f[..., None]).sum(axis=1).reshape(x.shape)
            return x + mixed
        key = jax.random.key(seed)
        ks = jax.random.split(key, 16)
        inp = {'latents': jax.random.normal(ks[0], (B, L, D), jnp.float32), 'tokens': jax.random.normal(ks[1], (B, T, D), jnp.float32), 'sa_ln_g': jnp.ones((D,)), 'sa_ln_b': jnp.zeros((D,)), 'sa_in_w': _xavier(ks[2], (3 * D, D)), 'sa_in_b': jnp.zeros((3 * D,)), 'sa_out_w': _xavier(ks[3], (D, D)), 'sa_out_b': jnp.zeros((D,)), 'ca_q_ln_g': jnp.ones((D,)), 'ca_q_ln_b': jnp.zeros((D,)), 'ca_kv_ln_g': jnp.ones((D,)), 'ca_kv_ln_b': jnp.zeros((D,)), 'ca_in_w': _xavier(ks[4], (3 * D, D)), 'ca_in_b': jnp.zeros((3 * D,)), 'ca_out_w': _xavier(ks[5], (D, D)), 'ca_out_b': jnp.zeros((D,)), 'moe_ln_g': jnp.ones((D,)), 'moe_ln_b': jnp.zeros((D,)), 'router_w': _xavier(ks[6], (E, D)), 'router_b': jnp.zeros((E,)), 'e_fc1_w': jax.vmap(lambda k: _xavier(k, (DFF, D)))(jax.random.split(ks[7], E)), 'e_fc1_b': jnp.zeros((E, DFF)), 'e_fc2_w': jax.vmap(lambda k: _xavier(k, (D, DFF)))(jax.random.split(ks[8], E)), 'e_fc2_b': jnp.zeros((E, D))}
        return inp
    _L0_xattn_all = _L0_xattn_setup()
    _L0_xattn_in = {k: v for k, v in _L0_xattn_all.items() if k in ('sa_ln_g', 'sa_ln_b', 'sa_in_w', 'sa_in_b', 'sa_out_w', 'sa_out_b', 'ca_q_ln_g', 'ca_q_ln_b', 'ca_kv_ln_g', 'ca_kv_ln_b', 'ca_in_w', 'ca_in_b', 'ca_out_w', 'ca_out_b', 'moe_ln_g', 'moe_ln_b', 'router_w', 'router_b', 'e_fc1_w', 'e_fc1_b', 'e_fc2_w', 'e_fc2_b')}
    del _L0_xattn_all

    def _L1_xattn_setup():
        import jax, jax.numpy as jnp
        import numpy as np
        TOPK = 10
        NUM_HEADS = 16
        key = jax.random.key(seed)
        ks = jax.random.split(key, 8)
        B, N, S, D = (32, 512, 512, 256)
        sc = 1.0 / np.sqrt(D)
        return {'base_hidden': jax.random.normal(ks[0], (B, N, D), jnp.float32), 'scaffold_hidden': jax.random.normal(ks[1], (B, S, D), jnp.float32), 'in_proj_w': jax.random.normal(ks[2], (3 * D, D), jnp.float32) * sc, 'in_proj_b': jax.random.normal(ks[3], (3 * D,), jnp.float32) * 0.02, 'out_w': jax.random.normal(ks[4], (D, D), jnp.float32) * sc, 'out_b': jax.random.normal(ks[5], (D,), jnp.float32) * 0.02, 'score_w': jax.random.normal(ks[6], (1, D), jnp.float32) * sc, 'score_b': jax.random.normal(ks[7], (1,), jnp.float32) * 0.02}
    _L1_xattn_all = _L1_xattn_setup()
    _L1_xattn_in = {k: v for k, v in _L1_xattn_all.items() if k in ('in_proj_w', 'in_proj_b', 'out_w', 'out_b', 'score_w', 'score_b')}
    del _L1_xattn_all

    def _L2_xattn_setup():
        import jax, jax.numpy as jnp
        import numpy as np
        import math
        H, NH, NKV, HD, FF = (256, 16, 4, 64, 1024)
        B, S = (2, 512)
        EPS, THETA = (1e-06, 10000.0)

        def _rmsnorm(x, w, eps=EPS):
            v = jnp.mean(x.astype(jnp.float32) ** 2, axis=-1, keepdims=True)
            return (x.astype(jnp.float32) * jax.lax.rsqrt(v + eps)).astype(x.dtype) * w

        def _rope_tables(seq_len, head_dim, theta=THETA):
            inv_freq = 1.0 / theta ** (jnp.arange(0, head_dim, 2, dtype=jnp.float32) / head_dim)
            freqs = jnp.arange(seq_len, dtype=jnp.float32)[:, None] * inv_freq[None, :]
            emb = jnp.concatenate([freqs, freqs], axis=-1)
            return (jnp.cos(emb), jnp.sin(emb))

        def _rotate_half(x):
            x1, x2 = jnp.split(x, 2, axis=-1)
            return jnp.concatenate([-x2, x1], axis=-1)

        def _apply_rope(x, cos, sin):
            return x * cos[None, None] + _rotate_half(x) * sin[None, None]
        key = jax.random.key(seed)
        ks = jax.random.split(key, 12)
        std = 0.02
        return {'hidden_states': jax.random.normal(ks[0], (B, S, H), jnp.float32), 'kv_states': jax.random.normal(ks[1], (B, S, H), jnp.float32), 'attention_mask': jnp.zeros((B, 1, S, S), jnp.float32), 'ln1_w': jnp.ones((H,), jnp.float32), 'ln2_w': jnp.ones((H,), jnp.float32), 'Wq': jax.random.normal(ks[2], (H, NH * HD), jnp.float32) * std, 'Wk': jax.random.normal(ks[3], (H, NKV * HD), jnp.float32) * std, 'Wv': jax.random.normal(ks[4], (H, NKV * HD), jnp.float32) * std, 'Wo': jax.random.normal(ks[5], (NH * HD, H), jnp.float32) * std, 'Wgate': jax.random.normal(ks[6], (H, FF), jnp.float32) * std, 'Wup': jax.random.normal(ks[7], (H, FF), jnp.float32) * std, 'Wdown': jax.random.normal(ks[8], (FF, H), jnp.float32) * std}
    _L2_xattn_all = _L2_xattn_setup()
    _L2_xattn_in = {k: v for k, v in _L2_xattn_all.items() if k in ('ln1_w', 'ln2_w', 'Wq', 'Wk', 'Wv', 'Wo', 'Wgate', 'Wup', 'Wdown')}
    del _L2_xattn_all

    def _L3_xattn_setup():
        import jax, jax.numpy as jnp
        import numpy as np
        D_MODEL = 256
        NUM_HEADS = 16
        HEAD_DIM = D_MODEL // NUM_HEADS
        SCALE = HEAD_DIM ** (-0.5)
        LN_EPS = 1e-05
        Q_EPS = 1e-05

        def bit_quant(W):
            gamma = jnp.mean(jnp.abs(W))
            Wq = jnp.clip(jnp.round(W / (gamma + Q_EPS)), -1.0, 1.0) * gamma
            return W + jax.lax.stop_gradient(Wq - W)

        def layer_norm(x, gamma, beta):
            mu = jnp.mean(x, axis=-1, keepdims=True)
            var = jnp.mean(jnp.square(x - mu), axis=-1, keepdims=True)
            return (x - mu) * jax.lax.rsqrt(var + LN_EPS) * gamma + beta
        key = jax.random.key(seed)
        ks = jax.random.split(key, 8)
        B, T, T_ctx, C = (4, 256, 512, D_MODEL)
        w_std = C ** (-0.5)
        return {'x': jax.random.normal(ks[0], (B, T, C), jnp.float32), 'context': jax.random.normal(ks[1], (B, T_ctx, C), jnp.float32), 'Wq': jax.random.normal(ks[2], (C, C), jnp.float32) * w_std, 'bq': jnp.zeros((C,), jnp.float32), 'Wk': jax.random.normal(ks[3], (C, C), jnp.float32) * w_std, 'bk': jnp.zeros((C,), jnp.float32), 'Wv': jax.random.normal(ks[4], (C, C), jnp.float32) * w_std, 'bv': jnp.zeros((C,), jnp.float32), 'Wo': jax.random.normal(ks[5], (C, C), jnp.float32) * w_std, 'bo': jnp.zeros((C,), jnp.float32), 'ln_gamma': jnp.ones((C,), jnp.float32), 'ln_beta': jnp.zeros((C,), jnp.float32)}
    _L3_xattn_all = _L3_xattn_setup()
    _L3_xattn_in = {k: v for k, v in _L3_xattn_all.items() if k in ('Wq', 'bq', 'Wk', 'bk', 'Wv', 'bv', 'Wo', 'bo', 'ln_gamma', 'ln_beta')}
    del _L3_xattn_all
    return {'x': x, 'ctx_1024': ctx_1024, 'mask_Bx1xSxS2_ff0': mask_Bx1xSxS2_ff0, 'L0_xattn_sa_ln_g': _L0_xattn_in['sa_ln_g'], 'L0_xattn_sa_ln_b': _L0_xattn_in['sa_ln_b'], 'L0_xattn_sa_in_w': _L0_xattn_in['sa_in_w'], 'L0_xattn_sa_in_b': _L0_xattn_in['sa_in_b'], 'L0_xattn_sa_out_w': _L0_xattn_in['sa_out_w'], 'L0_xattn_sa_out_b': _L0_xattn_in['sa_out_b'], 'L0_xattn_ca_q_ln_g': _L0_xattn_in['ca_q_ln_g'], 'L0_xattn_ca_q_ln_b': _L0_xattn_in['ca_q_ln_b'], 'L0_xattn_ca_kv_ln_g': _L0_xattn_in['ca_kv_ln_g'], 'L0_xattn_ca_kv_ln_b': _L0_xattn_in['ca_kv_ln_b'], 'L0_xattn_ca_in_w': _L0_xattn_in['ca_in_w'], 'L0_xattn_ca_in_b': _L0_xattn_in['ca_in_b'], 'L0_xattn_ca_out_w': _L0_xattn_in['ca_out_w'], 'L0_xattn_ca_out_b': _L0_xattn_in['ca_out_b'], 'L0_xattn_moe_ln_g': _L0_xattn_in['moe_ln_g'], 'L0_xattn_moe_ln_b': _L0_xattn_in['moe_ln_b'], 'L0_xattn_router_w': _L0_xattn_in['router_w'], 'L0_xattn_router_b': _L0_xattn_in['router_b'], 'L0_xattn_e_fc1_w': _L0_xattn_in['e_fc1_w'], 'L0_xattn_e_fc1_b': _L0_xattn_in['e_fc1_b'], 'L0_xattn_e_fc2_w': _L0_xattn_in['e_fc2_w'], 'L0_xattn_e_fc2_b': _L0_xattn_in['e_fc2_b'], 'L1_xattn_in_proj_w': _L1_xattn_in['in_proj_w'], 'L1_xattn_in_proj_b': _L1_xattn_in['in_proj_b'], 'L1_xattn_out_w': _L1_xattn_in['out_w'], 'L1_xattn_out_b': _L1_xattn_in['out_b'], 'L1_xattn_score_w': _L1_xattn_in['score_w'], 'L1_xattn_score_b': _L1_xattn_in['score_b'], 'L2_xattn_ln1_w': _L2_xattn_in['ln1_w'], 'L2_xattn_ln2_w': _L2_xattn_in['ln2_w'], 'L2_xattn_Wq': _L2_xattn_in['Wq'], 'L2_xattn_Wk': _L2_xattn_in['Wk'], 'L2_xattn_Wv': _L2_xattn_in['Wv'], 'L2_xattn_Wo': _L2_xattn_in['Wo'], 'L2_xattn_Wgate': _L2_xattn_in['Wgate'], 'L2_xattn_Wup': _L2_xattn_in['Wup'], 'L2_xattn_Wdown': _L2_xattn_in['Wdown'], 'L3_xattn_Wq': _L3_xattn_in['Wq'], 'L3_xattn_bq': _L3_xattn_in['bq'], 'L3_xattn_Wk': _L3_xattn_in['Wk'], 'L3_xattn_bk': _L3_xattn_in['bk'], 'L3_xattn_Wv': _L3_xattn_in['Wv'], 'L3_xattn_bv': _L3_xattn_in['bv'], 'L3_xattn_Wo': _L3_xattn_in['Wo'], 'L3_xattn_bo': _L3_xattn_in['bo'], 'L3_xattn_ln_gamma': _L3_xattn_in['ln_gamma'], 'L3_xattn_ln_beta': _L3_xattn_in['ln_beta']}

def reference(x, ctx_1024, mask_Bx1xSxS2_ff0, L0_xattn_sa_ln_g, L0_xattn_sa_ln_b, L0_xattn_sa_in_w, L0_xattn_sa_in_b, L0_xattn_sa_out_w, L0_xattn_sa_out_b, L0_xattn_ca_q_ln_g, L0_xattn_ca_q_ln_b, L0_xattn_ca_kv_ln_g, L0_xattn_ca_kv_ln_b, L0_xattn_ca_in_w, L0_xattn_ca_in_b, L0_xattn_ca_out_w, L0_xattn_ca_out_b, L0_xattn_moe_ln_g, L0_xattn_moe_ln_b, L0_xattn_router_w, L0_xattn_router_b, L0_xattn_e_fc1_w, L0_xattn_e_fc1_b, L0_xattn_e_fc2_w, L0_xattn_e_fc2_b, L1_xattn_in_proj_w, L1_xattn_in_proj_b, L1_xattn_out_w, L1_xattn_out_b, L1_xattn_score_w, L1_xattn_score_b, L2_xattn_ln1_w, L2_xattn_ln2_w, L2_xattn_Wq, L2_xattn_Wk, L2_xattn_Wv, L2_xattn_Wo, L2_xattn_Wgate, L2_xattn_Wup, L2_xattn_Wdown, L3_xattn_Wq, L3_xattn_bq, L3_xattn_Wk, L3_xattn_bk, L3_xattn_Wv, L3_xattn_bv, L3_xattn_Wo, L3_xattn_bo, L3_xattn_ln_gamma, L3_xattn_ln_beta):
    import jax
    import jax.numpy as jnp

    def _L0_xattn_ref(latents, tokens, sa_ln_g, sa_ln_b, sa_in_w, sa_in_b, sa_out_w, sa_out_b, ca_q_ln_g, ca_q_ln_b, ca_kv_ln_g, ca_kv_ln_b, ca_in_w, ca_in_b, ca_out_w, ca_out_b, moe_ln_g, moe_ln_b, router_w, router_b, e_fc1_w, e_fc1_b, e_fc2_w, e_fc2_b):
        import jax, jax.numpy as jnp
        import numpy as np
        D, H, E, K, DFF = (256, 16, 8, 2, 1024)
        B, L, T = (4, 128, 512)
        EPS = 1e-05

        def _xavier(key, shape):
            fan_in, fan_out = (shape[-1], shape[-2])
            a = jnp.sqrt(6.0 / (fan_in + fan_out))
            return jax.random.uniform(key, shape, jnp.float32, -a, a)

        def _ln(x, g, b):
            m = x.mean(-1, keepdims=True)
            v = ((x - m) ** 2).mean(-1, keepdims=True)
            return (x - m) / jnp.sqrt(v + EPS) * g + b

        def _mha(q_in, kv_in, in_w, in_b, out_w, out_b):
            wq, wk, wv = jnp.split(in_w, 3, axis=0)
            bq, bk, bv = jnp.split(in_b, 3, axis=0)
            dh = D // H

            def heads(x, w, b):
                y = x @ w.T + b
                return y.reshape(x.shape[0], x.shape[1], H, dh).transpose(0, 2, 1, 3)
            q = heads(q_in, wq, bq)
            k = heads(kv_in, wk, bk)
            v = heads(kv_in, wv, bv)
            scores = jnp.einsum('bhqd,bhkd->bhqk', q, k) / jnp.sqrt(jnp.float32(dh))
            attn = jax.nn.softmax(scores, axis=-1)
            out = jnp.einsum('bhqk,bhkd->bhqd', attn, v)
            out = out.transpose(0, 2, 1, 3).reshape(q_in.shape[0], q_in.shape[1], D)
            return out @ out_w.T + out_b

        def _fuse_moe(x, ln_g, ln_b, rw, rb, fc1_w, fc1_b, fc2_w, fc2_b):
            h = _ln(x, ln_g, ln_b)
            logits = h @ rw.T + rb
            vals, idx = jax.lax.top_k(logits, K)
            gates = jax.nn.softmax(vals, axis=-1)
            N = x.shape[0] * x.shape[1]
            hf = h.reshape(N, D)
            h1 = jax.nn.gelu(jnp.einsum('nd,efd->enf', hf, fc1_w) + fc1_b[:, None, :], approximate=False)
            eo = jnp.einsum('enf,edf->end', h1, fc2_w) + fc2_b[:, None, :]
            idx_f = idx.reshape(N, K)
            gates_f = gates.reshape(N, K)
            gathered = eo[idx_f, jnp.arange(N)[:, None], :]
            mixed = (gathered * gates_f[..., None]).sum(axis=1).reshape(x.shape)
            return x + mixed
        q = _ln(latents, sa_ln_g, sa_ln_b)
        x = latents + _mha(q, q, sa_in_w, sa_in_b, sa_out_w, sa_out_b)
        qc = _ln(x, ca_q_ln_g, ca_q_ln_b)
        kv = _ln(tokens, ca_kv_ln_g, ca_kv_ln_b)
        x = x + _mha(qc, kv, ca_in_w, ca_in_b, ca_out_w, ca_out_b)
        return _fuse_moe(x, moe_ln_g, moe_ln_b, router_w, router_b, e_fc1_w, e_fc1_b, e_fc2_w, e_fc2_b)

    def _L1_xattn_ref(base_hidden, scaffold_hidden, in_proj_w, in_proj_b, out_w, out_b, score_w, score_b):
        import jax, jax.numpy as jnp
        import numpy as np
        TOPK = 10
        NUM_HEADS = 16
        B, N, D = base_hidden.shape
        H = NUM_HEADS
        dh = D // H
        scores = jnp.einsum('bnd,d->bn', base_hidden, score_w[0]) + score_b[0]
        _, topk_idx = jax.lax.top_k(scores, TOPK)
        sparse_hidden = jnp.take_along_axis(base_hidden, topk_idx[:, :, None], axis=1)
        Wq, Wk, Wv = jnp.split(in_proj_w, 3, axis=0)
        bq, bk, bv = jnp.split(in_proj_b, 3)
        q = (sparse_hidden @ Wq.T + bq).reshape(B, TOPK, H, dh).transpose(0, 2, 1, 3)
        k = (scaffold_hidden @ Wk.T + bk).reshape(B, -1, H, dh).transpose(0, 2, 1, 3)
        v = (scaffold_hidden @ Wv.T + bv).reshape(B, -1, H, dh).transpose(0, 2, 1, 3)
        scale = 1.0 / np.sqrt(dh).astype(np.float32)
        logits = jnp.einsum('bhqd,bhkd->bhqk', q, k) * scale
        attn = jax.nn.softmax(logits, axis=-1)
        o = jnp.einsum('bhqk,bhkd->bhqd', attn, v).transpose(0, 2, 1, 3).reshape(B, TOPK, D)
        attn_out = o @ out_w.T + out_b
        return base_hidden.at[jnp.arange(B)[:, None], topk_idx].set(attn_out)

    def _L2_xattn_ref(hidden_states, kv_states, attention_mask, ln1_w, ln2_w, Wq, Wk, Wv, Wo, Wgate, Wup, Wdown):
        import jax, jax.numpy as jnp
        import numpy as np
        import math
        H, NH, NKV, HD, FF = (256, 16, 4, 64, 1024)
        B, S = (2, 512)
        EPS, THETA = (1e-06, 10000.0)

        def _rmsnorm(x, w, eps=EPS):
            v = jnp.mean(x.astype(jnp.float32) ** 2, axis=-1, keepdims=True)
            return (x.astype(jnp.float32) * jax.lax.rsqrt(v + eps)).astype(x.dtype) * w

        def _rope_tables(seq_len, head_dim, theta=THETA):
            inv_freq = 1.0 / theta ** (jnp.arange(0, head_dim, 2, dtype=jnp.float32) / head_dim)
            freqs = jnp.arange(seq_len, dtype=jnp.float32)[:, None] * inv_freq[None, :]
            emb = jnp.concatenate([freqs, freqs], axis=-1)
            return (jnp.cos(emb), jnp.sin(emb))

        def _rotate_half(x):
            x1, x2 = jnp.split(x, 2, axis=-1)
            return jnp.concatenate([-x2, x1], axis=-1)

        def _apply_rope(x, cos, sin):
            return x * cos[None, None] + _rotate_half(x) * sin[None, None]
        bsz, q_len, _ = hidden_states.shape
        k_len = kv_states.shape[1]
        residual = hidden_states
        h = _rmsnorm(hidden_states, ln1_w)
        kv = _rmsnorm(kv_states, ln1_w)
        q = (h @ Wq).reshape(bsz, q_len, NH, HD).transpose(0, 2, 1, 3)
        k = (kv @ Wk).reshape(bsz, k_len, NKV, HD).transpose(0, 2, 1, 3)
        v = (kv @ Wv).reshape(bsz, k_len, NKV, HD).transpose(0, 2, 1, 3)
        cos_q, sin_q = _rope_tables(q_len, HD)
        cos_k, sin_k = _rope_tables(k_len, HD)
        q = _apply_rope(q, cos_q, sin_q)
        k = _apply_rope(k, cos_k, sin_k)
        groups = NH // NKV
        k = jnp.repeat(k, groups, axis=1)
        v = jnp.repeat(v, groups, axis=1)
        scores = jnp.einsum('bhqd,bhkd->bhqk', q, k) / math.sqrt(HD)
        scores = scores + attention_mask
        probs = jax.nn.softmax(scores.astype(jnp.float32), axis=-1).astype(q.dtype)
        attn = jnp.einsum('bhqk,bhkd->bhqd', probs, v)
        attn = attn.transpose(0, 2, 1, 3).reshape(bsz, q_len, NH * HD)
        attn = attn @ Wo
        hidden = residual + attn
        residual = hidden
        x = _rmsnorm(hidden, ln2_w)
        x = jax.nn.silu(x @ Wgate) * (x @ Wup) @ Wdown
        return residual + x

    def _L3_xattn_ref(x, context, Wq, bq, Wk, bk, Wv, bv, Wo, bo, ln_gamma, ln_beta):
        import jax, jax.numpy as jnp
        import numpy as np
        D_MODEL = 256
        NUM_HEADS = 16
        HEAD_DIM = D_MODEL // NUM_HEADS
        SCALE = HEAD_DIM ** (-0.5)
        LN_EPS = 1e-05
        Q_EPS = 1e-05

        def bit_quant(W):
            gamma = jnp.mean(jnp.abs(W))
            Wq = jnp.clip(jnp.round(W / (gamma + Q_EPS)), -1.0, 1.0) * gamma
            return W + jax.lax.stop_gradient(Wq - W)

        def layer_norm(x, gamma, beta):
            mu = jnp.mean(x, axis=-1, keepdims=True)
            var = jnp.mean(jnp.square(x - mu), axis=-1, keepdims=True)
            return (x - mu) * jax.lax.rsqrt(var + LN_EPS) * gamma + beta
        B, T, C = x.shape
        T_ctx = context.shape[1]
        residual = x
        xn = layer_norm(x, ln_gamma, ln_beta)
        q = xn @ bit_quant(Wq).T + bq
        k = context @ bit_quant(Wk).T + bk
        v = context @ bit_quant(Wv).T + bv
        q = q.reshape(B, T, NUM_HEADS, HEAD_DIM)
        k = k.reshape(B, T_ctx, NUM_HEADS, HEAD_DIM)
        v = v.reshape(B, T_ctx, NUM_HEADS, HEAD_DIM)
        scores = jnp.einsum('bqhd,bkhd->bhqk', q, k) * SCALE
        probs = jax.nn.softmax(scores, axis=-1)
        out = jnp.einsum('bhqk,bkhd->bqhd', probs, v).reshape(B, T, C)
        return residual + (out @ bit_quant(Wo).T + bo)
    x = _L0_xattn_ref(x, ctx_1024, L0_xattn_sa_ln_g, L0_xattn_sa_ln_b, L0_xattn_sa_in_w, L0_xattn_sa_in_b, L0_xattn_sa_out_w, L0_xattn_sa_out_b, L0_xattn_ca_q_ln_g, L0_xattn_ca_q_ln_b, L0_xattn_ca_kv_ln_g, L0_xattn_ca_kv_ln_b, L0_xattn_ca_in_w, L0_xattn_ca_in_b, L0_xattn_ca_out_w, L0_xattn_ca_out_b, L0_xattn_moe_ln_g, L0_xattn_moe_ln_b, L0_xattn_router_w, L0_xattn_router_b, L0_xattn_e_fc1_w, L0_xattn_e_fc1_b, L0_xattn_e_fc2_w, L0_xattn_e_fc2_b)
    x = _L1_xattn_ref(x, ctx_1024, L1_xattn_in_proj_w, L1_xattn_in_proj_b, L1_xattn_out_w, L1_xattn_out_b, L1_xattn_score_w, L1_xattn_score_b)
    x = _L2_xattn_ref(x, ctx_1024, mask_Bx1xSxS2_ff0, L2_xattn_ln1_w, L2_xattn_ln2_w, L2_xattn_Wq, L2_xattn_Wk, L2_xattn_Wv, L2_xattn_Wo, L2_xattn_Wgate, L2_xattn_Wup, L2_xattn_Wdown)
    x = _L3_xattn_ref(x, ctx_1024, L3_xattn_Wq, L3_xattn_bq, L3_xattn_Wk, L3_xattn_bk, L3_xattn_Wv, L3_xattn_bv, L3_xattn_Wo, L3_xattn_bo, L3_xattn_ln_gamma, L3_xattn_ln_beta)
    return x

_drawn_inputs = setup_inputs


def setup_inputs(seed=0):
    import zlib

    import numpy as np

    out = dict(_drawn_inputs(seed))
    spreads = {'L0_xattn_sa_ln_g': (1.0, 0.2),
     'L0_xattn_sa_ln_b': (0.0, 0.1),
     'L0_xattn_sa_in_b': (0.0, 0.1),
     'L0_xattn_sa_out_b': (0.0, 0.1),
     'L0_xattn_ca_q_ln_g': (1.0, 0.2),
     'L0_xattn_ca_q_ln_b': (0.0, 0.1),
     'L0_xattn_ca_kv_ln_g': (1.0, 0.2),
     'L0_xattn_ca_kv_ln_b': (0.0, 0.1),
     'L0_xattn_ca_in_b': (0.0, 0.1),
     'L0_xattn_ca_out_b': (0.0, 0.1),
     'L0_xattn_moe_ln_g': (1.0, 0.2),
     'L0_xattn_moe_ln_b': (0.0, 0.1),
     'L0_xattn_router_b': (0.0, 0.1),
     'L0_xattn_e_fc1_b': (0.0, 0.1),
     'L0_xattn_e_fc2_b': (0.0, 0.1),
     'L2_xattn_ln1_w': (1.0, 0.6),
     'L2_xattn_ln2_w': (1.0, 0.6),
     'L3_xattn_bq': (0.0, 0.8),
     'L3_xattn_bk': (0.0, 2.0),
     'L3_xattn_bv': (0.0, 0.1),
     'L3_xattn_bo': (0.0, 0.1),
     'L3_xattn_ln_gamma': (1.0, 0.6),
     'L3_xattn_ln_beta': (0.0, 2.0)}
    factors = {'L1_xattn_in_proj_b': 8.0, 'L1_xattn_out_b': 8.0, 'L2_xattn_Wq': 8.0, 'L2_xattn_Wk': 8.0}
    for name, (base, spread) in spreads.items():
        noise = np.random.default_rng([zlib.crc32(name.encode()), seed]).standard_normal(out[name].shape)
        drawn = base * np.exp(spread * noise) if base else spread * noise
        out[name] = jnp.asarray(drawn.astype(out[name].dtype))
    for name, factor in factors.items():
        out[name] = (out[name] * factor).astype(out[name].dtype)
    return out
```

```python
from contextlib import ExitStack

import numpy as np

import concourse.bass as bass
from concourse import mybir

F32 = mybir.dt.float32
ALU = mybir.AluOpType
ACT = mybir.ActivationFunctionType
AX = mybir.AxisListType.X

P = 128
B = 16
D = 256
C = D // P
GB = 4
G = B // GB
NT = GB * P
H = 16
DH = D // H
E = 8
FF = 1024
FC = FF // P
HD = 64
NKV = 4
HALF = HD // 2
TOPK = 10
R = 32
LN_EPS = 1e-5
RMS_EPS = 1e-6

COLS = ["sa_g", "sa_b", "sa_bq", "sa_bk", "sa_bv", "cq_g", "cq_b", "ck_g", "ck_b", "ca_bq", "ca_bk", "ca_bv",
        "me_g", "me_b", "l1_bq", "l1_bk", "l1_bv", "ln1", "ln2", "l3_g", "l3_b", "l3_bq", "l3_bk", "l3_bv"]
ROWS = ["sa_ob", "ca_ob", "l1_ob", "l3_ob", "l1_sw"]


class Jobs:

    def __init__(self, names):
        self.at = {n: (k % 2, k // 2) for k, n in enumerate(names)}
        assert len(self.at) == len(names)

    def __getitem__(self, name):
        return self.at[name]


def build(nc, A, out):
    with ExitStack() as ctx:
        def sb(name, shape, dt=F32):
            return ctx.enter_context(nc.sbuf_tensor(name, shape, dt))

        def sem(name):
            return ctx.enter_context(nc.semaphore(name))

        xres = sb("xres", [P, B, D])
        ctxr = sb("ctxr", [P, B, D])
        w_sa = sb("w_sa", [P, C, 4 * D])
        w_ca = sb("w_ca", [P, C, 4 * D])
        w_l1 = sb("w_l1", [P, C, 4 * D])
        w_l3 = sb("w_l3", [P, C, 4 * D])
        cols = sb("cols", [P, 2 * len(COLS)])
        rows = sb("rows", [P, len(ROWS), D])
        fc1b = sb("fc1b", [P, E * FC])
        fc2b = sb("fc2b", [E, D])
        rw = sb("rw", [P, C, E])
        rb = sb("rb", [E, 1])
        sbias = sb("sbias", [P, 1])
        rope = sb("rope", [P, 2, P])
        shape_c = sb("shape_c", [P, 2 + P + R + E * E])
        parity = shape_c[:, 0:2]
        before = shape_c[:, 2:2 + P]
        ranks = shape_c[:, 2 + P:2 + P + R]
        ebefore = shape_c[:, 2 + P + R:2 + P + R + E * E].rearrange("p (e f) -> p e f", e=E)
        ident = sb("ident", [P, P])
        ones = sb("ones", [P, P])
        nhalf = sb("nhalf", [P, GB])

        st = sb("st", [P, 2, GB, 6])
        mv = sb("mv", [P, 2, GB, 2])
        ve = sb("ve", [P, 2, GB])
        rstd = sb("rstd", [P, 2, GB])
        mx = sb("mx", [P, 2, H])
        rden = sb("rden", [P, 2, H])
        small = sb("small", [P, 64])
        gates = sb("gates", [P, B, E])
        logit = sb("logit", [P, B, E])
        gl1 = sb("gl1", [P, B, E])

        W = 33792
        reg = sb("reg", [P, W])

        def view(at, shape):
            n = int(np.prod(shape))
            assert at + n <= W, (at, n)
            v = reg[:, at:at + n]
            if len(shape) == 1:
                return v
            names = "abcd"[:len(shape)]
            return v.rearrange(f"p ({' '.join(names)}) -> p {' '.join(names)}",
                               **{k: s for k, s in zip(names[:-1], shape)})

        xn = view(0, [GB, D])
        cn = view(1024, [GB, D])
        hT = view(2048, [C, NT])
        cT = view(3072, [C, NT])
        SP = view(4096, [2, 4, 4, P])
        PT = view(8192, [2, H, P])
        qT = view(12288, [C, NT])
        kM = view(13312, [2, C, NT])
        VA = view(15360, [GB, H, DH + 1])
        on = view(16448, [GB, D])
        oT = view(17472, [C, NT])
        xs = view(18496, [GB, D])
        colb = view(19520, [GB, P])
        gat = view(20032, [GB, R])
        gatT = view(20160, [P])
        xsT = view(20288, [C, P])
        q1T = view(20544, [C, P])
        yo = view(20800, [D])
        junk = view(21056, [D])
        hall = view(1024, [C, B * P])
        fcw = [view(5120 + 4096 * k, [4096]) for k in range(2)]
        h1 = view(13312, [2, FC, NT])
        lt = view(21504, [NT])
        l2w = 22528
        wq2 = view(l2w, [C, FF])
        wkv2 = view(l2w + 2048, [C, 2 * D])
        wo2 = view(l2w + 3072, [FC, D])
        wg2 = view(l2w + 5120, [C, FF])
        wu2 = view(l2w + 7168, [C, FF])
        wd2 = view(l2w + 9216, [FC, D])
        qr = view(12288, [GB, 2, NT])
        kr = view(16384, [2, NT])
        V2 = view(17408, [GB, NKV, HD + 1])
        o2 = view(18448, [FF])
        o2T = view(0, [FC, NT])
        act2 = view(12288, [FC, NT])
        mask2 = w_sa[:, :, :].rearrange("p c n -> p (c n)").rearrange("p (b k) -> p b k", b=B)
        rt = w_ca[:, :, :].rearrange("p c n -> p (c n)").rearrange("p (a n) -> p a n", a=4)

        banks = [ctx.enter_context(nc.psum_tensor(f"bank{i}", [P, 512], F32)) for i in range(8)]
        S = banks[0:4]
        T = banks[4:6]
        Q = banks[6:8]

        ld = {n: sem("ld_" + n) for n in ("x", "ctx", "small", "sa", "ca", "l1", "l3", "l2", "fc0", "mask")}
        names = ["q_full0", "q_full1", "q_free0", "q_free1", "chain", "pchain", "const", "stats", "rstd_ok", "xn_ok",
                 "cn_ok", "ones_ok", "scored", "masked", "shifted", "maxed", "probs", "turned", "pt_ok", "biased",
                 "stored", "done", "multiplied", "roped", "act_ok", "fc1_full", "fc1_free", "fc2_full", "fc2_free",
                 "w_in0", "w_in1", "xs_ok", "colb_ok", "gat_ok", "exp_ok", "gates_ok"]
        M = {n: sem(n) for n in names}
        turn_sems = range(M[names[0]].num, M[names[-1]].num + 1)
        assert len(turn_sems) == len(names)
        q_full = [M["q_full0"], M["q_full1"]]
        q_free = [M["q_free0"], M["q_free1"]]

        def end_turn():
            nc.all_engine_barrier(sems_to_clear=turn_sems)

        def col(name, c):
            k = COLS.index(name)
            return cols[:, 2 * k + c:2 * k + c + 1]

        def row(name):
            return rows[:, ROWS.index(name), :]

        def at(t, b, n=1):
            v = t[:, bass.ds(b, n), :]
            return v.rearrange("p a d -> p (a d)") if n == 1 else v

        def claim(pe, J, name):
            b, k = J[name]
            if k > 0:
                pe.wait_ge(q_free[b], k)
            return Q[b]

        def await_full(eng, J, name):
            b, k = J[name]
            eng.wait_ge(q_full[b], k + 1)
            return Q[b]

        def await_read(eng, J, name):
            b, k = J[name]
            eng.wait_ge(q_free[b], k + 1)

        def chained(eng, s):
            n = [0]

            def link(ins):
                n[0] += 1
                ins.then_inc(s, 1)
                eng.wait_ge(s, n[0])
            return link

        with nc.Block(no_gpsimd_drain=True) as block:
            @block.sync
            def _(sp):
                sp.dma_start(xres[:], A["x"].rearrange("b p d -> p b d")).then_inc(ld["x"], 16)
                sp.dma_start(ctxr[:], A["ctx"].rearrange("b p d -> p b d")).then_inc(ld["ctx"], 16)
                for n, t in (("ca", w_ca), ("l1", w_l1), ("l3", w_l3)):
                    sp.dma_start(t[:], A["w_" + n].rearrange("(c p) n -> p c n", p=P)).then_inc(ld[n], 16)
                for n, t in (("wq2", wq2), ("wkv2", wkv2), ("wo2", wo2), ("wg2", wg2), ("wu2", wu2), ("wd2", wd2)):
                    sp.dma_start(t, A[n].rearrange("(c p) n -> p c n", p=P)).then_inc(ld["l2"], 16)

            @block.scalar
            def _(act):
                for t, n in ((cols, "cols"), (rows, "rows"), (fc1b, "fc1b"), (fc2b, "fc2b"), (rb, "rb"), (sbias, "sbias"),
                             (rope, "rope"), (shape_c, "shape_c")):
                    act.dma_start(t[:], A[n]).then_inc(ld["small"], 16)
                act.dma_start(rw[:], A["rw"].rearrange("(c p) e -> p c e", p=P)).then_inc(ld["small"], 16)
                act.dma_start(w_sa[:], A["w_sa"].rearrange("(c p) n -> p c n", p=P)).then_inc(ld["sa"], 16)
                act.wait_ge(ld["small"], 16 * 9)

            @block.gpsimd
            def _(pool):
                nc.gpsimd.memset(ident[:], 0.0).then_inc(M["const"], 1)
                nc.gpsimd.memset(ones[:], 1.0)
                nc.gpsimd.memset(nhalf[:], -0.5)
                pool.wait_ge(M["const"], 1)
                nc.gpsimd.affine_select(out=ident[:], in_=ident[:], compare_op=ALU.not_equal, fill=1.0, base=0,
                                        pattern=[[-1, P]], channel_multiplier=1)

        end_turn()

        def dve_stats(dve, link, src, g, k):
            for j in range(GB):
                last = nc.vector.bn_stats(st[:, k, j, :], at(src, g * GB + j))
            link(last)
            for j in range(GB):
                nc.vector.bn_aggr(mv[:, k, j, :], st[:, k, j, :]).then_inc(M["stats"], 1)

        def pool_rstd(pool, link, k, n_stats, eps):
            pool.wait_ge(M["stats"], n_stats)
            link(nc.gpsimd.tensor_scalar(ve[:, k, :], mv[:, k, :, 1], eps, 1.0, ALU.add, ALU.mult))
            nc.gpsimd.tensor_tensor(rstd[:, k, :], ve[:, k, :], nhalf[:], ALU.pow).then_inc(M["rstd_ok"], 1)

        def dve_centre(dve, src, dst, g, k, ok):
            for j in range(GB):
                nc.vector.tensor_scalar(dst[:, j, :], at(src, g * GB + j), mv[:, k, j, 0:1], rstd[:, k, j:j + 1],
                                        ALU.subtract, ALU.mult).then_inc(ok, 1)

        def pe_turn_rows(pe, J, names, src, ok):
            for c in range(C):
                bank = claim(pe, J, names[c])
                for j in range(GB):
                    if c == 0:
                        pe.wait_ge(ok, j + 1)
                    ins = nc.tensor.transpose(bank[:, j * P:(j + 1) * P], src[:, j, c * P:(c + 1) * P], ident[:])
                ins.then_inc(q_full[J[names[c]][0]], 1)

        def act_affine(act, J, names, dst, gain, bias):
            for c in range(C):
                bank = await_full(act, J, names[c])
                if gain is None:
                    ins = nc.scalar.activation(dst[:, c, :], bank[:, :], ACT.Copy)
                else:
                    ins = nc.scalar.activation(dst[:, c, :], bank[:, :], ACT.Identity, scale=col(gain, c),
                                               bias=col(bias, c) if bias else 0.0)
                ins.then_inc(q_free[J[names[c]][0]], 1)

        def pe_project(pe, J, name, w, w0, src, n=NT):
            bank = claim(pe, J, name)
            for c in range(C):
                ins = nc.tensor.matmul(bank[:, 0:n], w[:, c, w0:w0 + P], src[:, c, :], start=(c == 0), stop=(c == C - 1))
            ins.then_inc(q_full[J[name][0]], 1)

        def pe_values(pe, J, names, w, w0, src):
            for v, name in enumerate(names):
                bank = claim(pe, J, name)
                for jj in range(2):
                    j = 2 * v + jj
                    for c in range(C):
                        ins = nc.tensor.matmul(bank[:, jj * D:(jj + 1) * D], src[:, c, j * P:(j + 1) * P],
                                               w[:, c, w0:w0 + D], start=(c == 0), stop=(c == C - 1))
                ins.then_inc(q_full[J[name][0]], 1)

        def act_values(act, J, names):
            for v, name in enumerate(names):
                bank = await_full(act, J, name)
                nc.scalar.activation(
                    VA[:, 2 * v:2 * v + 2, :, 0:DH],
                    bank[:, :].rearrange("p (j h d) -> p j h d", j=2, d=DH), ACT.Copy).then_inc(q_free[J[name][0]], 1)

        def dve_keys(dve, J, m, bias):
            bank = await_full(dve, J, f"k{m}")
            for par in range(2):
                ins = nc.vector.tensor_scalar(kM[:, par, m, :], bank[:, :], col(bias, m), parity[:, par:par + 1],
                                              ALU.add, ALU.mult)
            ins.then_inc(q_free[J[f"k{m}"][0]], 1)

        def pe_scores(pe, j, i):
            r = slice(32 * i, 32 * i + 32)
            for m in range(C):
                ins = nc.tensor.matmul(S[i][:, m * 256:(m + 1) * 256], qT[r, m, j * P:(j + 1) * P],
                                       kM[r, :, m, j * P:(j + 1) * P], start=True, stop=True)
            ins.then_inc(M["scored"], 1)

        def head(i, s):
            return 8 * (s // 2) + 2 * i + s % 2

        def dve_shift(dve, j, last_turned=True):
            def shift(i):
                n = 4 * j + i
                dve.wait_ge(M["maxed"], n + 1)
                if j >= 2:
                    dve.wait_ge(M["turned"], 4 * (j - 2) + i + 1)
                nc.vector.tensor_tensor(SP[:, j % 2, i, :, :], S[i][:, :].rearrange("p (s k) -> p s k", k=P),
                                        mx[:, j % 2, 4 * i:4 * i + 4].unsqueeze(2).to_broadcast([P, 4, P]),
                                        ALU.subtract).then_inc(M["shifted"], 1)
            for i in range(4):
                dve.wait_ge(M["scored"], 4 * j + i + 1)
                nc.vector.tensor_reduce(mx[:, j % 2, 4 * i:4 * i + 4], S[i][:, :].rearrange("p (s k) -> p s k", k=P),
                                        AX, ALU.max).then_inc(M["maxed"], 1)
                if i >= 1:
                    shift(i - 1)
            shift(3)

        def act_softmax(act, n_batches, scale, pv_done):
            N = 4 * n_batches
            for n in range(N + 2):
                if n < N:
                    act.wait_ge(M["shifted"], n + 1)
                    v = SP[:, (n // 4) % 2, n % 4, :, :]
                    nc.scalar.activation(v, v, ACT.Exp, scale=scale).then_inc(M["probs"], 1)
                if n >= 2:
                    act_copy_turned(act, n - 2, pv_done)

        def act_copy_turned(act, m, pv_done):
            j, i = divmod(m, 4)
            act.wait_ge(M["turned"], m + 1)
            if j >= 2:
                pv_done(j - 2)
            nc.scalar.activation(PT[:, j % 2, 4 * i:4 * i + 4, :], T[m % 2][:, :].rearrange("p (s q) -> p s q", q=P),
                                 ACT.Copy).then_inc(M["pt_ok"], 1)

        def pe_turn(pe, j, i):
            n = 4 * j + i
            pe.wait_ge(M["probs"], n + 1)
            if n >= 2:
                pe.wait_ge(M["pt_ok"], n - 1)
            for s in range(4):
                ins = nc.tensor.transpose(T[n % 2][:, s * P:(s + 1) * P], SP[:, j % 2, i, s, :], ident[:])
            ins.then_inc(M["turned"], 1)

        def dve_divide(dve, link, J, name, dst, rd, nh, w):
            bank = await_full(dve, J, name)
            o = bank[:, 0:nh * (w + 1)].rearrange("p (h d) -> p h d", d=w + 1)
            link(nc.vector.reciprocal(rd, o[:, :, w]))
            nc.vector.tensor_tensor(dst.rearrange("p (h d) -> p h d", d=w), o[:, :, 0:w],
                                    rd.unsqueeze(2).to_broadcast([P, nh, w]), ALU.mult).then_inc(q_free[J[name][0]], 1)

        def attention(q_norm, kv, w, bq, bk, bv, ob, loads, store=False):
            jobs = ["hx0", "hx1"] + ([] if kv == "self" else ["hc0", "hc1"])
            jobs += ["q0", "q1", "k0", "k1", "v0", "v1"] + [f"pv{j}" for j in range(GB)] + ["o0", "o1", "y0", "y1"]
            J = Jobs(jobs)
            kvT = hT if kv == "self" else cT
            with nc.Fori(0, G) as g:
                with nc.Block(no_gpsimd_drain=True) as block:
                    @block.tensor
                    def _(pe):
                        for s in loads:
                            pe.wait_ge(ld[s], 16)
                        pe_turn_rows(pe, J, ["hx0", "hx1"], xn, M["xn_ok"])
                        if kv != "self":
                            pe_turn_rows(pe, J, ["hc0", "hc1"], cn, M["cn_ok"])
                        await_read(pe, J, "hx0")
                        await_read(pe, J, "hx1")
                        for m in range(C):
                            pe_project(pe, J, f"q{m}", w, m * P, hT)
                        if kv != "self":
                            await_read(pe, J, "hc0")
                            await_read(pe, J, "hc1")
                        for m in range(C):
                            pe_project(pe, J, f"k{m}", w, D + m * P, kvT)
                        pe_values(pe, J, ["v0", "v1"], w, 2 * D, kvT)
                        await_read(pe, J, "q1")
                        await_read(pe, J, "q0")
                        await_read(pe, J, "k0")
                        await_read(pe, J, "k1")
                        for i in range(4):
                            pe_scores(pe, 0, i)

                        def products(j):
                            pe.wait_ge(M["pt_ok"], 4 * j + 4)
                            if j == 0:
                                pe.wait_ge(M["ones_ok"], 1)
                                await_read(pe, J, "v0")
                                await_read(pe, J, "v1")
                            bank = claim(pe, J, f"pv{j}")
                            for i in range(4):
                                for s in range(4):
                                    h = head(i, s)
                                    ins = nc.tensor.matmul(bank[:, h * (DH + 1):(h + 1) * (DH + 1)],
                                                           PT[:, j % 2, 4 * i + s, :], VA[:, j, h, :], start=True, stop=True)
                            ins.then_inc(q_full[J[f"pv{j}"][0]], 1)

                        for j in range(GB):
                            for i in range(4):
                                if j + 1 < GB:
                                    pe.wait_ge(M["shifted"], 4 * j + i + 1)
                                    pe_scores(pe, j + 1, i)
                                pe_turn(pe, j, i)
                                if i == 1 and j > 0:
                                    products(j - 1)
                        products(GB - 1)
                        for c in range(C):
                            bank = claim(pe, J, f"o{c}")
                            for j in range(GB):
                                if c == 0:
                                    await_read(pe, J, f"pv{j}")
                                ins = nc.tensor.transpose(bank[:, j * P:(j + 1) * P], on[:, j, c * P:(c + 1) * P], ident[:])
                            ins.then_inc(q_full[J[f"o{c}"][0]], 1)
                        await_read(pe, J, "o0")
                        await_read(pe, J, "o1")
                        for y in range(2):
                            bank = claim(pe, J, f"y{y}")
                            for jj in range(2):
                                j = 2 * y + jj
                                for c in range(C):
                                    ins = nc.tensor.matmul(bank[:, jj * D:(jj + 1) * D], oT[:, c, j * P:(j + 1) * P],
                                                           w[:, c, 3 * D:4 * D], start=(c == 0), stop=(c == C - 1))
                            ins.then_inc(q_full[J[f"y{y}"][0]], 1)

                    @block.scalar
                    def _(act):
                        act_affine(act, J, ["hx0", "hx1"], hT, q_norm[0], q_norm[1])
                        if kv == "norm":
                            act_affine(act, J, ["hc0", "hc1"], cT, "ck_g", "ck_b")
                        elif kv == "raw":
                            act_affine(act, J, ["hc0", "hc1"], cT, None, None)
                        for m in range(C):
                            bank = await_full(act, J, f"q{m}")
                            nc.scalar.activation(qT[:, m, :], bank[:, :], ACT.Identity, bias=col(bq, m))\
                                .then_inc(q_free[J[f"q{m}"][0]], 1)
                        act_values(act, J, ["v0", "v1"])
                        act_softmax(act, GB, DH ** -0.5, lambda j: await_full(act, J, f"pv{j}"))
                        for c in range(C):
                            bank = await_full(act, J, f"o{c}")
                            nc.scalar.activation(oT[:, c, :], bank[:, :], ACT.Identity, bias=col(bv, c))\
                                .then_inc(q_free[J[f"o{c}"][0]], 1)

                    @block.gpsimd
                    def _(pool):
                        link = chained(pool, M["pchain"])
                        nc.gpsimd.memset(VA[:, :, :, DH:DH + 1], 1.0).then_inc(M["ones_ok"], 1)
                        pool_rstd(pool, link, 0, GB, LN_EPS)
                        if kv == "norm":
                            pool_rstd(pool, link, 1, 2 * GB, LN_EPS)
                        if kv == "raw":
                            if "ctx" in loads:
                                pool.wait_ge(ld["ctx"], 16)
                            for j in range(GB):
                                nc.gpsimd.tensor_copy(cn[:, j, :], at(ctxr, g * GB + j)).then_inc(M["cn_ok"], 1)
                        pool.wait_ge(M["xn_ok"], GB)
                        for j in range(GB):
                            nc.gpsimd.tensor_tensor(at(xres, g * GB + j), at(xres, g * GB + j), row(ob), ALU.add)\
                                .then_inc(M["biased"], 1)

                    @block.vector
                    def _(dve):
                        link = chained(dve, M["chain"])
                        if "x" in loads:
                            dve.wait_ge(ld["x"], 16)
                        dve_stats(dve, link, xres, g, 0)
                        if kv == "norm":
                            dve.wait_ge(ld["ctx"], 16)
                            dve_stats(dve, link, ctxr, g, 1)
                        dve.wait_ge(M["rstd_ok"], 1)
                        dve_centre(dve, xres, xn, g, 0, M["xn_ok"])
                        if kv == "norm":
                            dve.wait_ge(M["rstd_ok"], 2)
                            dve_centre(dve, ctxr, cn, g, 1, M["cn_ok"])
                        for m in range(C):
                            dve_keys(dve, J, m, bk)

                        def divide(j):
                            dve_divide(dve, link, J, f"pv{j}", on[:, j, :], rden[:, j % 2, :], H, DH)

                        for j in range(GB):
                            dve_shift(dve, j)
                            if j > 0:
                                divide(j - 1)
                        divide(GB - 1)
                        dve.wait_ge(M["biased"], GB)
                        for y in range(2):
                            bank = await_full(dve, J, f"y{y}")
                            x2 = at(xres, g * GB + 2 * y, 2)
                            ins = nc.vector.tensor_tensor(x2, bank[:, :].rearrange("p (j d) -> p j d", j=2), x2, ALU.add)
                            ins.then_inc(M["stored"], 1)

                    @block.sync
                    def _(sp):
                        if store:
                            sp.wait_ge(M["stored"], 2)
                            sp.dma_start(out.rearrange("b p d -> p b d")[:, bass.ds(g * GB, GB), :],
                                         at(xres, g * GB, GB)).then_inc(M["done"], 16)
                            sp.wait_ge(M["done"], 16)
                end_turn()

        attention(("sa_g", "sa_b"), "self", w_sa, "sa_bq", "sa_bk", "sa_bv", "sa_ob", ["sa", "x"])
        attention(("cq_g", "cq_b"), "norm", w_ca, "ca_bq", "ca_bk", "ca_bv", "ca_ob", ["ca"])

        def fc_weights(k):
            return (fcw[k][:, 0:C * FF].rearrange("p (c f) -> p c f", c=C),
                    fcw[k][:, C * FF:].rearrange("p (f d) -> p f d", f=FC))

        def load_expert(sp, e, k, s):
            w1, w2 = fc_weights(k)
            sp.dma_start(w1, A["fc1"][bass.ds(e * D, D), :].rearrange("(c p) f -> p c f", p=P)).then_inc(s, 16)
            sp.dma_start(w2, A["fc2"][bass.ds(e * FF, FF), :].rearrange("(f p) d -> p f d", p=P)).then_inc(s, 16)

        with nc.Block(no_gpsimd_drain=True) as block:
            @block.sync
            def _(sp):
                load_expert(sp, 0, 0, ld["fc0"])
                sp.dma_start(mask2, A["mask"].rearrange("b q k -> q b k")).then_inc(ld["mask"], 16)

        J_route = Jobs(["hx0", "hx1", "logits", "turned"])
        with nc.Fori(0, G) as g:
            with nc.Block(no_gpsimd_drain=True) as block:
                @block.tensor
                def _(pe):
                    J = J_route
                    pe_turn_rows(pe, J, ["hx0", "hx1"], xn, M["xn_ok"])
                    await_read(pe, J, "hx0")
                    await_read(pe, J, "hx1")
                    bank = claim(pe, J, "logits")
                    for c in range(C):
                        ins = nc.tensor.matmul(bank[0:E, :], rw[:, c, :], hall[:, c, bass.ds(g * NT, NT)],
                                               start=(c == 0), stop=(c == C - 1))
                    ins.then_inc(q_full[J["logits"][0]], 1)
                    await_read(pe, J, "logits")
                    bank = claim(pe, J, "turned")
                    for j in range(GB):
                        ins = nc.tensor.transpose(bank[:, j * E:(j + 1) * E], lt[0:E, j * P:(j + 1) * P], ident[0:E, 0:E])
                    ins.then_inc(q_full[J["turned"][0]], 1)

                @block.scalar
                def _(act):
                    J = J_route
                    for c in range(C):
                        bank = await_full(act, J, f"hx{c}")
                        nc.scalar.activation(hall[:, c, bass.ds(g * NT, NT)], bank[:, :], ACT.Identity,
                                             scale=col("me_g", c), bias=col("me_b", c)).then_inc(q_free[J[f"hx{c}"][0]], 1)
                    bank = await_full(act, J, "logits")
                    nc.scalar.activation(lt[0:E, :], bank[0:E, :], ACT.Identity, bias=rb[:, 0:1])\
                        .then_inc(q_free[J["logits"][0]], 1)

                @block.gpsimd
                def _(pool):
                    pool_rstd(pool, chained(pool, M["pchain"]), 0, GB, LN_EPS)

                @block.vector
                def _(dve):
                    J = J_route
                    dve_stats(dve, chained(dve, M["chain"]), xres, g, 0)
                    dve.wait_ge(M["rstd_ok"], 1)
                    dve_centre(dve, xres, xn, g, 0, M["xn_ok"])
                    bank = await_full(dve, J, "turned")
                    nc.vector.tensor_copy(logit[:, bass.ds(g * GB, GB), :],
                                          bank[:, 0:GB * E].rearrange("p (j e) -> p j e", e=E))\
                        .then_inc(q_free[J["turned"][0]], 1)
            end_turn()

        above = view(13312, [B, E, E])
        tied = view(13312 + B * E * E, [B, E, E])
        rank = view(13312 + 2 * B * E * E, [B, E])
        top = small[:, 0:B]
        total = small[:, B:2 * B]
        inverse = small[:, 2 * B:3 * B]
        gateT = view(17408, [B * P])
        J_gate = Jobs([f"t{k}" for k in range(G)] + [f"b{k}" for k in range(B // 2)])
        with nc.Block(no_gpsimd_drain=True) as block:
            @block.vector
            def _(dve):
                J = J_gate
                link = chained(dve, M["chain"])
                others = logit[:, :, :].unsqueeze(2).to_broadcast([P, B, E, E])
                own = logit[:, :, :].unsqueeze(3).to_broadcast([P, B, E, E])
                nc.vector.tensor_tensor(above, others, own, ALU.is_gt)
                nc.vector.tensor_reduce(top, logit[:, :, :], AX, ALU.max)
                link(nc.vector.tensor_tensor(tied, others, own, ALU.is_equal))
                nc.vector.tensor_tensor(gl1[:, :, :], logit[:, :, :], top.unsqueeze(2).to_broadcast([P, B, E]),
                                        ALU.subtract).then_inc(M["shifted"], 1)
                link(nc.vector.tensor_tensor(tied, tied, ebefore.unsqueeze(1).to_broadcast([P, B, E, E]), ALU.mult))
                link(nc.vector.tensor_tensor(above, above, tied, ALU.add))
                link(nc.vector.tensor_reduce(rank, above, AX, ALU.add))
                link(nc.vector.tensor_scalar(rank, rank, 1.5, None, ALU.is_lt))
                dve.wait_ge(M["exp_ok"], 1)
                link(nc.vector.tensor_tensor(gl1[:, :, :], gl1[:, :, :], rank, ALU.mult))
                link(nc.vector.tensor_reduce(total, gl1[:, :, :], AX, ALU.add))
                link(nc.vector.reciprocal(inverse, total))
                nc.vector.tensor_tensor(gates[:, :, :], gl1[:, :, :], inverse.unsqueeze(2).to_broadcast([P, B, E]),
                                        ALU.mult).then_inc(M["gates_ok"], 1)
                for k in range(B // 2):
                    bank = await_full(dve, J, f"b{k}")
                    x2 = xres[:, 2 * k:2 * k + 2, :]
                    nc.vector.tensor_tensor(x2, bank[:, :].rearrange("p (j d) -> p j d", j=2), x2, ALU.add)\
                        .then_inc(q_free[J[f"b{k}"][0]], 1)

            @block.scalar
            def _(act):
                J = J_gate
                act.wait_ge(M["shifted"], 1)
                nc.scalar.activation(gl1[:, :, :], gl1[:, :, :], ACT.Exp).then_inc(M["exp_ok"], 1)
                for k in range(G):
                    bank = await_full(act, J, f"t{k}")
                    nc.scalar.activation(gateT[0:E, k * NT:(k + 1) * NT], bank[0:E, :], ACT.Copy)\
                        .then_inc(q_free[J[f"t{k}"][0]], 1)

            @block.tensor
            def _(pe):
                J = J_gate
                pe.wait_ge(M["gates_ok"], 1)
                for k in range(G):
                    bank = claim(pe, J, f"t{k}")
                    for j in range(GB):
                        ins = nc.tensor.transpose(bank[0:E, j * P:(j + 1) * P], gates[:, k * GB + j, :], ident[:])
                    ins.then_inc(q_full[J[f"t{k}"][0]], 1)
                for k in range(G):
                    await_read(pe, J, f"t{k}")
                for k in range(B // 2):
                    bank = claim(pe, J, f"b{k}")
                    for j in range(2):
                        b = 2 * k + j
                        ins = nc.tensor.matmul(bank[:, j * D:(j + 1) * D], gateT[0:E, b * P:(b + 1) * P], fc2b[:, :],
                                               start=True, stop=True)
                    ins.then_inc(q_full[J[f"b{k}"][0]], 1)
        end_turn()

        def experts(p, last):
            U = 2 * G
            with nc.Block(no_gpsimd_drain=True) as block:
                @block.sync
                def _(sp):
                    load_expert(sp, p * 2 + 1, 1, M["w_in1"])
                    if not last:
                        sp.wait_ge(M["fc2_full"], 2 * G)
                        load_expert(sp, p * 2 + 2, 0, M["w_in0"])
                        sp.wait_ge(M["w_in0"], 32)

                @block.tensor
                def _(pe):
                    pe.wait_ge(ld["fc0"], 32)

                    def up(u):
                        w1, _ = fc_weights(u // G)
                        if u == G:
                            pe.wait_ge(M["w_in1"], 32)
                        for f in range(FC):
                            n = FC * u + f
                            if n >= 4:
                                pe.wait_ge(M["fc1_free"], n - 3)
                            for c in range(C):
                                ins = nc.tensor.matmul(banks[n % 4][:, :], w1[:, c, f * P:(f + 1) * P],
                                                       hall[:, c, (u % G) * NT:(u % G + 1) * NT],
                                                       start=(c == 0), stop=(c == C - 1))
                            ins.then_inc(M["fc1_full"], 1)

                    def down(u):
                        _, w2 = fc_weights(u // G)
                        pe.wait_ge(M["fc1_free"], FC * (u + 1))
                        for m in range(2):
                            n = 2 * u + m
                            if n >= 4:
                                pe.wait_ge(M["fc2_free"], n - 3)
                            for t in range(2):
                                for f in range(FC):
                                    j = 2 * m + t
                                    ins = nc.tensor.matmul(banks[4 + n % 4][:, t * D:(t + 1) * D],
                                                           h1[:, u % 2, f, j * P:(j + 1) * P], w2[:, f, :],
                                                           start=(f == 0), stop=(f == FC - 1))
                            ins.then_inc(M["fc2_full"], 1)

                    for u in range(U + 1):
                        if u < U:
                            up(u)
                        if u > 0:
                            down(u - 1)

                @block.scalar
                def _(act):
                    for u in range(U):
                        if u >= 2:
                            act.wait_ge(M["fc2_full"], 2 * (u - 1))
                        for f in range(FC):
                            n = FC * u + f
                            act.wait_ge(M["fc1_full"], n + 1)
                            nc.scalar.activation(h1[:, u % 2, f, :], banks[n % 4][:, :], ACT.Gelu,
                                                 bias=fc1b[:, bass.ds(p * 2 * FC + (u // G) * FC + f, 1)])\
                                .then_inc(M["fc1_free"], 1)

                @block.vector
                def _(dve):
                    for u in range(U):
                        for m in range(2):
                            n = 2 * u + m
                            dve.wait_ge(M["fc2_full"], n + 1)
                            if u >= G:
                                dve.wait_ge(M["fc2_free"], n - 2 * G + 1)
                            for t in range(2):
                                b = (u % G) * GB + 2 * m + t
                                gate = gates[:, b, bass.ds(p * 2 + u // G, 1)]
                                ins = nc.vector.scalar_tensor_tensor(
                                    out=xres[:, b, :], in0=banks[4 + n % 4][:, t * D:(t + 1) * D], scalar=gate,
                                    in1=xres[:, b, :], op0=ALU.mult, op1=ALU.add)
                            ins.then_inc(M["fc2_free"], 1)
            end_turn()

        with nc.Fori(0, E // 2 - 1) as p:
            experts(p, False)
        experts(E // 2 - 1, True)

        score, scoreb = small[:, 0:GB], small[:, 4:4 + GB]
        n_above, n_tied = small[:, 8:8 + GB], small[:, 12:12 + GB]
        place, keep = small[:, 16:16 + GB], small[:, 20:20 + GB]
        J_best = Jobs(["hc0", "hc1", "row", "k0", "k1", "v0", "v1", "xs", "gt", "q0", "q1", "pv", "o", "y"]
                      + [f"s{j}" for j in range(GB)])
        with nc.Fori(0, G) as g:
            with nc.Block(no_gpsimd_drain=True) as block:
                @block.tensor
                def _(pe):
                    J = J_best
                    pe.wait_ge(ld["l1"], 16)
                    pe_turn_rows(pe, J, ["hc0", "hc1"], cn, M["cn_ok"])
                    bank = claim(pe, J, "row")
                    pe.wait_ge(M["colb_ok"], GB)
                    for j in range(GB):
                        ins = nc.tensor.transpose(bank[:, j * P:(j + 1) * P], colb[:, j, :], ident[:])
                    ins.then_inc(q_full[J["row"][0]], 1)
                    await_read(pe, J, "hc0")
                    await_read(pe, J, "hc1")
                    for m in range(C):
                        pe_project(pe, J, f"k{m}", w_l1, D + m * P, cT)
                    pe_values(pe, J, ["v0", "v1"], w_l1, 2 * D, cT)
                    bank = claim(pe, J, "xs")
                    pe.wait_ge(M["gat_ok"], GB)
                    pe.wait_ge(M["xs_ok"], GB)
                    for c in range(C):
                        for j in range(GB):
                            ins = nc.tensor.matmul(bank[:, c * P + j * R:c * P + (j + 1) * R], xs[:, j, c * P:(c + 1) * P],
                                                   gat[:, j, :], start=True, stop=True)
                    ins.then_inc(q_full[J["xs"][0]], 1)
                    bank = claim(pe, J, "gt")
                    nc.tensor.transpose(bank[:, 0:P], gat[:, :, :].rearrange("p j r -> p (j r)"), ident[:])\
                        .then_inc(q_full[J["gt"][0]], 1)
                    await_read(pe, J, "xs")
                    for m in range(C):
                        pe_project(pe, J, f"q{m}", w_l1, m * P, xsT, P)
                    for n in ("k0", "k1", "q0", "q1"):
                        await_read(pe, J, n)
                    for i in range(4):
                        r = slice(32 * i, 32 * i + 32)
                        for m in range(C):
                            for j in range(GB):
                                ins = nc.tensor.matmul(S[i][j * R:(j + 1) * R, m * 256:(m + 1) * 256],
                                                       q1T[r, m, j * R:(j + 1) * R], kM[r, :, m, j * P:(j + 1) * P],
                                                       start=True, stop=True)
                        ins.then_inc(M["scored"], 1)
                    for i in range(4):
                        pe_turn(pe, 0, i)
                    pe.wait_ge(M["pt_ok"], 4)
                    pe.wait_ge(M["ones_ok"], 1)
                    await_read(pe, J, "v0")
                    await_read(pe, J, "v1")
                    bank = claim(pe, J, "pv")
                    for i in range(4):
                        for s in range(4):
                            h = head(i, s)
                            for j in range(GB):
                                ins = nc.tensor.matmul(bank[j * R:(j + 1) * R, h * (DH + 1):(h + 1) * (DH + 1)],
                                                       PT[:, 0, 4 * i + s, j * R:(j + 1) * R], VA[:, j, h, :],
                                                       start=True, stop=True)
                    ins.then_inc(q_full[J["pv"][0]], 1)
                    await_read(pe, J, "pv")
                    bank = claim(pe, J, "o")
                    for c in range(C):
                        ins = nc.tensor.transpose(bank[:, c * P:(c + 1) * P], on[:, 0, c * P:(c + 1) * P], ident[:])
                    ins.then_inc(q_full[J["o"][0]], 1)
                    await_read(pe, J, "o")
                    bank = claim(pe, J, "y")
                    for c in range(C):
                        ins = nc.tensor.matmul(bank[:, 0:D], oT[:, c, 0:P], w_l1[:, c, 3 * D:4 * D],
                                               start=(c == 0), stop=(c == C - 1))
                    ins.then_inc(q_full[J["y"][0]], 1)
                    await_read(pe, J, "y")
                    await_read(pe, J, "gt")
                    for j in range(GB):
                        bank = claim(pe, J, f"s{j}")
                        r = slice(j * R, (j + 1) * R)
                        nc.tensor.matmul(bank[:, 0:D], gatT[r, :], yo[r, :], start=True, stop=True)\
                            .then_inc(q_full[J[f"s{j}"][0]], 1)

                @block.scalar
                def _(act):
                    J = J_best
                    act_affine(act, J, ["hc0", "hc1"], cT, None, None)
                    act_values(act, J, ["v0", "v1"])
                    bank = await_full(act, J, "xs")
                    nc.scalar.activation(xsT[:, :, :], bank[:, 0:C * P].rearrange("p (c n) -> p c n", c=C), ACT.Copy)\
                        .then_inc(q_free[J["xs"][0]], 1)
                    bank = await_full(act, J, "gt")
                    nc.scalar.activation(gatT, bank[:, 0:P], ACT.Copy).then_inc(q_free[J["gt"][0]], 1)
                    for m in range(C):
                        bank = await_full(act, J, f"q{m}")
                        nc.scalar.activation(q1T[:, m, :], bank[:, 0:P], ACT.Identity, bias=col("l1_bq", m))\
                            .then_inc(q_free[J[f"q{m}"][0]], 1)
                    act_softmax(act, 1, DH ** -0.5, None)
                    bank = await_full(act, J, "o")
                    for c in range(C):
                        ins = nc.scalar.activation(oT[:, c, 0:P], bank[:, c * P:(c + 1) * P], ACT.Identity,
                                                   bias=col("l1_bv", c))
                    ins.then_inc(q_free[J["o"][0]], 1)

                @block.gpsimd
                def _(pool):
                    nc.gpsimd.memset(VA[:, :, :, DH:DH + 1], 1.0).then_inc(M["ones_ok"], 1)
                    for j in range(GB):
                        nc.gpsimd.tensor_copy(xs[:, j, :], at(xres, g * GB + j)).then_inc(M["xs_ok"], 1)
                    for j in range(GB):
                        nc.gpsimd.tensor_copy(cn[:, j, :], at(ctxr, g * GB + j)).then_inc(M["cn_ok"], 1)

                @block.vector
                def _(dve):
                    J = J_best
                    link = chained(dve, M["chain"])
                    for j in range(GB):
                        dve.wait_ge(M["xs_ok"], j + 1)
                        link(nc.vector.scalar_tensor_tensor(out=junk, in0=xs[:, j, :], scalar=1.0, in1=row("l1_sw"),
                                                            op0=ALU.mult, op1=ALU.mult, accum_out=score[:, j:j + 1]))
                    link(nc.vector.tensor_scalar(scoreb, score, sbias[:, 0:1], None, ALU.add))
                    for j in range(GB):
                        nc.vector.tensor_scalar(colb[:, j, :], ones[:, :], scoreb[:, j:j + 1], None, ALU.mult)\
                            .then_inc(M["colb_ok"], 1)
                    bank = await_full(dve, J, "row")
                    for j in range(GB):
                        each = bank[:, j * P:(j + 1) * P]
                        link(nc.vector.tensor_scalar(junk[:, 0:P], each, scoreb[:, j:j + 1], None, ALU.is_gt, ALU.add,
                                                     accum_out=n_above[:, j:j + 1]))
                        link(nc.vector.scalar_tensor_tensor(out=junk[:, 0:P], in0=each, scalar=scoreb[:, j:j + 1],
                                                            in1=before, op0=ALU.is_equal, op1=ALU.mult,
                                                            accum_out=n_tied[:, j:j + 1]))
                    nc.vector.tensor_copy(junk[:, 0:1], bank[:, 0:1]).then_inc(q_free[J["row"][0]], 1)
                    link(nc.vector.tensor_tensor(place, n_above, n_tied, ALU.add))
                    for j in range(GB):
                        nc.vector.tensor_scalar(gat[:, j, :], ranks, place[:, j:j + 1], None, ALU.is_equal)\
                            .then_inc(M["gat_ok"], 1)
                    link(nc.vector.tensor_scalar(keep, place, TOPK - 0.5, None, ALU.is_gt))
                    for m in range(C):
                        dve_keys(dve, J, m, "l1_bk")
                    dve_shift(dve, 0)
                    dve_divide(dve, link, J, "pv", on[:, 0, :], rden[:, 0, :], H, DH)
                    bank = await_full(dve, J, "y")
                    nc.vector.tensor_tensor(yo, bank[:, 0:D], row("l1_ob"), ALU.add).then_inc(q_free[J["y"][0]], 1)
                    for j in range(GB):
                        bank = await_full(dve, J, f"s{j}")
                        nc.vector.scalar_tensor_tensor(out=at(xres, g * GB + j), in0=at(xres, g * GB + j),
                                                       scalar=keep[:, j:j + 1], in1=bank[:, 0:D],
                                                       op0=ALU.mult, op1=ALU.add).then_inc(q_free[J[f"s{j}"][0]], 1)
            end_turn()

        A4 = H // NKV
        jobs = ["hx0", "hx1", "hc0", "hc1", "kA", "kB"] + [f"q{a}{h}" for a in range(A4) for h in "AB"] + ["v0", "v1"]
        for j in range(GB + 1):
            if j > 0:
                jobs += [f"pv{j - 1}_{i}" for i in range(4)] + [f"o{j - 1}_0", f"o{j - 1}_1"]
        jobs += ["w0", "w1", "n0", "n1"] + [f"{x}{f}" for f in range(FC) for x in "gu"] + ["d0", "d1"]
        J_l2 = Jobs(jobs)
        scratch = [w_ca, w_l1]

        def products4(k, r):
            return scratch[r % 2][:, :, :].rearrange("p c n -> p (c n)")[:, k * NT:(k + 1) * NT]\
                .rearrange("p (j n) -> p j n", j=GB)

        with nc.Fori(0, G) as g:
            with nc.Block(no_gpsimd_drain=True) as block:
                @block.tensor
                def _(pe):
                    J = J_l2
                    pe.wait_ge(ld["l2"], 16 * 6)
                    pe_turn_rows(pe, J, ["hx0", "hx1"], xn, M["xn_ok"])
                    pe_turn_rows(pe, J, ["hc0", "hc1"], cn, M["cn_ok"])
                    for n in ("hx0", "hx1", "hc0", "hc1"):
                        await_read(pe, J, n)
                    for h in range(2):
                        pe_project(pe, J, "k" + "AB"[h], wkv2, h * P, cT)
                    for a in range(A4):
                        for h in range(2):
                            pe_project(pe, J, f"q{a}" + "AB"[h], wq2, (2 * a + h) * P, hT)
                    pe_values(pe, J, ["v0", "v1"], wkv2, D, cT)

                    def scores(j, i):
                        r = slice(32 * i, 32 * i + 32)
                        for a in range(A4):
                            for h in range(2):
                                ins = nc.tensor.matmul(S[i][:, a * P:(a + 1) * P], qr[r, a, h, j * P:(j + 1) * P],
                                                       kr[r, h, j * P:(j + 1) * P], start=(h == 0), stop=(h == 1))
                        ins.then_inc(M["scored"], 1)

                    def products(j, i):
                        name = f"pv{j}_{i}"
                        pe.wait_ge(M["pt_ok"], 4 * j + i + 1)
                        bank = claim(pe, J, name)
                        for a in range(A4):
                            ins = nc.tensor.matmul(bank[:, a * (HD + 1):(a + 1) * (HD + 1)], PT[:, j % 2, 4 * i + a, :],
                                                   V2[:, j, i, :], start=True, stop=True)
                        ins.then_inc(q_full[J[name][0]], 1)

                    def turn_out(j):
                        for i in range(4):
                            await_read(pe, J, f"pv{j}_{i}")
                        for q in range(2):
                            name = f"o{j}_{q}"
                            bank = claim(pe, J, name)
                            for f in range(4):
                                k = 4 * q + f
                                ins = nc.tensor.transpose(bank[:, f * P:(f + 1) * P], o2[:, k * P:(k + 1) * P], ident[:])
                            ins.then_inc(q_full[J[name][0]], 1)

                    pe.wait_ge(M["roped"], 2 * (1 + A4))
                    for i in range(4):
                        scores(0, i)
                    pe.wait_ge(M["ones_ok"], 1)
                    await_read(pe, J, "v0")
                    await_read(pe, J, "v1")
                    for j in range(GB + 1):
                        for i in range(4):
                            if j + 1 < GB:
                                pe.wait_ge(M["masked"], 4 * j + i + 1)
                                scores(j + 1, i)
                            if j < GB:
                                pe_turn(pe, j, i)
                            if j > 0:
                                products(j - 1, i)
                        if j > 0:
                            turn_out(j - 1)
                    for j in range(GB):
                        await_read(pe, J, f"o{j}_0")
                        await_read(pe, J, f"o{j}_1")

                    def rows_out(names, w, src):
                        for y, name in enumerate(names):
                            bank = claim(pe, J, name)
                            for jj in range(2):
                                j = 2 * y + jj
                                for f in range(FC):
                                    ins = nc.tensor.matmul(bank[:, jj * D:(jj + 1) * D], src[:, f, j * P:(j + 1) * P],
                                                           w[:, f, :], start=(f == 0), stop=(f == FC - 1))
                            ins.then_inc(q_full[J[name][0]], 1)

                    rows_out(["w0", "w1"], wo2, o2T)
                    for c in range(C):
                        bank = claim(pe, J, f"n{c}")
                        for j in range(GB):
                            if c == 0:
                                pe.wait_ge(M["xn_ok"], GB + j + 1)
                            ins = nc.tensor.transpose(bank[:, j * P:(j + 1) * P], xn[:, j, c * P:(c + 1) * P], ident[:])
                        ins.then_inc(q_full[J[f"n{c}"][0]], 1)
                    await_read(pe, J, "n0")
                    await_read(pe, J, "n1")
                    for f in range(FC):
                        pe_project(pe, J, f"g{f}", wg2, f * P, hT)
                        pe_project(pe, J, f"u{f}", wu2, f * P, hT)
                    for f in range(FC):
                        await_read(pe, J, f"u{f}")
                    rows_out(["d0", "d1"], wd2, act2)

                @block.scalar
                def _(act):
                    J = J_l2
                    act_affine(act, J, ["hx0", "hx1"], hT, "ln1", None)
                    act_affine(act, J, ["hc0", "hc1"], cT, "ln1", None)
                    for v in range(2):
                        bank = await_full(act, J, f"v{v}")
                        nc.scalar.activation(V2[:, 2 * v:2 * v + 2, :, 0:HD],
                                             bank[:, :].rearrange("p (j h d) -> p j h d", j=2, d=HD), ACT.Copy)\
                            .then_inc(q_free[J[f"v{v}"][0]], 1)

                    def out_copies(j):
                        for q in range(2):
                            name = f"o{j}_{q}"
                            bank = await_full(act, J, name)
                            nc.scalar.activation(o2T[:, 4 * q:4 * q + 4, j * P:(j + 1) * P],
                                                 bank[:, :].rearrange("p (f n) -> p f n", f=4), ACT.Copy)\
                                .then_inc(q_free[J[name][0]], 1)

                    def all_products(j):
                        for i in range(4):
                            await_full(act, J, f"pv{j}_{i}")

                    for n in range(4 * GB + 2):
                        j, i = divmod(n, 4)
                        if n < 4 * GB:
                            act.wait_ge(M["maxed"], n + 1)
                            for a in range(A4):
                                v = SP[:, j % 2, i, a, :]
                                h = 4 * i + a
                                ins = nc.scalar.activation(v, v, ACT.Exp, bias=mx[:, j % 2, h:h + 1])
                            ins.then_inc(M["probs"], 1)
                        if n >= 2:
                            act_copy_turned(act, n - 2, all_products)
                        if i == 0 and j >= 2:
                            out_copies(j - 2)
                    out_copies(GB - 1)
                    for c in range(C):
                        bank = await_full(act, J, f"n{c}")
                        nc.scalar.activation(hT[:, c, :], bank[:, :], ACT.Identity, scale=col("ln2", c))\
                            .then_inc(q_free[J[f"n{c}"][0]], 1)
                    for f in range(FC):
                        bank = await_full(act, J, f"g{f}")
                        nc.scalar.activation(act2[:, f, :], bank[:, :], ACT.Silu).then_inc(q_free[J[f"g{f}"][0]], 1)

                @block.gpsimd
                def _(pool):
                    link = chained(pool, M["pchain"])
                    nc.gpsimd.memset(V2[:, :, :, HD:HD + 1], 1.0).then_inc(M["ones_ok"], 1)

                    def rms(k, n_stats):
                        pool.wait_ge(M["stats"], n_stats)
                        link(nc.gpsimd.tensor_tensor(ve[:, k, :], mv[:, k, :, 0], mv[:, k, :, 0], ALU.mult))
                        link(nc.gpsimd.tensor_tensor(ve[:, k, :], ve[:, k, :], mv[:, k, :, 1], ALU.add))
                        link(nc.gpsimd.tensor_scalar(ve[:, k, :], ve[:, k, :], RMS_EPS, 1.0, ALU.add, ALU.mult))
                        nc.gpsimd.tensor_tensor(rstd[:, k, :], ve[:, k, :], nhalf[:], ALU.pow).then_inc(M["rstd_ok"], 1)

                    rms(0, GB)
                    rms(1, 2 * GB)
                    for r in range(1 + A4):
                        pool.wait_ge(M["multiplied"], 4 * (r + 1))
                        first, second = (kr[:, 0, :], kr[:, 1, :]) if r == 0 else (qr[:, r - 1, 0, :], qr[:, r - 1, 1, :])
                        for dst, k1, k2, op in ((first, 0, 1, ALU.subtract), (second, 2, 3, ALU.add)):
                            nc.gpsimd.tensor_tensor(dst.rearrange("p (j n) -> p j n", j=GB), products4(k1, r),
                                                    products4(k2, r), op).then_inc(M["roped"], 1)
                    rms(0, 3 * GB)

                @block.vector
                def _(dve):
                    J = J_l2
                    link = chained(dve, M["chain"])

                    def scale_rows(src, dst, k, ok):
                        for j in range(GB):
                            nc.vector.tensor_scalar(dst[:, j, :], at(src, g * GB + j), rstd[:, k, j:j + 1], None,
                                                    ALU.mult).then_inc(ok, 1)

                    dve_stats(dve, link, xres, g, 0)
                    dve_stats(dve, link, ctxr, g, 1)
                    dve.wait_ge(M["rstd_ok"], 1)
                    scale_rows(xres, xn, 0, M["xn_ok"])
                    dve.wait_ge(M["rstd_ok"], 2)
                    scale_rows(ctxr, cn, 1, M["cn_ok"])
                    cos = rope[:, 0, :].unsqueeze(1).to_broadcast([P, GB, P])
                    sin = rope[:, 1, :].unsqueeze(1).to_broadcast([P, GB, P])
                    for r in range(1 + A4):
                        n = "k" if r == 0 else f"q{r - 1}"
                        if r >= 2:
                            dve.wait_ge(M["roped"], 2 * (r - 1))
                        for half, table in ((0, ((0, cos), (3, sin))), (1, ((1, sin), (2, cos)))):
                            bank = await_full(dve, J, n + "AB"[half])
                            for k, t in table:
                                nc.vector.tensor_tensor(products4(k, r), bank[:, :].rearrange("p (j n) -> p j n", j=GB),
                                                        t, ALU.mult).then_inc(M["multiplied"], 1)
                            dve.wait_ge(M["multiplied"], 4 * r + 2 * half + 2)
                            dve.sem_inc(q_free[J[n + "AB"[half]][0]], 1)

                    def divide(j, i):
                        if i == 0 and j > 0:
                            await_full(dve, J, f"o{j - 1}_1")
                        dve_divide(dve, link, J, f"pv{j}_{i}", o2[:, 4 * i * HD:(4 * i + 4) * HD],
                                   rden[:, j % 2, 4 * i:4 * i + 4], 4, HD)

                    dve.wait_ge(ld["mask"], 16)
                    for j in range(GB + 1):
                        for i in range(4):
                            n = 4 * j + i
                            if j < GB:
                                dve.wait_ge(M["scored"], n + 1)
                                if j >= 2:
                                    dve.wait_ge(M["turned"], 4 * (j - 2) + i + 1)
                                sp4 = SP[:, j % 2, i, :, :]
                                nc.vector.scalar_tensor_tensor(
                                    out=sp4, in0=S[i][:, :].rearrange("p (a k) -> p a k", a=A4), scalar=HD ** -0.5,
                                    in1=mask2[:, bass.ds(g * GB + j, 1), :].to_broadcast([P, A4, P]),
                                    op0=ALU.mult, op1=ALU.add).then_inc(M["masked"], 1)
                                dve.wait_ge(M["masked"], n + 1)
                                nc.vector.tensor_reduce(mx[:, j % 2, 4 * i:4 * i + 4], sp4, AX, ALU.max, negate=True)\
                                    .then_inc(M["maxed"], 1)
                            if j > 0:
                                divide(j - 1, i)

                    def add_rows(names):
                        for y, name in enumerate(names):
                            bank = await_full(dve, J, name)
                            x2 = at(xres, g * GB + 2 * y, 2)
                            link(nc.vector.tensor_tensor(x2, bank[:, :].rearrange("p (j d) -> p j d", j=2), x2, ALU.add))
                            dve.sem_inc(q_free[J[name][0]], 1)

                    add_rows(["w0", "w1"])
                    dve_stats(dve, link, xres, g, 0)
                    dve.wait_ge(M["rstd_ok"], 3)
                    scale_rows(xres, xn, 0, M["xn_ok"])
                    for f in range(FC):
                        await_read(dve, J, f"g{f}")
                        bank = await_full(dve, J, f"u{f}")
                        nc.vector.tensor_tensor(act2[:, f, :], bank[:, :], act2[:, f, :], ALU.mult)\
                            .then_inc(q_free[J[f"u{f}"][0]], 1)
                    add_rows(["d0", "d1"])
            end_turn()

        part = small[:, 32:36]
        gamma, half_step, minus = small[:, 36:40], small[:, 40:44], small[:, 44:48]
        up_w, down_w = view(2048, [C, D]), view(2560, [C, D])
        with nc.Block(no_gpsimd_drain=True) as block:
            @block.tensor
            def _(pe):
                pe.wait_ge(M["maxed"], 4)
                nc.tensor.matmul(Q[0][:, 0:4], ones[:, :], part, start=True, stop=True).then_inc(M["scored"], 1)

            @block.vector
            def _(dve):
                link = chained(dve, M["chain"])
                dve.wait_ge(ld["l3"], 16)
                W4 = [w_l3[:, :, k * D:(k + 1) * D] for k in range(4)]
                for k in range(4):
                    nc.vector.tensor_reduce(part[:, k:k + 1], W4[k], mybir.AxisListType.XY, ALU.add,
                                            apply_absolute_value=True).then_inc(M["maxed"], 1)
                dve.wait_ge(M["scored"], 1)
                link(nc.vector.tensor_scalar(gamma, Q[0][:, 0:4], 1.0 / (D * D), None, ALU.mult))
                link(nc.vector.tensor_scalar(half_step, gamma, LN_EPS, 0.5, ALU.add, ALU.mult))
                link(nc.vector.tensor_scalar(minus, half_step, -1.0, None, ALU.mult))
                for k in range(4):
                    link(nc.vector.tensor_scalar(up_w, W4[k], half_step[:, k:k + 1], gamma[:, k:k + 1], ALU.is_gt, ALU.mult))
                    link(nc.vector.tensor_scalar(down_w, W4[k], minus[:, k:k + 1], gamma[:, k:k + 1], ALU.is_lt, ALU.mult))
                    link(nc.vector.tensor_tensor(up_w, up_w, down_w, ALU.subtract))
                    link(nc.vector.tensor_tensor(up_w, up_w, W4[k], ALU.subtract))
                    link(nc.vector.tensor_tensor(W4[k], W4[k], up_w, ALU.add))
        end_turn()
        attention(("l3_g", "l3_b"), "raw", w_l3, "l3_bq", "l3_bk", "l3_bv", "l3_ob", ["l3"], store=True)


def shape_tables():
    d = np.arange(P) % HALF
    inv = (1.0 / np.float32(10000.0) ** (np.arange(0, HD, 2, dtype=np.float32) / np.float32(HD))).astype(np.float32)
    angle = np.arange(P, dtype=np.float32)[None, :] * inv[d][:, None]
    rope = np.stack([np.cos(angle), np.sin(angle)], axis=1).astype(np.float32)
    p = np.arange(P)
    odd = (p // DH) % 2
    parity = np.stack([1 - odd, odd], axis=1)
    before = p[None, :] < p[:, None]
    ranks = np.broadcast_to(np.where(np.arange(R) < TOPK, np.arange(R), -1)[None], (P, R))
    e = np.arange(E)
    ebefore = np.broadcast_to((e[None, :] < e[:, None]).reshape(1, E * E), (P, E * E))
    table = np.concatenate([parity, before, ranks, ebefore], axis=1).astype(np.float32)
    return rope, table


def lay_out(i):
    def chunks(v):
        return v.reshape(C, P).T

    def thirds(name, v):
        return [v[k * D:(k + 1) * D] for k in range(3)]

    L0, L1, L2, L3 = "L0_xattn_", "L1_xattn_", "L2_xattn_", "L3_xattn_"
    sq, sk, sv = thirds("sa", i[L0 + "sa_in_b"])
    cq, ck, cv = thirds("ca", i[L0 + "ca_in_b"])
    oq, ok, ov = thirds("l1", i[L1 + "in_proj_b"])
    vec = {"sa_g": i[L0 + "sa_ln_g"], "sa_b": i[L0 + "sa_ln_b"], "sa_bq": sq, "sa_bk": sk, "sa_bv": sv,
           "cq_g": i[L0 + "ca_q_ln_g"], "cq_b": i[L0 + "ca_q_ln_b"], "ck_g": i[L0 + "ca_kv_ln_g"],
           "ck_b": i[L0 + "ca_kv_ln_b"], "ca_bq": cq, "ca_bk": ck, "ca_bv": cv,
           "me_g": i[L0 + "moe_ln_g"], "me_b": i[L0 + "moe_ln_b"], "l1_bq": oq, "l1_bk": ok, "l1_bv": ov,
           "ln1": i[L2 + "ln1_w"], "ln2": i[L2 + "ln2_w"], "l3_g": i[L3 + "ln_gamma"], "l3_b": i[L3 + "ln_beta"],
           "l3_bq": i[L3 + "bq"], "l3_bk": i[L3 + "bk"], "l3_bv": i[L3 + "bv"]}
    rows = {"sa_ob": i[L0 + "sa_out_b"], "ca_ob": i[L0 + "ca_out_b"], "l1_ob": i[L1 + "out_b"], "l3_ob": i[L3 + "bo"],
            "l1_sw": i[L1 + "score_w"].reshape(D)}
    rope, table = shape_tables()
    cat = np.concatenate
    out = {
        "x": i["x"], "ctx": i["ctx_1024"], "mask": i["mask_Bx1xSxS2_ff0"].reshape(B, P, P),
        "cols": cat([chunks(vec[n]) for n in COLS], axis=1),
        "rows": np.broadcast_to(np.stack([rows[n] for n in ROWS])[None], (P, len(ROWS), D)),
        "fc1b": i[L0 + "e_fc1_b"].reshape(E * FC, P).T, "fc2b": i[L0 + "e_fc2_b"],
        "rw": i[L0 + "router_w"].T, "rb": i[L0 + "router_b"].reshape(E, 1),
        "sbias": np.broadcast_to(i[L1 + "score_b"].reshape(1, 1), (P, 1)),
        "rope": rope, "shape_c": table,
        "w_sa": cat([i[L0 + "sa_in_w"].T, i[L0 + "sa_out_w"].T], axis=1),
        "w_ca": cat([i[L0 + "ca_in_w"].T, i[L0 + "ca_out_w"].T], axis=1),
        "w_l1": cat([i[L1 + "in_proj_w"].T, i[L1 + "out_w"].T], axis=1),
        "w_l3": cat([i[L3 + n].T for n in ("Wq", "Wk", "Wv", "Wo")], axis=1),
        "fc1": i[L0 + "e_fc1_w"].transpose(0, 2, 1).reshape(E * D, FF),
        "fc2": i[L0 + "e_fc2_w"].transpose(0, 2, 1).reshape(E * FF, D),
        "wq2": i[L2 + "Wq"].reshape(D, NKV, H // NKV, 2, HALF).transpose(0, 2, 3, 1, 4).reshape(D, FF),
        "wkv2": cat([i[L2 + "Wk"].reshape(D, NKV, 2, HALF).transpose(0, 2, 1, 3).reshape(D, D), i[L2 + "Wv"]], axis=1),
        "wo2": i[L2 + "Wo"], "wg2": i[L2 + "Wgate"], "wu2": i[L2 + "Wup"], "wd2": i[L2 + "Wdown"],
    }
    return {n: np.ascontiguousarray(a) for n, a in out.items()}


def kernel(**inputs):
    import concourse.bacc as bacc
    from concourse.bass_utils import run_bass_kernel_spmd

    arrays = lay_out({n: np.asarray(a) for n, a in inputs.items()})
    nc = bacc.Bacc("TRN2", target_bir_lowering=False, num_devices=1)
    aps = {n: nc.dram_tensor("in_" + n, a.shape, mybir.dt.from_np(a.dtype), kind="ExternalInput").ap()
           for n, a in arrays.items()}
    out = nc.dram_tensor("out", (B, P, D), F32, kind="ExternalOutput").ap()
    build(nc, aps, out)
    r = run_bass_kernel_spmd(nc, [{"in_" + n: a for n, a in arrays.items()}], core_ids=[0])
    return r.results[0]["out"]
```

```python
from contextlib import ExitStack

import numpy as np

import concourse.bass as bass
from concourse import mybir

F32 = mybir.dt.float32
ALU = mybir.AluOpType
ACT = mybir.ActivationFunctionType
AX = mybir.AxisListType.X

P = 128
B = 16
D = 256
C = D // P
GB = 4
G = B // GB
NT = GB * P
H = 16
DH = D // H
E = 8
FF = 1024
FC = FF // P
HD = 64
NKV = 4
HALF = HD // 2
BT = 3
BR = BT * P
NSTEP = -(-B * P // BR)
NBLK = (2 * B * P + E * (BR - 1)) // BR
NBLK += NBLK % 2
TOPK = 10
R = 32
LN_EPS = 1e-5
RMS_EPS = 1e-6

COLS = ["sa_g", "sa_b", "sa_bq", "sa_bk", "sa_bv", "cq_g", "cq_b", "ck_g", "ck_b", "ca_bq", "ca_bk", "ca_bv",
        "me_g", "me_b", "l1_bq", "l1_bk", "l1_bv", "ln1", "ln2", "l3_g", "l3_b", "l3_bq", "l3_bk", "l3_bv"]
ROWS = ["sa_ob", "ca_ob", "l1_ob", "l3_ob", "l1_sw"]


class Jobs:

    def __init__(self, names):
        self.at = {n: (k % 2, k // 2) for k, n in enumerate(names)}
        assert len(self.at) == len(names)

    def __getitem__(self, name):
        return self.at[name]


def build(nc, A, out):
    with ExitStack() as ctx:
        def sb(name, shape, dt=F32):
            return ctx.enter_context(nc.sbuf_tensor(name, shape, dt))

        def sem(name):
            return ctx.enter_context(nc.semaphore(name))

        xres = sb("xres", [P, B, D])
        ctxr = sb("ctxr", [P, B, D])
        w_sa = sb("w_sa", [P, C, 4 * D])
        w_ca = sb("w_ca", [P, C, 4 * D])
        w_l1 = sb("w_l1", [P, C, 4 * D])
        w_l3 = sb("w_l3", [P, C, 4 * D])
        cols = sb("cols", [P, 2 * len(COLS)])
        rows = sb("rows", [P, len(ROWS), D])
        fc1b = sb("fc1b", [P, E * FC])
        fc2b = sb("fc2b", [E, D])
        rw = sb("rw", [P, C, E])
        rb = sb("rb", [E, 1])
        sbias = sb("sbias", [P, 1])
        rope = sb("rope", [P, 2, P])
        shape_c = sb("shape_c", [P, 8 + P + R + E * E + NSTEP + NBLK])
        of_four = shape_c[:, 0:4]
        of_key_head = shape_c[:, 4:8]
        before = shape_c[:, 8:8 + P]
        ranks = shape_c[:, 8 + P:8 + P + R]
        ebefore = shape_c[:, 8 + P + R:8 + P + R + E * E].rearrange("p (e f) -> p e f", e=E)
        steps = shape_c[:, 8 + P + R + E * E:8 + P + R + E * E + NSTEP]
        block_ids = shape_c[:, 8 + P + R + E * E + NSTEP:]
        ident = sb("ident", [P, P])
        ones = sb("ones", [P, P])
        nhalf = sb("nhalf", [P, GB])

        st = sb("st", [P, 2, GB, 6])
        mv = sb("mv", [P, 2, GB, 2])
        ve = sb("ve", [P, 2, GB])
        rstd = sb("rstd", [P, 2, GB])
        mx = sb("mx", [P, 2, H])
        psum = sb("psum", [P, 2, H])
        rden = sb("rden", [P, 2, H])
        small = sb("small", [P, 64])
        gates = sb("gates", [P, B, E])
        logit = sb("logit", [P, B, E])
        gl1 = sb("gl1", [P, B, E])
        pick_gate = sb("pick_gate", [P, 2, B])
        pick_row = sb("pick_row", [P, 2, B], mybir.dt.int32)
        block_expert = sb("block_expert", [P, NBLK], mybir.dt.int32)

        xs_dram = nc.dram_tensor("sorted_rows", (NBLK * BR, D), F32, kind="Internal").ap()
        ys_dram = nc.dram_tensor("expert_rows", (NBLK * BR, D), F32, kind="Internal").ap()

        W = 33280
        reg = sb("reg", [P, W])

        def view(at, shape):
            n = int(np.prod(shape))
            assert at + n <= W, (at, n)
            v = reg[:, at:at + n]
            if len(shape) == 1:
                return v
            names = "abcd"[:len(shape)]
            return v.rearrange(f"p ({' '.join(names)}) -> p {' '.join(names)}",
                               **{k: s for k, s in zip(names[:-1], shape)})

        xn = view(0, [GB, D])
        cn = view(1024, [GB, D])
        hT = view(2048, [C, NT])
        cT = view(3072, [C, NT])
        SP = view(4096, [2, 4, 4, P])
        PT = view(8192, [2, H, P])
        qT = view(12288, [C, NT])
        kM = view(13312, [4, C, NT])
        VA = view(17408, [GB, H, 2 * DH])
        oT = view(19456, [C, NT])
        xs = view(0, [GB, D])
        colb = view(12288, [GB, P])
        gat = view(12800, [GB, R])
        gatT = view(12928, [P])
        yo = view(13056, [D])
        xsT = view(20480, [C, P])
        q1T = view(20736, [C, P])
        junk = view(20992, [D])
        xnall = view(13312, [B, D])
        up_w8 = [view(5120 + 2048 * k, [C, FF]) for k in range(2)]
        down_w8 = [view(9216 + 2048 * k, [FC, D]) for k in range(2)]
        xb = view(0, [2, BT, D])
        xbT = view(2048, [2, C, BR])
        h1 = view(13312, [2, FC, BR])
        yb = view(19968, [2, BT, D])
        picked = view(5120, [2 * B, D])
        lt = view(21504, [NT])
        l2w = 22016
        wq2 = view(l2w, [C, FF])
        wkv2 = view(l2w + 2048, [C, 2 * D])
        wo2 = view(l2w + 3072, [FC, D])
        wg2 = view(l2w + 5120, [C, FF])
        wu2 = view(l2w + 7168, [C, FF])
        wd2 = view(l2w + 9216, [FC, D])
        qr = view(12288, [GB, 2, NT])
        kr = view(0, [2, NT])
        kM2 = view(16384, [NKV, 2, NT])
        V2 = view(20480, [GB, NKV, HD])
        o2T = view(0, [FC, NT])
        act2 = view(12288, [FC, NT])
        mask2 = w_sa[:, :, :].rearrange("p c n -> p (c n)").rearrange("p (b k) -> p b k", b=B)
        rt = w_ca[:, :, :].rearrange("p c n -> p (c n)").rearrange("p (a n) -> p a n", a=4)

        banks = [ctx.enter_context(nc.psum_tensor(f"bank{i}", [P, 512], F32)) for i in range(8)]
        S = banks[0:4]
        T = banks[4:6]
        Q = banks[6:8]

        ld = {n: sem("ld_" + n) for n in ("x", "ctx", "small", "sa", "ca", "l1", "l3", "l2", "zeros", "mask")}
        ld_picked = [sem(f"ld_picked{k}") for k in range(G)]
        names = ["q_full0", "q_full1", "q_free0", "q_free1", "chain", "pchain", "const", "stats", "rstd_ok", "xn_ok",
                 "cn_ok", "summed", "divided", "scaled", "values_ok", "scored", "masked", "shifted", "maxed", "probs", "turned", "pt_ok", "biased",
                 "stored", "done", "multiplied", "roped", "act_ok", "fc1_full", "fc1_free", "fc2_full", "y_ok",
                 "up_in0", "up_in1", "down_in0", "down_in1", "rows_in0", "rows_in1", "y_out", "turned_in", "routed", "keys_ok",
                 "counted", "scattered", "xs_ok", "colb_ok", "gat_ok", "exp_ok", "gates_ok"]
        M = {n: sem(n) for n in names}
        turn_sems = range(M[names[0]].num, M[names[-1]].num + 1)
        assert len(turn_sems) == len(names)
        q_full = [M["q_full0"], M["q_full1"]]
        q_free = [M["q_free0"], M["q_free1"]]

        def end_turn():
            nc.all_engine_barrier(sems_to_clear=turn_sems)

        def col(name, c):
            k = COLS.index(name)
            return cols[:, 2 * k + c:2 * k + c + 1]

        def row(name):
            return rows[:, ROWS.index(name), :]

        def at(t, b, n=1):
            v = t[:, bass.ds(b, n), :]
            return v.rearrange("p a d -> p (a d)") if n == 1 else v

        def claim(pe, J, name):
            b, k = J[name]
            if k > 0:
                pe.wait_ge(q_free[b], k)
            return Q[b]

        def await_full(eng, J, name):
            b, k = J[name]
            eng.wait_ge(q_full[b], k + 1)
            return Q[b]

        def await_read(eng, J, name):
            b, k = J[name]
            eng.wait_ge(q_free[b], k + 1)

        def chained(eng, s):
            n = [0]

            def link(ins):
                n[0] += 1
                ins.then_inc(s, 1)
                eng.wait_ge(s, n[0])
            return link

        ZN = NBLK * BR * D // P // 9
        zeros = view(20480, [ZN])
        with nc.Block(no_gpsimd_drain=True) as block:
            @block.sync
            def _(sp):
                sp.dma_start(xres[:], A["x"].rearrange("b p d -> p b d")).then_inc(ld["x"], 16)
                sp.dma_start(w_sa[:], A["w_sa"].rearrange("(c p) n -> p c n", p=P)).then_inc(ld["sa"], 16)

            @block.scalar
            def _(act):
                for t, n in ((cols, "cols"), (rows, "rows"), (fc1b, "fc1b"), (fc2b, "fc2b"), (rb, "rb"), (sbias, "sbias"),
                             (rope, "rope"), (shape_c, "shape_c")):
                    act.dma_start(t[:], A[n]).then_inc(ld["small"], 16)
                act.dma_start(rw[:], A["rw"].rearrange("(c p) e -> p c e", p=P)).then_inc(ld["small"], 16)
                act.wait_ge(ld["small"], 16 * 9)

            @block.gpsimd
            def _(pool):
                nc.gpsimd.memset(ident[:], 0.0).then_inc(M["const"], 1)
                nc.gpsimd.memset(ones[:], 1.0)
                nc.gpsimd.memset(nhalf[:], -0.5)
                nc.gpsimd.memset(zeros, 0.0)
                pool.wait_ge(M["const"], 1)
                nc.gpsimd.affine_select(out=ident[:], in_=ident[:], compare_op=ALU.not_equal, fill=1.0, base=0,
                                        pattern=[[-1, P]], channel_multiplier=1)

        end_turn()

        def load_the_rest(sp):
            sp.dma_start(ctxr[:], A["ctx"].rearrange("b p d -> p b d")).then_inc(ld["ctx"], 16)
            for n, t in (("ca", w_ca), ("l1", w_l1), ("l3", w_l3)):
                sp.dma_start(t[:], A["w_" + n].rearrange("(c p) n -> p c n", p=P)).then_inc(ld[n], 16)
            for k in range(9):
                sp.dma_start(xs_dram.rearrange("(p r) d -> p (r d)", p=P)[:, k * ZN:(k + 1) * ZN], zeros)\
                    .then_inc(ld["zeros"], 16)
            for n, t in (("wq2", wq2), ("wkv2", wkv2), ("wo2", wo2), ("wg2", wg2), ("wu2", wu2), ("wd2", wd2)):
                sp.dma_start(t, A[n].rearrange("(c p) n -> p c n", p=P)).then_inc(ld["l2"], 16)

        def dve_stats(dve, link, src, g, k):
            for j in range(GB):
                last = nc.vector.bn_stats(st[:, k, j, :], at(src, g * GB + j))
            link(last)
            for j in range(GB):
                nc.vector.bn_aggr(mv[:, k, j, :], st[:, k, j, :]).then_inc(M["stats"], 1)

        def pool_copy(pool, g):
            for j in range(GB):
                nc.gpsimd.tensor_copy(cn[:, j, :], at(ctxr, g * GB + j)).then_inc(M["cn_ok"], 1)

        def pool_rstd(pool, link, k, n_stats, eps):
            pool.wait_ge(M["stats"], n_stats)
            link(nc.gpsimd.tensor_scalar(ve[:, k, :], mv[:, k, :, 1], eps, 1.0, ALU.add, ALU.mult))
            nc.gpsimd.tensor_tensor(rstd[:, k, :], ve[:, k, :], nhalf[:], ALU.pow).then_inc(M["rstd_ok"], 1)

        def dve_centre(dve, src, dst, g, k, ok, batches=range(GB)):
            for j in batches:
                nc.vector.tensor_scalar(dst[:, j, :], at(src, g * GB + j), mv[:, k, j, 0:1], rstd[:, k, j:j + 1],
                                        ALU.subtract, ALU.mult).then_inc(ok, 1)

        def pe_turn_rows(pe, J, names, src, ok):
            for c in range(C):
                bank = claim(pe, J, names[c])
                for j in range(GB):
                    if c == 0:
                        pe.wait_ge(ok, j + 1)
                    ins = nc.tensor.transpose(bank[:, j * P:(j + 1) * P], src[:, j, c * P:(c + 1) * P], ident[:])
                ins.then_inc(q_full[J[names[c]][0]], 1)

        def act_affine(act, J, names, dst, gain, bias):
            for c in range(C):
                bank = await_full(act, J, names[c])
                if gain is None:
                    ins = nc.scalar.activation(dst[:, c, :], bank[:, :], ACT.Copy)
                else:
                    ins = nc.scalar.activation(dst[:, c, :], bank[:, :], ACT.Identity, scale=col(gain, c),
                                               bias=col(bias, c) if bias else 0.0)
                ins.then_inc(q_free[J[names[c]][0]], 1)

        def pe_project(pe, J, name, w, w0, src, n=NT):
            bank = claim(pe, J, name)
            for c in range(C):
                ins = nc.tensor.matmul(bank[:, 0:n], w[:, c, w0:w0 + P], src[:, c, :], start=(c == 0), stop=(c == C - 1))
            ins.then_inc(q_full[J[name][0]], 1)

        def pe_values(pe, J, names, w, w0, src):
            for v, name in enumerate(names):
                bank = claim(pe, J, name)
                for jj in range(2):
                    j = 2 * v + jj
                    for c in range(C):
                        ins = nc.tensor.matmul(bank[:, jj * D:(jj + 1) * D], src[:, c, j * P:(j + 1) * P],
                                               w[:, c, w0:w0 + D], start=(c == 0), stop=(c == C - 1))
                ins.then_inc(q_full[J[name][0]], 1)

        def act_values(act, J, names):
            for v, name in enumerate(names):
                bank = await_full(act, J, name)
                pairs = VA[:, 2 * v:2 * v + 2, :, :].rearrange("p j h d -> p (j h d)")\
                    .rearrange("p (n s d) -> p n s d", s=4, d=DH)[:, :, 0:4:3, :]
                nc.scalar.activation(pairs, bank[:, :].rearrange("p (n s d) -> p n s d", s=2, d=DH), ACT.Copy)\
                    .then_inc(q_free[J[name][0]], 1)

        def dve_keys(dve, J, m, bias):
            bank = await_full(dve, J, f"k{m}")
            for k in range(4):
                ins = nc.vector.tensor_scalar(kM[:, k, m, :], bank[:, :], col(bias, m), of_four[:, k:k + 1],
                                              ALU.add, ALU.mult)
            ins.then_inc(q_free[J[f"k{m}"][0]], 1)

        def pe_scores(pe, j, i):
            r = slice(64 * (i % 2), 64 * (i % 2) + 64)
            nc.tensor.matmul(S[i][:, :], qT[r, i // 2, j * P:(j + 1) * P], kM[r, :, i // 2, j * P:(j + 1) * P],
                             start=True, stop=True).then_inc(M["scored"], 1)

        def bank_of(n):
            return SP[:, (n // 4) % 2, n % 4, :, :], S[n % 4][:, :].rearrange("p (s k) -> p s k", k=P)

        def cols_of(t, n):
            return t[:, (n // 4) % 2, 4 * (n % 4):4 * (n % 4) + 4]

        def spread(t, n):
            return cols_of(t, n).unsqueeze(2).to_broadcast([P, 4, P])

        TURN_LAG = 1
        COPY_LAG = 4 + TURN_LAG

        def dve_softmax(dve, N, pv_done, between=None):
            for n in range(N + COPY_LAG):
                if n < N:
                    dve.wait_ge(M["scored"], n + 1)
                    nc.vector.tensor_reduce(cols_of(mx, n), bank_of(n)[1], AX, ALU.max, negate=True)\
                        .then_inc(M["maxed"], 1)
                if 2 <= n < N + 2:
                    dve.wait_ge(M["probs"], n - 1)
                    nc.vector.reciprocal(cols_of(rden, n - 2), cols_of(psum, n - 2)).then_inc(M["divided"], 1)
                if n >= COPY_LAG:
                    m = n - COPY_LAG
                    dve.wait_ge(M["turned"], m + 1)
                    if m >= 8:
                        pv_done(m // 4 - 2)
                    nc.vector.tensor_copy(turned_tile(m), T[m % 2][:, :].rearrange("p (s q) -> p s q", q=P))\
                        .then_inc(M["pt_ok"], 1)
                if between:
                    between(n)

        def turned_tile(m):
            return PT[:, (m // 4) % 2, 4 * (m % 4):4 * (m % 4) + 4, :]

        def pool_scale(pool, m):
            pool.wait_ge(M["divided"], m + 1)
            v = bank_of(m)[0]
            nc.gpsimd.tensor_tensor(v, v, spread(rden, m), ALU.mult).then_inc(M["scaled"], 1)

        def act_exp(act, n, source):
            act.wait_ge(M["maxed"], n + 1)
            if n >= 8:
                act.wait_ge(M["turned"], n - 7)
            for a in range(4):
                ins = nc.scalar.activation(bank_of(n)[0][:, a, :], source[:, a, :], ACT.Exp,
                                           bias=cols_of(mx, n)[:, a:a + 1], accum_out=cols_of(psum, n)[:, a:a + 1])
            ins.then_inc(M["probs"], 1)

        def pe_turn(pe, n):
            pe.wait_ge(M["scaled"], n + 1)
            if n >= 2:
                pe.wait_ge(M["pt_ok"], n - 1)
            for s in range(4):
                ins = nc.tensor.transpose(T[n % 2][:, s * P:(s + 1) * P], bank_of(n)[0][:, s, :], ident[:])
            ins.then_inc(M["turned"], 1)

        def pe_products(pe, bank, j, out_cols, in_cols, half):
            for m in range(C):
                for par in range(2):
                    for x in range(4):
                        h = 8 * m + 2 * x + par
                        ins = nc.tensor.matmul(bank[32 * x:32 * x + 32, m * P + out_cols.start:m * P + out_cols.stop],
                                               VA[:, j, h, :], PT[:, half, h, in_cols],
                                               start=(par == 0), stop=(par == 1))
            return ins

        def act_products(act, J, name, bv, dst_cols):
            bank = await_full(act, J, name)
            for c in range(C):
                ins = nc.scalar.activation(oT[:, c, dst_cols], bank[:, c * P:(c + 1) * P], ACT.Identity, bias=col(bv, c))
            ins.then_inc(q_free[J[name][0]], 1)

        def attention(q_norm, kv, w, bq, bk, bv, ob, loads, store=False):
            turn = ["hx0", "hx1"] + ([] if kv == "self" else ["hc0", "hc1"])
            J_first = Jobs(turn)
            J = Jobs(["q0", "q1", "k0", "k1", "v0", "v1", "pv0", "pv1", "pv2"] + turn + ["y0", "pv3", "y1"])
            kvT = hT if kv == "self" else cT

            def pe_turn_group(pe, J):
                pe_turn_rows(pe, J, ["hx0", "hx1"], xn, M["xn_ok"])
                if kv != "self":
                    pe_turn_rows(pe, J, ["hc0", "hc1"], cn, M["cn_ok"])

            def act_norm_group(act, J):
                act_affine(act, J, ["hx0", "hx1"], hT, *q_norm)
                if kv == "norm":
                    act_affine(act, J, ["hc0", "hc1"], cT, "ck_g", "ck_b")
                elif kv == "raw":
                    act_affine(act, J, ["hc0", "hc1"], cT, None, None)

            def pool_norm_group(pool, link, g):
                pool_rstd(pool, link, 0, GB, LN_EPS)
                if kv == "norm":
                    pool_rstd(pool, link, 1, 2 * GB, LN_EPS)
                if kv == "raw":
                    pool_copy(pool, g)

            def dve_stats_group(dve, link, g):
                dve_stats(dve, link, xres, g, 0)
                if kv == "norm":
                    dve_stats(dve, link, ctxr, g, 1)

            def dve_centre_group(dve, g):
                dve.wait_ge(M["rstd_ok"], 1)
                dve_centre(dve, xres, xn, g, 0, M["xn_ok"])
                if kv == "norm":
                    dve.wait_ge(M["rstd_ok"], 2)
                    dve_centre(dve, ctxr, cn, g, 1, M["cn_ok"])

            with nc.Block(no_gpsimd_drain=True) as block:
                @block.tensor
                def _(pe):
                    pe_turn_group(pe, J_first)

                @block.scalar
                def _(act):
                    act_norm_group(act, J_first)

                @block.gpsimd
                def _(pool):
                    if kv == "raw":
                        pool.wait_ge(ld["ctx"], 16)
                    nc.gpsimd.memset(VA[:, :, :, :], 0.0)
                    pool_norm_group(pool, chained(pool, M["pchain"]), 0)

                @block.vector
                def _(dve):
                    dve.wait_ge(ld["x"], 16)
                    if kv == "norm":
                        dve.wait_ge(ld["ctx"], 16)
                    dve_stats_group(dve, chained(dve, M["chain"]), 0)
                    dve_centre_group(dve, 0)

                @block.sync
                def _(sp):
                    if kv == "self":
                        load_the_rest(sp)
            end_turn()

            N = 4 * GB
            with nc.Fori(0, G) as g:
                g_next = (g + 1) & (G - 1)
                with nc.Block(no_gpsimd_drain=True) as block:
                    @block.tensor
                    def _(pe):
                        for s in loads:
                            pe.wait_ge(ld[s], 16)
                        for m in range(C):
                            pe_project(pe, J, f"q{m}", w, m * P, hT)
                        for m in range(C):
                            pe_project(pe, J, f"k{m}", w, D + m * P, kvT)
                        for n in ("q0", "q1", "k0", "k1"):
                            await_read(pe, J, n)
                        for i in range(4):
                            pe_scores(pe, 0, i)
                        pe_values(pe, J, ["v0", "v1"], w, 2 * D, kvT)

                        def products(j):
                            pe.wait_ge(M["pt_ok"], 4 * j + 4)
                            if j == 0:
                                await_read(pe, J, "v0")
                                await_read(pe, J, "v1")
                            bank = claim(pe, J, f"pv{j}")
                            pe_products(pe, bank, j, slice(0, P), slice(0, P), j % 2).then_inc(q_full[J[f"pv{j}"][0]], 1)

                        def out_rows(y):
                            await_read(pe, J, f"pv{2 * y}")
                            await_read(pe, J, f"pv{2 * y + 1}")
                            bank = claim(pe, J, f"y{y}")
                            for jj in range(2):
                                j = 2 * y + jj
                                for c in range(C):
                                    ins = nc.tensor.matmul(bank[:, jj * D:(jj + 1) * D], oT[:, c, j * P:(j + 1) * P],
                                                           w[:, c, 3 * D:4 * D], start=(c == 0), stop=(c == C - 1))
                            ins.then_inc(q_full[J[f"y{y}"][0]], 1)

                        for n in range(N + TURN_LAG):
                            if n + 4 < N:
                                pe.wait_ge(M["probs"], n + 1)
                                pe_scores(pe, n // 4 + 1, n % 4)
                            m = n - TURN_LAG
                            if m >= 0:
                                pe_turn(pe, m)
                            if m % 4 == 2 and m > 4:
                                products(m // 4 - 1)
                        pe_turn_group(pe, J)
                        out_rows(0)
                        products(GB - 1)
                        out_rows(1)

                    @block.scalar
                    def _(act):
                        for m in range(C):
                            bank = await_full(act, J, f"q{m}")
                            nc.scalar.activation(qT[:, m, :], bank[:, :], ACT.Identity, bias=col(bq, m))\
                                .then_inc(q_free[J[f"q{m}"][0]], 1)

                        for n in range(N):
                            act_exp(act, n, bank_of(n)[1])
                            if n == 3:
                                act_values(act, J, ["v0", "v1"])
                            j = (n - 10 - TURN_LAG) // 4
                            if j >= 0 and n == 4 * j + 10 + TURN_LAG:
                                act_products(act, J, f"pv{j}", bv, slice(j * P, (j + 1) * P))
                        act_products(act, J, "pv2", bv, slice(2 * P, 3 * P))
                        act_norm_group(act, J)
                        act_products(act, J, "pv3", bv, slice(3 * P, 4 * P))

                    @block.gpsimd
                    def _(pool):
                        link = chained(pool, M["pchain"])
                        for j in range(GB):
                            nc.gpsimd.tensor_tensor(at(xres, g * GB + j), at(xres, g * GB + j), row(ob), ALU.add)\
                                .then_inc(M["biased"], 1)
                        for n in range(N):
                            pool_scale(pool, n)
                            if n == 2:
                                pool_norm_group(pool, link, g_next)

                    @block.vector
                    def _(dve):
                        link = chained(dve, M["chain"])
                        for m in range(C):
                            dve_keys(dve, J, m, bk)

                        def between(n):
                            if n == 5:
                                dve_stats(dve, link, xres, g_next, 0)
                            if n == 7 and kv == "norm":
                                dve_stats(dve, link, ctxr, g_next, 1)
                            j = n - 9
                            if j == 0:
                                dve.wait_ge(M["rstd_ok"], 2 if kv == "norm" else 1)
                            if 0 <= j < GB:
                                dve_centre(dve, xres, xn, g_next, 0, M["xn_ok"], [j])
                                if kv == "norm":
                                    dve_centre(dve, ctxr, cn, g_next, 1, M["cn_ok"], [j])
                        dve_softmax(dve, N, lambda j: await_full(dve, J, f"pv{j}"), between)
                        dve.wait_ge(M["biased"], GB)
                        for y in range(2):
                            bank = await_full(dve, J, f"y{y}")
                            x2 = at(xres, g * GB + 2 * y, 2)
                            nc.vector.tensor_tensor(x2, bank[:, :].rearrange("p (j d) -> p j d", j=2), x2, ALU.add)\
                                .then_inc(q_free[J[f"y{y}"][0]], 1)

                    @block.sync
                    def _(sp):
                        if store:
                            await_read(sp, J, "y0")
                            await_read(sp, J, "y1")
                            sp.dma_start(out.rearrange("b p d -> p b d")[:, bass.ds(g * GB, GB), :],
                                         at(xres, g * GB, GB)).then_inc(M["done"], 16)
                            sp.wait_ge(M["done"], 16)
                end_turn()

        attention(("sa_g", "sa_b"), "self", w_sa, "sa_bq", "sa_bk", "sa_bv", "sa_ob", ["sa"])
        attention(("cq_g", "cq_b"), "norm", w_ca, "ca_bq", "ca_bk", "ca_bv", "ca_ob", ["ca"])

        with nc.Block(no_gpsimd_drain=True) as block:
            @block.sync
            def _(sp):
                sp.wait_ge(ld["zeros"], 16 * 9)
                sp.dma_start(mask2, A["mask"].rearrange("b q k -> q b k")).then_inc(ld["mask"], 16)

        def expert_of(eng, k):
            return eng.value_load(block_expert[0:1, bass.ds(k, 1)], min_val=0, max_val=E - 1)

        def load_up(sp, block_k, k, s):
            e = expert_of(sp, block_k)
            sp.dma_start(up_w8[k], A["fc1"][bass.ds(e * D, D), :].rearrange("(c p) f -> p c f", p=P)).then_inc(s, 16)

        def load_down(sp, block_k, k, s):
            e = expert_of(sp, block_k)
            sp.dma_start(down_w8[k], A["fc2"][bass.ds(e * FF, FF), :].rearrange("(f p) d -> p f d", p=P)).then_inc(s, 16)

        def load_rows(sp, block_k, k):
            sp.dma_start(xb[:, k, :, :], xs_dram[bass.ds(block_k * BR, BR), :].rearrange("(t p) d -> p t d", p=P))\
                .then_inc(M[f"rows_in{k}"], 16)

        def pe_block_rows(pe, k):
            pe.wait_ge(M[f"rows_in{k}"], 16)
            for c in range(C):
                for t in range(BT):
                    ins = nc.tensor.transpose(S[2 * k + c][:, t * P:(t + 1) * P], xb[:, k, t, c * P:(c + 1) * P], ident[:])
            ins.then_inc(M["turned_in"], 1)

        def act_block_rows(act, k):
            act.wait_ge(M["turned_in"], k + 1)
            for c in range(C):
                nc.scalar.activation(xbT[:, k, c, :], S[2 * k + c][:, 0:BR], ACT.Identity, scale=col("me_g", c),
                                     bias=col("me_b", c))

        J_route = Jobs(["hx0", "hx1", "logits", "turned"])
        with nc.Fori(0, G) as g:
            with nc.Block(no_gpsimd_drain=True) as block:
                @block.tensor
                def _(pe):
                    J = J_route
                    pe_turn_rows(pe, J, ["hx0", "hx1"], xn, M["xn_ok"])
                    await_read(pe, J, "hx0")
                    await_read(pe, J, "hx1")
                    bank = claim(pe, J, "logits")
                    for c in range(C):
                        ins = nc.tensor.matmul(bank[0:E, :], rw[:, c, :], hT[:, c, :],
                                               start=(c == 0), stop=(c == C - 1))
                    ins.then_inc(q_full[J["logits"][0]], 1)
                    await_read(pe, J, "logits")
                    bank = claim(pe, J, "turned")
                    for j in range(GB):
                        ins = nc.tensor.transpose(bank[:, j * E:(j + 1) * E], lt[0:E, j * P:(j + 1) * P], ident[0:E, 0:E])
                    ins.then_inc(q_full[J["turned"][0]], 1)

                @block.scalar
                def _(act):
                    J = J_route
                    for c in range(C):
                        bank = await_full(act, J, f"hx{c}")
                        nc.scalar.activation(hT[:, c, :], bank[:, :], ACT.Identity,
                                             scale=col("me_g", c), bias=col("me_b", c)).then_inc(q_free[J[f"hx{c}"][0]], 1)
                    bank = await_full(act, J, "logits")
                    nc.scalar.activation(lt[0:E, :], bank[0:E, :], ACT.Identity, bias=rb[:, 0:1])\
                        .then_inc(q_free[J["logits"][0]], 1)

                @block.gpsimd
                def _(pool):
                    pool_rstd(pool, chained(pool, M["pchain"]), 0, GB, LN_EPS)
                    for j in range(GB):
                        pool.wait_ge(M["xn_ok"], j + 1)
                        nc.gpsimd.tensor_copy(at(xnall, g * GB + j), xn[:, j, :])

                @block.vector
                def _(dve):
                    J = J_route
                    dve_stats(dve, chained(dve, M["chain"]), xres, g, 0)
                    dve.wait_ge(M["rstd_ok"], 1)
                    dve_centre(dve, xres, xn, g, 0, M["xn_ok"])
                    bank = await_full(dve, J, "turned")
                    nc.vector.tensor_copy(logit[:, bass.ds(g * GB, GB), :],
                                          bank[:, 0:GB * E].rearrange("p (j e) -> p j e", e=E))\
                        .then_inc(q_free[J["turned"][0]], 1)
            end_turn()

        above = view(17408, [B, E, E])
        tied = view(17408 + B * E * E, [B, E, E])
        at_be = [view(19456 + k * B * E, [B, E]) for k in range(6)]
        rank, chosen, first, second, row_of, part_be = at_be
        per_expert = view(19456 + 6 * B * E, [6, E])
        n_chosen, n_rows, n_blocks, start, end = [per_expert[:, k, :] for k in range(5)]
        over = view(20480, [E, NSTEP])
        earlier = view(20608, [E, E])
        ended = view(20736, [NBLK, E])
        block_at = view(20992, [NBLK])
        later = view(21056, [P])
        top = small[:, 0:B]
        total = small[:, B:2 * B]
        inverse = small[:, 2 * B:3 * B]
        gateT = view(11264, [B * P])
        J_gate = Jobs([f"t{k}" for k in range(G)] + [f"b{k}" for k in range(B // 2)])
        with nc.Block(no_gpsimd_drain=True) as block:
            @block.vector
            def _(dve):
                J = J_gate
                link = chained(dve, M["chain"])
                others = logit[:, :, :].unsqueeze(2).to_broadcast([P, B, E, E])
                own = logit[:, :, :].unsqueeze(3).to_broadcast([P, B, E, E])
                nc.vector.tensor_tensor(above, others, own, ALU.is_gt)
                nc.vector.tensor_reduce(top, logit[:, :, :], AX, ALU.max)
                link(nc.vector.tensor_tensor(tied, others, own, ALU.is_equal))
                nc.vector.tensor_tensor(gl1[:, :, :], logit[:, :, :], top.unsqueeze(2).to_broadcast([P, B, E]),
                                        ALU.subtract).then_inc(M["shifted"], 1)
                nc.vector.tensor_tensor(later, ones[:, :], before, ALU.subtract)
                link(nc.vector.tensor_tensor(tied, tied, ebefore.unsqueeze(1).to_broadcast([P, B, E, E]), ALU.mult))
                nc.vector.tensor_tensor(later, later, ident[:, :], ALU.subtract)
                link(nc.vector.tensor_tensor(above, above, tied, ALU.add))
                link(nc.vector.tensor_reduce(rank, above, AX, ALU.add))
                nc.vector.tensor_scalar(chosen, rank, 1.5, None, ALU.is_lt)
                nc.vector.tensor_scalar(first, rank, 0.0, None, ALU.is_equal)
                link(nc.vector.tensor_scalar(second, rank, 1.0, None, ALU.is_equal))
                nc.vector.tensor_reduce(n_chosen, chosen.rearrange("p b e -> p e b"), AX, ALU.add)\
                    .then_inc(M["routed"], 1)
                dve.wait_ge(M["counted"], 1)
                link(nc.vector.tensor_copy(n_rows, T[1][:, 0:E]))
                link(nc.vector.tensor_tensor(over, n_rows.unsqueeze(2).to_broadcast([P, E, NSTEP]),
                                             steps.unsqueeze(1).to_broadcast([P, E, NSTEP]), ALU.is_gt))
                link(nc.vector.tensor_reduce(n_blocks, over, AX, ALU.add))
                link(nc.vector.tensor_tensor(earlier, n_blocks.unsqueeze(1).to_broadcast([P, E, E]), ebefore, ALU.mult))
                link(nc.vector.tensor_reduce(start, earlier, AX, ALU.add))
                link(nc.vector.tensor_tensor(end, start, n_blocks, ALU.add))
                link(nc.vector.tensor_tensor(ended, end.unsqueeze(1).to_broadcast([P, NBLK, E]),
                                             block_ids.unsqueeze(2).to_broadcast([P, NBLK, E]), ALU.is_le))
                link(nc.vector.tensor_reduce(block_at, ended, AX, ALU.add))
                nc.vector.tensor_scalar(block_expert[:, :], block_at, E - 1.0, None, ALU.min).then_inc(M["routed"], 1)
                link(nc.vector.tensor_scalar(start, start, float(BR), None, ALU.mult))
                link(nc.vector.tensor_tensor(row_of, T[0][:, 0:B * E].rearrange("p (b e) -> p b e", e=E),
                                             start.unsqueeze(1).to_broadcast([P, B, E]), ALU.add))
                for k, mask in enumerate((first, second)):
                    link(nc.vector.tensor_tensor(part_be, row_of, mask, ALU.mult))
                    link(nc.vector.tensor_reduce(total, part_be, AX, ALU.add))
                    nc.vector.tensor_copy(pick_row[:, k, :], total).then_inc(M["routed"], 1)
                dve.wait_ge(M["exp_ok"], 1)
                link(nc.vector.tensor_tensor(gl1[:, :, :], gl1[:, :, :], chosen, ALU.mult))
                link(nc.vector.tensor_reduce(total, gl1[:, :, :], AX, ALU.add))
                link(nc.vector.reciprocal(inverse, total))
                nc.vector.tensor_tensor(gates[:, :, :], gl1[:, :, :], inverse.unsqueeze(2).to_broadcast([P, B, E]),
                                        ALU.mult).then_inc(M["gates_ok"], 1)
                dve.wait_ge(M["gates_ok"], 1)
                for k, mask in enumerate((first, second)):
                    link(nc.vector.tensor_tensor(part_be, gates[:, :, :], mask, ALU.mult))
                    link(nc.vector.tensor_reduce(pick_gate[:, k, :], part_be, AX, ALU.add))
                for k in range(B // 2):
                    bank = await_full(dve, J, f"b{k}")
                    x2 = xres[:, 2 * k:2 * k + 2, :]
                    nc.vector.tensor_tensor(x2, bank[:, :].rearrange("p (j d) -> p j d", j=2), x2, ALU.add)\
                        .then_inc(q_free[J[f"b{k}"][0]], 1)

            @block.gpsimd
            def _(pool):
                for k in range(2):
                    pool.wait_ge(M["routed"], 3 + k)
                    for b in range(B):
                        nc.gpsimd.indirect_dma_start(xs_dram, bass.IndirectOffsetOnAxis(pick_row[:, k, b:b + 1], 0),
                                                     xnall[:, b, :], None).then_inc(M["scattered"], 16)
                pool.wait_ge(M["scattered"], 16 * 2 * B)

            @block.sync
            def _(sp):
                sp.wait_ge(M["routed"], 2)
                for k in range(2):
                    load_up(sp, k, k, M[f"up_in{k}"])
                load_down(sp, 0, 0, M["down_in0"])
                sp.wait_ge(M["scattered"], 16 * 2 * B)
                for k in range(2):
                    load_rows(sp, k, k)
                for n in ("up_in0", "up_in1"):
                    sp.wait_ge(M[n], 16)
                sp.wait_ge(M["down_in0"], 16)

            @block.scalar
            def _(act):
                J = J_gate
                act.wait_ge(M["shifted"], 1)
                nc.scalar.activation(gl1[:, :, :], gl1[:, :, :], ACT.Exp).then_inc(M["exp_ok"], 1)
                for k in range(G):
                    bank = await_full(act, J, f"t{k}")
                    nc.scalar.activation(gateT[0:E, k * NT:(k + 1) * NT], bank[0:E, :], ACT.Copy)\
                        .then_inc(q_free[J[f"t{k}"][0]], 1)
                for k in range(2):
                    act_block_rows(act, k)

            @block.tensor
            def _(pe):
                J = J_gate
                pe.wait_ge(M["routed"], 1)
                nc.tensor.matmul(T[0][:, 0:B * E], later, chosen.rearrange("p b e -> p (b e)"), start=True, stop=False)
                for b in range(B - 1):
                    nc.tensor.matmul(T[0][:, (b + 1) * E:B * E].rearrange("p (b e) -> p b e", e=E), ones[:, :],
                                     chosen[:, b:b + 1, :].to_broadcast([P, B - 1 - b, E]), start=False,
                                     stop=(b == B - 2))
                nc.tensor.matmul(T[1][:, 0:E], ones[:, :], n_chosen, start=True, stop=True).then_inc(M["counted"], 1)
                pe.wait_ge(M["gates_ok"], 1)
                for k in range(G):
                    bank = claim(pe, J, f"t{k}")
                    for j in range(GB):
                        ins = nc.tensor.transpose(bank[0:E, j * P:(j + 1) * P], gates[:, k * GB + j, :], ident[:])
                    ins.then_inc(q_full[J[f"t{k}"][0]], 1)
                for k in range(G):
                    await_read(pe, J, f"t{k}")
                for k in range(B // 2):
                    bank = claim(pe, J, f"b{k}")
                    for j in range(2):
                        b = 2 * k + j
                        ins = nc.tensor.matmul(bank[:, j * D:(j + 1) * D], gateT[0:E, b * P:(b + 1) * P], fc2b[:, :],
                                               start=True, stop=True)
                    ins.then_inc(q_full[J[f"b{k}"][0]], 1)
                for k in range(2):
                    pe_block_rows(pe, k)
        end_turn()

        def experts(p, last):
            with nc.Block(no_gpsimd_drain=True) as block:
                @block.sync
                def _(sp):
                    load_down(sp, p * 2 + 1, 1, M["down_in1"])
                    if not last:
                        for k in range(2):
                            load_rows(sp, p * 2 + 2 + k, k)
                        for k in range(2):
                            sp.wait_ge(M["fc1_full"], FC * (k + 1))
                            load_up(sp, p * 2 + 2 + k, k, M[f"up_in{k}"])
                        sp.wait_ge(M["fc2_full"], 2)
                        load_down(sp, p * 2 + 2, 0, M["down_in0"])
                    for k in range(2):
                        sp.wait_ge(M["y_ok"], 2 * (k + 1))
                        sp.dma_start(ys_dram[bass.ds((p * 2 + k) * BR, BR), :].rearrange("(t p) d -> p t d", p=P),
                                     yb[:, k, :, :]).then_inc(M["y_out"], 16)
                    if not last:
                        for n in ("up_in0", "up_in1"):
                            sp.wait_ge(M[n], 16)
                        sp.wait_ge(M["down_in0"], 16)
                    sp.wait_ge(M["y_out"], 32)

                @block.tensor
                def _(pe):
                    for k in range(2):
                        for f in range(FC):
                            n = FC * k + f
                            if n >= 4:
                                pe.wait_ge(M["fc1_free"], n - 3)
                            for c in range(C):
                                ins = nc.tensor.matmul(S[n % 4][:, 0:BR], up_w8[k][:, c, f * P:(f + 1) * P],
                                                       xbT[:, k, c, :], start=(c == 0), stop=(c == C - 1))
                            ins.then_inc(M["fc1_full"], 1)
                    for k in range(2):
                        pe.wait_ge(M["fc1_free"], FC * (k + 1))
                        if k == 1:
                            pe.wait_ge(M["down_in1"], 16)
                        for m, tiles in enumerate((range(2), range(2, BT))):
                            for t in tiles:
                                for f in range(FC):
                                    ins = nc.tensor.matmul(banks[4 + 2 * k + m][:, (t - 2 * m) * D:(t - 2 * m + 1) * D],
                                                           h1[:, k, f, t * P:(t + 1) * P], down_w8[k][:, f, :],
                                                           start=(f == 0), stop=(f == FC - 1))
                            ins.then_inc(M["fc2_full"], 1)
                    if not last:
                        for k in range(2):
                            pe_block_rows(pe, k)

                @block.scalar
                def _(act):
                    for k in range(2):
                        e = expert_of(act, p * 2 + k)
                        for f in range(FC):
                            n = FC * k + f
                            act.wait_ge(M["fc1_full"], n + 1)
                            nc.scalar.activation(h1[:, k, f, :], S[n % 4][:, 0:BR], ACT.Gelu,
                                                 bias=fc1b[:, bass.ds(e * FC + f, 1)]).then_inc(M["fc1_free"], 1)
                    if not last:
                        for k in range(2):
                            act_block_rows(act, k)

                @block.vector
                def _(dve):
                    for k in range(2):
                        for m, tiles in enumerate((slice(0, 2), slice(2, BT))):
                            n = tiles.stop - tiles.start
                            dve.wait_ge(M["fc2_full"], 2 * k + m + 1)
                            nc.vector.tensor_copy(yb[:, k, tiles, :], banks[4 + 2 * k + m][:, 0:n * D]
                                                  .rearrange("p (t d) -> p t d", d=D)).then_inc(M["y_ok"], 1)
            end_turn()

        with nc.Fori(0, NBLK // 2 - 1) as p:
            experts(p, False)
        experts(NBLK // 2 - 1, True)

        with nc.Block(no_gpsimd_drain=True) as block:
            @block.gpsimd
            def _(pool):
                for b in range(B):
                    for k in range(2):
                        nc.gpsimd.indirect_dma_start(picked[:, 2 * b + k, :], None, ys_dram,
                                                     bass.IndirectOffsetOnAxis(pick_row[:, k, b:b + 1], 0))\
                            .then_inc(ld_picked[b // GB], 16)

            @block.vector
            def _(dve):
                link = chained(dve, M["chain"])
                for g in range(G):
                    dve.wait_ge(ld_picked[g], 16 * 2 * GB)
                    for k in range(2):
                        for b in range(g * GB, (g + 1) * GB):
                            ins = nc.vector.scalar_tensor_tensor(
                                out=xres[:, b, :], in0=picked[:, 2 * b + k, :], scalar=pick_gate[:, k, b:b + 1],
                                in1=xres[:, b, :], op0=ALU.mult, op1=ALU.add)
                        link(ins)
        end_turn()

        score, scoreb = small[:, 0:GB], small[:, 4:4 + GB]
        n_above, n_tied = small[:, 8:8 + GB], small[:, 12:12 + GB]
        place, keep = small[:, 16:16 + GB], small[:, 20:20 + GB]
        J_best = Jobs(["hc0", "hc1", "row", "k0", "k1", "v0", "v1", "xs", "gt", "q0", "q1", "pv", "y"]
                      + [f"s{j}" for j in range(GB)])
        with nc.Block(no_gpsimd_drain=True) as block:
            @block.gpsimd
            def _(pool):
                nc.gpsimd.memset(VA[:, :, :, :], 0.0)
        end_turn()
        with nc.Fori(0, G) as g:
            with nc.Block(no_gpsimd_drain=True) as block:
                @block.tensor
                def _(pe):
                    J = J_best
                    pe.wait_ge(ld["l1"], 16)
                    pe_turn_rows(pe, J, ["hc0", "hc1"], cn, M["cn_ok"])
                    bank = claim(pe, J, "row")
                    pe.wait_ge(M["colb_ok"], GB)
                    for j in range(GB):
                        ins = nc.tensor.transpose(bank[:, j * P:(j + 1) * P], colb[:, j, :], ident[:])
                    ins.then_inc(q_full[J["row"][0]], 1)
                    await_read(pe, J, "hc0")
                    await_read(pe, J, "hc1")
                    for m in range(C):
                        pe_project(pe, J, f"k{m}", w_l1, D + m * P, cT)
                    pe_values(pe, J, ["v0", "v1"], w_l1, 2 * D, cT)
                    bank = claim(pe, J, "xs")
                    pe.wait_ge(M["gat_ok"], GB)
                    pe.wait_ge(M["xs_ok"], GB)
                    for c in range(C):
                        for j in range(GB):
                            ins = nc.tensor.matmul(bank[:, c * P + j * R:c * P + (j + 1) * R], xs[:, j, c * P:(c + 1) * P],
                                                   gat[:, j, :], start=True, stop=True)
                    ins.then_inc(q_full[J["xs"][0]], 1)
                    bank = claim(pe, J, "gt")
                    nc.tensor.transpose(bank[:, 0:P], gat[:, :, :].rearrange("p j r -> p (j r)"), ident[:])\
                        .then_inc(q_full[J["gt"][0]], 1)
                    await_read(pe, J, "xs")
                    for m in range(C):
                        pe_project(pe, J, f"q{m}", w_l1, m * P, xsT, P)
                    for n in ("k0", "k1", "q0", "q1"):
                        await_read(pe, J, n)
                    for i in range(4):
                        r = slice(64 * (i % 2), 64 * (i % 2) + 64)
                        for j in range(GB):
                            ins = nc.tensor.matmul(S[i][j * R:(j + 1) * R, :], q1T[r, i // 2, j * R:(j + 1) * R],
                                                   kM[r, :, i // 2, j * P:(j + 1) * P], start=True, stop=True)
                        ins.then_inc(M["scored"], 1)
                    for n in range(4):
                        pe_turn(pe, n)
                    pe.wait_ge(M["pt_ok"], 4)
                    await_read(pe, J, "v0")
                    await_read(pe, J, "v1")
                    bank = claim(pe, J, "pv")
                    for j in range(GB):
                        r = slice(j * R, (j + 1) * R)
                        ins = pe_products(pe, bank, j, r, r, 0)
                    ins.then_inc(q_full[J["pv"][0]], 1)
                    await_read(pe, J, "pv")
                    bank = claim(pe, J, "y")
                    for c in range(C):
                        ins = nc.tensor.matmul(bank[:, 0:D], oT[:, c, 0:P], w_l1[:, c, 3 * D:4 * D],
                                               start=(c == 0), stop=(c == C - 1))
                    ins.then_inc(q_full[J["y"][0]], 1)
                    await_read(pe, J, "y")
                    await_read(pe, J, "gt")
                    for j in range(GB):
                        bank = claim(pe, J, f"s{j}")
                        r = slice(j * R, (j + 1) * R)
                        nc.tensor.matmul(bank[:, 0:D], gatT[r, :], yo[r, :], start=True, stop=True)\
                            .then_inc(q_full[J[f"s{j}"][0]], 1)

                @block.scalar
                def _(act):
                    J = J_best
                    act_affine(act, J, ["hc0", "hc1"], cT, None, None)
                    act_values(act, J, ["v0", "v1"])
                    bank = await_full(act, J, "xs")
                    nc.scalar.activation(xsT[:, :, :], bank[:, 0:C * P].rearrange("p (c n) -> p c n", c=C), ACT.Copy)\
                        .then_inc(q_free[J["xs"][0]], 1)
                    bank = await_full(act, J, "gt")
                    nc.scalar.activation(gatT, bank[:, 0:P], ACT.Copy).then_inc(q_free[J["gt"][0]], 1)
                    for m in range(C):
                        bank = await_full(act, J, f"q{m}")
                        nc.scalar.activation(q1T[:, m, :], bank[:, 0:P], ACT.Identity, bias=col("l1_bq", m))\
                            .then_inc(q_free[J[f"q{m}"][0]], 1)
                    for n in range(4):
                        act_exp(act, n, bank_of(n)[1])
                    act_products(act, J, "pv", "l1_bv", slice(0, P))

                @block.gpsimd
                def _(pool):
                    for j in range(GB):
                        nc.gpsimd.tensor_copy(xs[:, j, :], at(xres, g * GB + j)).then_inc(M["xs_ok"], 1)
                    pool_copy(pool, g)
                    for n in range(4):
                        pool_scale(pool, n)

                @block.vector
                def _(dve):
                    J = J_best
                    link = chained(dve, M["chain"])
                    for j in range(GB):
                        dve.wait_ge(M["xs_ok"], j + 1)
                        link(nc.vector.scalar_tensor_tensor(out=junk, in0=xs[:, j, :], scalar=1.0, in1=row("l1_sw"),
                                                            op0=ALU.mult, op1=ALU.mult, accum_out=score[:, j:j + 1]))
                    link(nc.vector.tensor_scalar(scoreb, score, sbias[:, 0:1], None, ALU.add))
                    for j in range(GB):
                        nc.vector.tensor_scalar(colb[:, j, :], ones[:, :], scoreb[:, j:j + 1], None, ALU.mult)\
                            .then_inc(M["colb_ok"], 1)
                    bank = await_full(dve, J, "row")
                    for j in range(GB):
                        each = bank[:, j * P:(j + 1) * P]
                        link(nc.vector.tensor_scalar(junk[:, 0:P], each, scoreb[:, j:j + 1], None, ALU.is_gt, ALU.add,
                                                     accum_out=n_above[:, j:j + 1]))
                        link(nc.vector.scalar_tensor_tensor(out=junk[:, 0:P], in0=each, scalar=scoreb[:, j:j + 1],
                                                            in1=before, op0=ALU.is_equal, op1=ALU.mult,
                                                            accum_out=n_tied[:, j:j + 1]))
                    nc.vector.tensor_copy(junk[:, 0:1], bank[:, 0:1]).then_inc(q_free[J["row"][0]], 1)
                    link(nc.vector.tensor_tensor(place, n_above, n_tied, ALU.add))
                    for j in range(GB):
                        nc.vector.tensor_scalar(gat[:, j, :], ranks, place[:, j:j + 1], None, ALU.is_equal)\
                            .then_inc(M["gat_ok"], 1)
                    link(nc.vector.tensor_scalar(keep, place, TOPK - 0.5, None, ALU.is_gt))
                    for m in range(C):
                        dve_keys(dve, J, m, "l1_bk")
                    dve_softmax(dve, 4, None)
                    bank = await_full(dve, J, "y")
                    nc.vector.tensor_tensor(yo, bank[:, 0:D], row("l1_ob"), ALU.add).then_inc(q_free[J["y"][0]], 1)
                    for j in range(GB):
                        bank = await_full(dve, J, f"s{j}")
                        nc.vector.scalar_tensor_tensor(out=at(xres, g * GB + j), in0=at(xres, g * GB + j),
                                                       scalar=keep[:, j:j + 1], in1=bank[:, 0:D],
                                                       op0=ALU.mult, op1=ALU.add).then_inc(q_free[J[f"s{j}"][0]], 1)
            end_turn()

        A4 = H // NKV
        turn2 = ["hx0", "hx1", "hc0", "hc1"]
        jobs = ["kA", "kB"] + [f"q{a}{h}" for a in range(A4) for h in "AB"] + ["v0", "v1"]
        jobs += [f"pv{j}_{q}" for j in range(GB) for q in range(2)]
        jobs += ["w0", "w1", "n0", "n1"] + [f"{x}{f}" for f in range(FC) for x in "gu"] + turn2 + ["d0", "d1"]
        J_l2, J_l2_first = Jobs(jobs), Jobs(turn2)
        scratch = [w_ca, w_l1]

        def products4(k, r):
            return scratch[r % 2][:, :, :].rearrange("p c n -> p (c n)")[:, k * NT:(k + 1) * NT]\
                .rearrange("p (j n) -> p j n", j=GB)

        def rms(pool, link, k, n_stats):
            pool.wait_ge(M["stats"], n_stats)
            link(nc.gpsimd.tensor_tensor(ve[:, k, :], mv[:, k, :, 0], mv[:, k, :, 0], ALU.mult))
            link(nc.gpsimd.tensor_tensor(ve[:, k, :], ve[:, k, :], mv[:, k, :, 1], ALU.add))
            link(nc.gpsimd.tensor_scalar(ve[:, k, :], ve[:, k, :], RMS_EPS, 1.0, ALU.add, ALU.mult))
            nc.gpsimd.tensor_tensor(rstd[:, k, :], ve[:, k, :], nhalf[:], ALU.pow).then_inc(M["rstd_ok"], 1)

        def scale_rows(dve, src, dst, g, k, ok):
            for j in range(GB):
                nc.vector.tensor_scalar(dst[:, j, :], at(src, g * GB + j), rstd[:, k, j:j + 1], None,
                                        ALU.mult).then_inc(ok, 1)

        def dve_rms_group(dve, link, g, n_before):
            dve_stats(dve, link, xres, g, 0)
            dve_stats(dve, link, ctxr, g, 1)
            dve.wait_ge(M["rstd_ok"], n_before + 1)
            scale_rows(dve, xres, xn, g, 0, M["xn_ok"])
            dve.wait_ge(M["rstd_ok"], n_before + 2)
            scale_rows(dve, ctxr, cn, g, 1, M["cn_ok"])

        def act_rms_group(act, J):
            act_affine(act, J, ["hx0", "hx1"], hT, "ln1", None)
            act_affine(act, J, ["hc0", "hc1"], cT, "ln1", None)

        with nc.Block(no_gpsimd_drain=True) as block:
            @block.tensor
            def _(pe):
                pe_turn_rows(pe, J_l2_first, ["hx0", "hx1"], xn, M["xn_ok"])
                pe_turn_rows(pe, J_l2_first, ["hc0", "hc1"], cn, M["cn_ok"])

            @block.scalar
            def _(act):
                act_rms_group(act, J_l2_first)

            @block.gpsimd
            def _(pool):
                link = chained(pool, M["pchain"])
                rms(pool, link, 0, GB)
                rms(pool, link, 1, 2 * GB)

            @block.vector
            def _(dve):
                dve_rms_group(dve, chained(dve, M["chain"]), 0, 0)
        end_turn()

        with nc.Fori(0, G) as g:
            g_next = (g + 1) & (G - 1)
            with nc.Block(no_gpsimd_drain=True) as block:
                @block.tensor
                def _(pe):
                    J = J_l2
                    pe.wait_ge(ld["l2"], 16 * 6)
                    for h in range(2):
                        pe_project(pe, J, "k" + "AB"[h], wkv2, h * P, cT)
                    for a in range(A4):
                        for h in range(2):
                            pe_project(pe, J, f"q{a}" + "AB"[h], wq2, (2 * a + h) * P, hT)
                    def scores(j, a):
                        for h in range(2):
                            ins = nc.tensor.matmul(S[a][:, :], qr[:, a, h, j * P:(j + 1) * P],
                                                   kM2[:, :, h, j * P:(j + 1) * P], start=(h == 0), stop=(h == 1))
                        ins.then_inc(M["scored"], 1)

                    def products(j):
                        pe.wait_ge(M["pt_ok"], 4 * j + 4)
                        for q in range(2):
                            bank = claim(pe, J, f"pv{j}_{q}")
                            for half in range(2):
                                i = 2 * q + half
                                ins = nc.tensor.matmul(bank[half * HD:(half + 1) * HD, :], V2[:, j, i, :],
                                                       PT[:, j % 2, i::NKV, :],
                                                       start=True, stop=True)
                            ins.then_inc(q_full[J[f"pv{j}_{q}"][0]], 1)

                    pe_values(pe, J, ["v0", "v1"], wkv2, D, cT)
                    pe.wait_ge(M["keys_ok"], 2)
                    for a in range(A4):
                        pe.wait_ge(M["roped"], 2 * (a + 2))
                        scores(0, a)
                    for n in range(4 * GB):
                        if n + 4 < 4 * GB:
                            pe.wait_ge(M["masked"], n + 1)
                            scores(n // 4 + 1, n % 4)
                        pe_turn(pe, n)
                        if n == 3:
                            await_read(pe, J, "v0")
                            await_read(pe, J, "v1")
                        if n % 4 == 3 and n > 4:
                            products(n // 4 - 1)
                    products(GB - 1)
                    for j in range(GB):
                        await_read(pe, J, f"pv{j}_0")
                        await_read(pe, J, f"pv{j}_1")

                    def rows_out(names, w, src):
                        for y, name in enumerate(names):
                            bank = claim(pe, J, name)
                            for jj in range(2):
                                j = 2 * y + jj
                                for f in range(FC):
                                    ins = nc.tensor.matmul(bank[:, jj * D:(jj + 1) * D], src[:, f, j * P:(j + 1) * P],
                                                           w[:, f, :], start=(f == 0), stop=(f == FC - 1))
                            ins.then_inc(q_full[J[name][0]], 1)

                    rows_out(["w0", "w1"], wo2, o2T)
                    for c in range(C):
                        bank = claim(pe, J, f"n{c}")
                        for j in range(GB):
                            if c == 0:
                                pe.wait_ge(M["xn_ok"], j + 1)
                            ins = nc.tensor.transpose(bank[:, j * P:(j + 1) * P], xn[:, j, c * P:(c + 1) * P], ident[:])
                        ins.then_inc(q_full[J[f"n{c}"][0]], 1)
                    await_read(pe, J, "n0")
                    await_read(pe, J, "n1")
                    for f in range(FC):
                        pe_project(pe, J, f"g{f}", wg2, f * P, hT)
                        pe_project(pe, J, f"u{f}", wu2, f * P, hT)
                    for src, ok, names, seen in ((xn, M["xn_ok"], ["hx0", "hx1"], GB), (cn, M["cn_ok"], ["hc0", "hc1"], 0)):
                        for c in range(C):
                            bank = claim(pe, J, names[c])
                            pe.wait_ge(ok, seen + GB)
                            for j in range(GB):
                                ins = nc.tensor.transpose(bank[:, j * P:(j + 1) * P], src[:, j, c * P:(c + 1) * P], ident[:])
                            ins.then_inc(q_full[J[names[c]][0]], 1)
                    for f in range(FC):
                        await_read(pe, J, f"u{f}")
                    rows_out(["d0", "d1"], wd2, act2)

                @block.scalar
                def _(act):
                    J = J_l2
                    def values():
                        for v in range(2):
                            bank = await_full(act, J, f"v{v}")
                            nc.scalar.activation(V2[:, 2 * v:2 * v + 2, :, :],
                                                 bank[:, :].rearrange("p (j h d) -> p j h d", j=2, d=HD), ACT.Copy)\
                                .then_inc(q_free[J[f"v{v}"][0]], 1)

                    def out_copies(j):
                        for q in range(2):
                            name = f"pv{j}_{q}"
                            bank = await_full(act, J, name)
                            nc.scalar.activation(o2T[:, 4 * q:4 * q + 4, j * P:(j + 1) * P],
                                                 bank[:, :].rearrange("p (f n) -> p f n", f=4), ACT.Copy)\
                                .then_inc(q_free[J[name][0]], 1)

                    for h in range(2):
                        act.wait_ge(M["roped"], h + 1)
                        for i in range(NKV):
                            ins = nc.scalar.activation(kM2[:, i, h, :], kr[:, h, :], ACT.Copy, scale=of_key_head[:, i:i + 1])
                        ins.then_inc(M["keys_ok"], 1)
                    values()
                    N, LAG = 4 * GB, 4
                    for n in range(N + LAG):
                        if n < N:
                            act_exp(act, n, bank_of(n)[0])
                        if n >= LAG:
                            m = n - LAG
                            act.wait_ge(M["turned"], m + 1)
                            if m >= 8:
                                await_full(act, J, f"pv{m // 4 - 2}_1")
                            nc.scalar.activation(turned_tile(m), T[m % 2][:, :].rearrange("p (s q) -> p s q", q=P),
                                                 ACT.Copy).then_inc(M["pt_ok"], 1)
                        if n >= 8 + LAG - 1 and n % 4 == LAG - 1 and n // 4 - 2 < GB - 1:
                            out_copies(n // 4 - 2)
                    out_copies(GB - 1)
                    for c in range(C):
                        bank = await_full(act, J, f"n{c}")
                        nc.scalar.activation(hT[:, c, :], bank[:, :], ACT.Identity, scale=col("ln2", c))\
                            .then_inc(q_free[J[f"n{c}"][0]], 1)
                    for f in range(FC):
                        bank = await_full(act, J, f"g{f}")
                        nc.scalar.activation(act2[:, f, :], bank[:, :], ACT.Silu).then_inc(q_free[J[f"g{f}"][0]], 1)
                    act_rms_group(act, J)

                @block.gpsimd
                def _(pool):
                    link = chained(pool, M["pchain"])
                    for r in range(1 + A4):
                        pool.wait_ge(M["multiplied"], 4 * (r + 1))
                        first, second = (kr[:, 0, :], kr[:, 1, :]) if r == 0 else (qr[:, r - 1, 0, :], qr[:, r - 1, 1, :])
                        for dst, k1, k2, op in ((first, 0, 1, ALU.subtract), (second, 2, 3, ALU.add)):
                            nc.gpsimd.tensor_tensor(dst.rearrange("p (j n) -> p j n", j=GB), products4(k1, r),
                                                    products4(k2, r), op).then_inc(M["roped"], 1)
                    for n in range(4 * GB):
                        pool_scale(pool, n)
                    rms(pool, link, 0, GB)
                    rms(pool, link, 0, 2 * GB)
                    rms(pool, link, 1, 3 * GB)

                @block.vector
                def _(dve):
                    J = J_l2
                    link = chained(dve, M["chain"])

                    cos = rope[:, 0, :].unsqueeze(1).to_broadcast([P, GB, P])
                    sin = rope[:, 1, :].unsqueeze(1).to_broadcast([P, GB, P])
                    for r in range(1 + A4):
                        n = "k" if r == 0 else f"q{r - 1}"
                        if r >= 2:
                            dve.wait_ge(M["roped"], 2 * (r - 1))
                        for half, table in ((0, ((0, cos), (3, sin))), (1, ((1, sin), (2, cos)))):
                            bank = await_full(dve, J, n + "AB"[half])
                            for k, t in table:
                                nc.vector.tensor_tensor(products4(k, r), bank[:, :].rearrange("p (j n) -> p j n", j=GB),
                                                        t, ALU.mult).then_inc(M["multiplied"], 1)
                            dve.wait_ge(M["multiplied"], 4 * r + 2 * half + 2)
                            dve.sem_inc(q_free[J[n + "AB"[half]][0]], 1)

                    dve.wait_ge(ld["mask"], 16)
                    N = 4 * GB
                    for n in range(N + 3):
                        if n < N:
                            j = n // 4
                            dve.wait_ge(M["scored"], n + 1)
                            if n >= 8:
                                dve.wait_ge(M["turned"], n - 7)
                            nc.vector.scalar_tensor_tensor(
                                out=bank_of(n)[0], in0=bank_of(n)[1], scalar=HD ** -0.5,
                                in1=mask2[:, bass.ds(g * GB + j, 1), :].to_broadcast([P, A4, P]),
                                op0=ALU.mult, op1=ALU.add).then_inc(M["masked"], 1)
                        if 1 <= n <= N:
                            dve.wait_ge(M["masked"], n)
                            nc.vector.tensor_reduce(cols_of(mx, n - 1), bank_of(n - 1)[0], AX, ALU.max, negate=True)\
                                .then_inc(M["maxed"], 1)
                        if n >= 3:
                            dve.wait_ge(M["probs"], n - 2)
                            nc.vector.reciprocal(cols_of(rden, n - 3), cols_of(psum, n - 3)).then_inc(M["divided"], 1)

                    def add_rows(names):
                        for y, name in enumerate(names):
                            bank = await_full(dve, J, name)
                            x2 = at(xres, g * GB + 2 * y, 2)
                            link(nc.vector.tensor_tensor(x2, bank[:, :].rearrange("p (j d) -> p j d", j=2), x2, ALU.add))
                            dve.sem_inc(q_free[J[name][0]], 1)

                    add_rows(["w0", "w1"])
                    dve_stats(dve, link, xres, g, 0)
                    dve.wait_ge(M["rstd_ok"], 1)
                    scale_rows(dve, xres, xn, g, 0, M["xn_ok"])
                    for f in range(FC):
                        await_read(dve, J, f"g{f}")
                        bank = await_full(dve, J, f"u{f}")
                        nc.vector.tensor_tensor(act2[:, f, :], bank[:, :], act2[:, f, :], ALU.mult)\
                            .then_inc(q_free[J[f"u{f}"][0]], 1)
                        if f == 1:
                            dve_stats(dve, link, xres, g_next, 0)
                        if f == 2:
                            dve_stats(dve, link, ctxr, g_next, 1)
                        if f == 4:
                            dve.wait_ge(M["rstd_ok"], 2)
                            scale_rows(dve, xres, xn, g_next, 0, M["xn_ok"])
                        if f == 5:
                            dve.wait_ge(M["rstd_ok"], 3)
                            scale_rows(dve, ctxr, cn, g_next, 1, M["cn_ok"])
                    add_rows(["d0", "d1"])
            end_turn()

        part = small[:, 32:36]
        gamma, half_step, minus = small[:, 36:40], small[:, 40:44], small[:, 44:48]
        up_w, down_w = view(2048, [C, D]), view(2560, [C, D])
        with nc.Block(no_gpsimd_drain=True) as block:
            @block.tensor
            def _(pe):
                pe.wait_ge(M["maxed"], 4)
                nc.tensor.matmul(Q[0][:, 0:4], ones[:, :], part, start=True, stop=True).then_inc(M["scored"], 1)

            @block.vector
            def _(dve):
                link = chained(dve, M["chain"])
                dve.wait_ge(ld["l3"], 16)
                W4 = [w_l3[:, :, k * D:(k + 1) * D] for k in range(4)]
                for k in range(4):
                    nc.vector.tensor_reduce(part[:, k:k + 1], W4[k], mybir.AxisListType.XY, ALU.add,
                                            apply_absolute_value=True).then_inc(M["maxed"], 1)
                dve.wait_ge(M["scored"], 1)
                link(nc.vector.tensor_scalar(gamma, Q[0][:, 0:4], 1.0 / (D * D), None, ALU.mult))
                link(nc.vector.tensor_scalar(half_step, gamma, LN_EPS, 0.5, ALU.add, ALU.mult))
                link(nc.vector.tensor_scalar(minus, half_step, -1.0, None, ALU.mult))
                for k in range(4):
                    link(nc.vector.tensor_scalar(up_w, W4[k], half_step[:, k:k + 1], gamma[:, k:k + 1], ALU.is_gt, ALU.mult))
                    link(nc.vector.tensor_scalar(down_w, W4[k], minus[:, k:k + 1], gamma[:, k:k + 1], ALU.is_lt, ALU.mult))
                    link(nc.vector.tensor_tensor(up_w, up_w, down_w, ALU.subtract))
                    link(nc.vector.tensor_tensor(up_w, up_w, W4[k], ALU.subtract))
                    link(nc.vector.tensor_tensor(W4[k], W4[k], up_w, ALU.add))
        end_turn()
        attention(("l3_g", "l3_b"), "raw", w_l3, "l3_bq", "l3_bk", "l3_bv", "l3_ob", ["l3"], store=True)


def shape_tables():
    d = np.arange(P) % HALF
    inv = (1.0 / np.float32(10000.0) ** (np.arange(0, HD, 2, dtype=np.float32) / np.float32(HD))).astype(np.float32)
    angle = np.arange(P, dtype=np.float32)[None, :] * inv[d][:, None]
    rope = np.stack([np.cos(angle), np.sin(angle)], axis=1).astype(np.float32)
    p = np.arange(P)
    of_four = ((p // DH) % 4)[:, None] == np.arange(4)[None]
    of_key_head = (p // HALF)[:, None] == np.arange(NKV)[None]
    before = p[None, :] < p[:, None]
    ranks = np.broadcast_to(np.where(np.arange(R) < TOPK, np.arange(R), -1)[None], (P, R))
    e = np.arange(E)
    ebefore = np.broadcast_to((e[None, :] < e[:, None]).reshape(1, E * E), (P, E * E))
    steps = np.broadcast_to(np.arange(NSTEP)[None] * BR, (P, NSTEP))
    block_ids = np.broadcast_to(np.arange(NBLK)[None], (P, NBLK))
    table = np.concatenate([of_four * DH ** -0.5, of_key_head, before, ranks, ebefore, steps, block_ids], axis=1).astype(np.float32)
    return rope, table


def lay_out(i):
    def chunks(v):
        return v.reshape(C, P).T

    def thirds(name, v):
        return [v[k * D:(k + 1) * D] for k in range(3)]

    L0, L1, L2, L3 = "L0_xattn_", "L1_xattn_", "L2_xattn_", "L3_xattn_"
    sq, sk, sv = thirds("sa", i[L0 + "sa_in_b"])
    cq, ck, cv = thirds("ca", i[L0 + "ca_in_b"])
    oq, ok, ov = thirds("l1", i[L1 + "in_proj_b"])
    vec = {"sa_g": i[L0 + "sa_ln_g"], "sa_b": i[L0 + "sa_ln_b"], "sa_bq": sq, "sa_bk": sk, "sa_bv": sv,
           "cq_g": i[L0 + "ca_q_ln_g"], "cq_b": i[L0 + "ca_q_ln_b"], "ck_g": i[L0 + "ca_kv_ln_g"],
           "ck_b": i[L0 + "ca_kv_ln_b"], "ca_bq": cq, "ca_bk": ck, "ca_bv": cv,
           "me_g": i[L0 + "moe_ln_g"], "me_b": i[L0 + "moe_ln_b"], "l1_bq": oq, "l1_bk": ok, "l1_bv": ov,
           "ln1": i[L2 + "ln1_w"], "ln2": i[L2 + "ln2_w"], "l3_g": i[L3 + "ln_gamma"], "l3_b": i[L3 + "ln_beta"],
           "l3_bq": i[L3 + "bq"], "l3_bk": i[L3 + "bk"], "l3_bv": i[L3 + "bv"]}
    rows = {"sa_ob": i[L0 + "sa_out_b"], "ca_ob": i[L0 + "ca_out_b"], "l1_ob": i[L1 + "out_b"], "l3_ob": i[L3 + "bo"],
            "l1_sw": i[L1 + "score_w"].reshape(D)}
    rope, table = shape_tables()
    cat = np.concatenate
    out = {
        "x": i["x"], "ctx": i["ctx_1024"], "mask": i["mask_Bx1xSxS2_ff0"].reshape(B, P, P),
        "cols": cat([chunks(vec[n]) for n in COLS], axis=1),
        "rows": np.broadcast_to(np.stack([rows[n] for n in ROWS])[None], (P, len(ROWS), D)),
        "fc1b": i[L0 + "e_fc1_b"].reshape(E * FC, P).T, "fc2b": i[L0 + "e_fc2_b"],
        "rw": i[L0 + "router_w"].T, "rb": i[L0 + "router_b"].reshape(E, 1),
        "sbias": np.broadcast_to(i[L1 + "score_b"].reshape(1, 1), (P, 1)),
        "rope": rope, "shape_c": table,
        "w_sa": cat([i[L0 + "sa_in_w"].T, i[L0 + "sa_out_w"].T], axis=1),
        "w_ca": cat([i[L0 + "ca_in_w"].T, i[L0 + "ca_out_w"].T], axis=1),
        "w_l1": cat([i[L1 + "in_proj_w"].T, i[L1 + "out_w"].T], axis=1),
        "w_l3": cat([i[L3 + n].T for n in ("Wq", "Wk", "Wv", "Wo")], axis=1),
        "fc1": i[L0 + "e_fc1_w"].transpose(0, 2, 1).reshape(E * D, FF),
        "fc2": i[L0 + "e_fc2_w"].transpose(0, 2, 1).reshape(E * FF, D),
        "wq2": i[L2 + "Wq"].reshape(D, NKV, H // NKV, 2, HALF).transpose(0, 2, 3, 1, 4).reshape(D, FF),
        "wkv2": cat([i[L2 + "Wk"].reshape(D, NKV, 2, HALF).transpose(0, 2, 1, 3).reshape(D, D), i[L2 + "Wv"]], axis=1),
        "wo2": i[L2 + "Wo"].reshape(2, 2, H // NKV, HD, D).transpose(0, 2, 1, 3, 4).reshape(FF, D),
        "wg2": i[L2 + "Wgate"], "wu2": i[L2 + "Wup"], "wd2": i[L2 + "Wdown"],
    }
    return {n: np.ascontiguousarray(a) for n, a in out.items()}


def kernel(**inputs):
    import concourse.bacc as bacc
    from concourse.bass_utils import run_bass_kernel_spmd

    arrays = lay_out({n: np.asarray(a) for n, a in inputs.items()})
    nc = bacc.Bacc("TRN2", target_bir_lowering=False, num_devices=1)
    aps = {n: nc.dram_tensor("in_" + n, a.shape, mybir.dt.from_np(a.dtype), kind="ExternalInput").ap()
           for n, a in arrays.items()}
    out = nc.dram_tensor("out", (B, P, D), F32, kind="ExternalOutput").ap()
    build(nc, aps, out)
    r = run_bass_kernel_spmd(nc, [{"in_" + n: a for n, a in arrays.items()}], core_ids=[0])
    return r.results[0]["out"]
```

```python
from contextlib import ExitStack

import numpy as np

import concourse.bass as bass
from concourse import mybir

F32 = mybir.dt.float32
ALU = mybir.AluOpType
ACT = mybir.ActivationFunctionType
AX = mybir.AxisListType.X

P = 128
B = 16
D = 256
C = D // P
GB = 4
G = B // GB
NT = GB * P
H = 16
DH = D // H
E = 8
FF = 1024
FC = FF // P
HD = 64
NKV = 4
HALF = HD // 2
BT = 2
BR = BT * P
NSTEP = -(-B * P // BR)
NBLK = (2 * B * P + E * (BR - 1)) // BR
NBLK += NBLK % 2
PAIRS = [range(t, min(t + 2, BT)) for t in range(0, BT, 2)]
TOPK = 10
R = 32
LN_EPS = 1e-5
Q_EPS = 1e-5
RMS_EPS = 1e-6

COLS = ["sa_g", "sa_b", "sa_bq", "sa_bk", "sa_bv", "cq_g", "cq_b", "ck_g", "ck_b", "ca_bq", "ca_bk", "ca_bv",
        "me_g", "me_b", "l1_bq", "l1_bk", "l1_bv", "ln1", "ln2", "l3_g", "l3_b", "l3_bq", "l3_bk", "l3_bv"]
ROWS = ["sa_ob", "ca_ob", "l1_ob", "l3_ob", "l1_sw"]


class Jobs:

    def __init__(self, names):
        self.at = {n: (k % 2, k // 2) for k, n in enumerate(names)}
        assert len(self.at) == len(names)

    def __getitem__(self, name):
        return self.at[name]


def build(nc, A, out):
    with ExitStack() as ctx:
        def sb(name, shape, dt=F32):
            return ctx.enter_context(nc.sbuf_tensor(name, shape, dt))

        def sem(name):
            return ctx.enter_context(nc.semaphore(name))

        xres = sb("xres", [P, B, D])
        ctxr = sb("ctxr", [P, B, D])
        w_sa = sb("w_sa", [P, C, 4 * D])
        w_ca = sb("w_ca", [P, C, 4 * D])
        w_l1 = sb("w_l1", [P, C, 4 * D])
        w_l3 = sb("w_l3", [P, C, 4 * D])
        cols = sb("cols", [P, 2 * len(COLS)])
        rows = sb("rows", [P, len(ROWS), D])
        fc1b = sb("fc1b", [P, E * FC])
        fc2b = sb("fc2b", [E, D])
        rw = sb("rw", [P, C, E])
        rb = sb("rb", [P, E])
        sbias = sb("sbias", [P, 1])
        rope = sb("rope", [P, 2, P])
        shape_c = sb("shape_c", [P, 8 + P + R + E * E + NSTEP + NBLK])
        of_four = shape_c[:, 0:4]
        of_key_head = shape_c[:, 4:8]
        before = shape_c[:, 8:8 + P]
        ranks = shape_c[:, 8 + P:8 + P + R]
        ebefore = shape_c[:, 8 + P + R:8 + P + R + E * E].rearrange("p (e f) -> p e f", e=E)
        steps = shape_c[:, 8 + P + R + E * E:8 + P + R + E * E + NSTEP]
        block_ids = shape_c[:, 8 + P + R + E * E + NSTEP:]
        ident = sb("ident", [P, P])
        ones = sb("ones", [P, P])
        nhalf = sb("nhalf", [P, GB])

        st = sb("st", [P, 2, GB, 6])
        mv = sb("mv", [P, 2, GB, 2])
        ve = sb("ve", [P, 2, GB])
        rstd = sb("rstd", [P, 2, GB])
        mx = sb("mx", [P, 2, H])
        psum = sb("psum", [P, 2, H])
        rden = sb("rden", [P, 2, H])
        small = sb("small", [P, 64])
        gates = sb("gates", [P, B, E])
        logit = sb("logit", [P, B, E])
        gl1 = sb("gl1", [P, B, E])
        pick_gate = sb("pick_gate", [P, 2, B])
        pick_row = sb("pick_row", [P, 2, B], mybir.dt.int32)
        pick_now = sb("pick_now", [P, 2, GB], mybir.dt.int32)
        block_expert = sb("block_expert", [P, NBLK], mybir.dt.int32)

        xs_dram = nc.dram_tensor("sorted_rows", (NBLK * BR, D), F32, kind="Internal").ap()
        ys_dram = nc.dram_tensor("expert_rows", (NBLK * BR, D), F32, kind="Internal").ap()

        W = 33280
        reg = sb("reg", [P, W])

        def view(at, shape):
            n = int(np.prod(shape))
            assert at + n <= W, (at, n)
            v = reg[:, at:at + n]
            if len(shape) == 1:
                return v
            names = "abcd"[:len(shape)]
            return v.rearrange(f"p ({' '.join(names)}) -> p {' '.join(names)}",
                               **{k: s for k, s in zip(names[:-1], shape)})

        xn = view(0, [GB, D])
        cn = view(1024, [GB, D])
        hT = view(2048, [C, NT])
        cT = view(3072, [C, NT])
        SP = view(4096, [2, 4, 4, P])
        PT = view(8192, [2, H, P])
        qT = view(12288, [C, NT])
        kM = view(13312, [4, C, NT])
        VA = view(17408, [GB, H, 2 * DH])
        oT = view(19456, [C, NT])
        xs = view(0, [GB, D])
        colb = view(12288, [GB, P])
        gat = view(12800, [GB, R])
        gatT = view(12928, [P])
        yo = view(13056, [D])
        xsT = view(20480, [C, P])
        q1T = view(20736, [C, P])
        junk = view(20992, [D])
        xnall = view(13312, [B, D])
        up_w8 = [view(5120 + 2048 * k, [C, FF]) for k in range(2)]
        down_w8 = [view(9216 + 2048 * k, [FC, D]) for k in range(2)]
        xb = view(0, [2, BT, D])
        xbT = view(2048, [2, C, BR])
        h1 = view(13312, [2, FC, BR])
        yb = view(19968, [2, BT, D])
        picked = view(6144, [2, GB, D])
        l2w = 22016
        wq2 = view(l2w, [C, FF])
        wkv2 = view(l2w + 2048, [C, 2 * D])
        wo2 = view(l2w + 3072, [FC, D])
        wg2 = view(l2w + 5120, [C, FF])
        wu2 = view(l2w + 7168, [C, FF])
        wd2 = view(l2w + 9216, [FC, D])
        qr = view(12288, [GB, 2, NT])
        kr = view(0, [2, NT])
        kM2 = view(16384, [NKV, 2, NT])
        xn2 = view(16384, [GB, D])
        V2 = view(20480, [GB, NKV, HD])
        o2T = view(0, [FC, NT])
        act2 = view(12288, [FC, NT])
        mask2 = w_sa[:, :, :].rearrange("p c n -> p (c n)").rearrange("p (b k) -> p b k", b=B)
        rt = w_ca[:, :, :].rearrange("p c n -> p (c n)").rearrange("p (a n) -> p a n", a=4)

        banks = [ctx.enter_context(nc.psum_tensor(f"bank{i}", [P, 512], F32)) for i in range(8)]
        S = banks[0:4]
        T = banks[4:6]
        Q = banks[6:8]

        ld = {n: sem("ld_" + n) for n in ("x", "ctx", "small", "sa", "ca", "l1", "l3", "l2", "zeros", "mask")}
        stored = sem("stored")
        ld_picked = sem("ld_picked")
        y_stored = sem("y_stored")

        names = ["q_full0", "q_full1", "q_free0", "q_free1", "chain", "pchain", "const", "stats", "rstd_ok", "xn_ok",
                 "cn_ok", "summed", "divided", "scaled", "values_ok", "scored", "masked", "shifted", "maxed", "probs", "turned", "pt_ok", "biased",
                 "multiplied", "roped", "act_ok", "fc1_full", "fc1_free", "fc2_full", "y_ok",
                 "up_in0", "up_in1", "down_in0", "down_in1", "rows_in0", "rows_in1", "y_free", "turned_in", "routed", "picked_in", "taken", "measured", "keys_ok",
                 "counted", "scattered", "xs_ok", "colb_ok", "gat_ok", "exp_ok", "gates_ok"]
        M = {n: sem(n) for n in names}
        turn_sems = range(M[names[0]].num, M[names[-1]].num + 1)
        assert len(turn_sems) == len(names)
        q_full = [M["q_full0"], M["q_full1"]]
        q_free = [M["q_free0"], M["q_free1"]]

        def end_turn():
            nc.all_engine_barrier(sems_to_clear=turn_sems)

        def col(name, c):
            k = COLS.index(name)
            return cols[:, 2 * k + c:2 * k + c + 1]

        def row(name):
            return rows[:, ROWS.index(name), :]

        def at(t, b, n=1):
            v = t[:, bass.ds(b, n), :]
            return v.rearrange("p a d -> p (a d)") if n == 1 else v

        def claim(pe, J, name):
            b, k = J[name]
            if k > 0:
                pe.wait_ge(q_free[b], k)
            return Q[b]

        def await_full(eng, J, name):
            b, k = J[name]
            eng.wait_ge(q_full[b], k + 1)
            return Q[b]

        def await_read(eng, J, name):
            b, k = J[name]
            eng.wait_ge(q_free[b], k + 1)

        def chained(eng, s):
            n = [0]

            def link(ins):
                n[0] += 1
                ins.then_inc(s, 1)
                eng.wait_ge(s, n[0])
            return link

        ZEROS = 8
        ZN = NBLK * BR * D // P // ZEROS
        zeros = view(20480, [ZN])
        with nc.Block(no_gpsimd_drain=True) as block:
            @block.sync
            def _(sp):
                sp.dma_start(xres[:], A["x"].rearrange("b p d -> p b d")).then_inc(ld["x"], 16)
                sp.dma_start(w_sa[:], A["w_sa"].rearrange("(c p) n -> p c n", p=P)).then_inc(ld["sa"], 16)

            @block.scalar
            def _(act):
                for t, n in ((cols, "cols"), (rows, "rows"), (fc1b, "fc1b"), (fc2b, "fc2b"), (rb, "rb"), (sbias, "sbias"),
                             (rope, "rope"), (shape_c, "shape_c")):
                    act.dma_start(t[:], A[n]).then_inc(ld["small"], 16)
                act.dma_start(rw[:], A["rw"].rearrange("(c p) e -> p c e", p=P)).then_inc(ld["small"], 16)
                act.wait_ge(ld["small"], 16 * 9)

            @block.gpsimd
            def _(pool):
                nc.gpsimd.memset(ident[:], 0.0).then_inc(M["const"], 1)
                nc.gpsimd.memset(ones[:], 1.0)
                nc.gpsimd.memset(nhalf[:], -0.5)
                nc.gpsimd.memset(zeros, 0.0)
                pool.wait_ge(M["const"], 1)
                nc.gpsimd.affine_select(out=ident[:], in_=ident[:], compare_op=ALU.not_equal, fill=1.0, base=0,
                                        pattern=[[-1, P]], channel_multiplier=1)

        end_turn()

        def load_the_rest(sp):
            sp.dma_start(ctxr[:], A["ctx"].rearrange("b p d -> p b d")).then_inc(ld["ctx"], 16)
            for n, t in (("ca", w_ca), ("l1", w_l1), ("l3", w_l3)):
                sp.dma_start(t[:], A["w_" + n].rearrange("(c p) n -> p c n", p=P)).then_inc(ld[n], 16)
            for k in range(ZEROS):
                sp.dma_start(xs_dram.rearrange("(p r) d -> p (r d)", p=P)[:, k * ZN:(k + 1) * ZN], zeros)\
                    .then_inc(ld["zeros"], 16)
            for n, t in (("wq2", wq2), ("wkv2", wkv2), ("wo2", wo2), ("wg2", wg2), ("wu2", wu2), ("wd2", wd2)):
                sp.dma_start(t, A[n].rearrange("(c p) n -> p c n", p=P)).then_inc(ld["l2"], 16)

        def dve_stats(dve, link, src, g, k, batches=range(GB)):
            for j in batches:
                last = nc.vector.bn_stats(st[:, k, j, :], at(src, g * GB + j))
            link(last)
            for j in batches:
                nc.vector.bn_aggr(mv[:, k, j, :], st[:, k, j, :]).then_inc(M["stats"], 1)

        def pool_copy(pool, g, batches=range(GB)):
            for j in batches:
                nc.gpsimd.tensor_copy(cn[:, j, :], at(ctxr, g * GB + j)).then_inc(M["cn_ok"], 1)

        def pool_rstd(pool, link, k, n_stats, eps):
            pool.wait_ge(M["stats"], n_stats)
            link(nc.gpsimd.tensor_scalar(ve[:, k, :], mv[:, k, :, 1], eps, 1.0, ALU.add, ALU.mult))
            nc.gpsimd.tensor_tensor(rstd[:, k, :], ve[:, k, :], nhalf[:], ALU.pow).then_inc(M["rstd_ok"], 1)

        def dve_centre(dve, src, dst, g, k, ok, batches=range(GB)):
            for j in batches:
                nc.vector.tensor_scalar(dst[:, j, :], at(src, g * GB + j), mv[:, k, j, 0:1], rstd[:, k, j:j + 1],
                                        ALU.subtract, ALU.mult).then_inc(ok, 1)

        def pe_turn_rows(pe, J, names, src, ok):
            for c in range(C):
                bank = claim(pe, J, names[c])
                for j in range(GB):
                    if c == 0 and ok is not None:
                        pe.wait_ge(ok, j + 1)
                    ins = nc.tensor.transpose(bank[:, j * P:(j + 1) * P], src[:, j, c * P:(c + 1) * P], ident[:])
                ins.then_inc(q_full[J[names[c]][0]], 1)

        def act_affine(act, J, names, dst, gain, bias):
            for c in range(C):
                bank = await_full(act, J, names[c])
                if gain is None:
                    ins = nc.scalar.activation(dst[:, c, :], bank[:, :], ACT.Copy)
                else:
                    ins = nc.scalar.activation(dst[:, c, :], bank[:, :], ACT.Identity, scale=col(gain, c),
                                               bias=col(bias, c) if bias else 0.0)
                ins.then_inc(q_free[J[names[c]][0]], 1)

        def pe_project(pe, J, name, w, w0, src, n=NT):
            bank = claim(pe, J, name)
            for c in range(C):
                ins = nc.tensor.matmul(bank[:, 0:n], w[:, c, w0:w0 + P], src[:, c, :], start=(c == 0), stop=(c == C - 1))
            ins.then_inc(q_full[J[name][0]], 1)

        def pe_values(pe, J, names, w, w0, src):
            for v, name in enumerate(names):
                bank = claim(pe, J, name)
                for jj in range(2):
                    j = 2 * v + jj
                    for c in range(C):
                        ins = nc.tensor.matmul(bank[:, jj * D:(jj + 1) * D], src[:, c, j * P:(j + 1) * P],
                                               w[:, c, w0:w0 + D], start=(c == 0), stop=(c == C - 1))
                ins.then_inc(q_full[J[name][0]], 1)

        def act_values(act, J, names):
            for v, name in enumerate(names):
                bank = await_full(act, J, name)
                pairs = VA[:, 2 * v:2 * v + 2, :, :].rearrange("p j h d -> p (j h d)")\
                    .rearrange("p (n s d) -> p n s d", s=4, d=DH)[:, :, 0:4:3, :]
                nc.scalar.activation(pairs, bank[:, :].rearrange("p (n s d) -> p n s d", s=2, d=DH), ACT.Copy)\
                    .then_inc(q_free[J[name][0]], 1)

        def dve_keys(dve, J, m, bias):
            bank = await_full(dve, J, f"k{m}")
            for k in range(4):
                ins = nc.vector.tensor_scalar(kM[:, k, m, :], bank[:, :], col(bias, m), of_four[:, k:k + 1],
                                              ALU.add, ALU.mult)
            ins.then_inc(q_free[J[f"k{m}"][0]], 1)

        def pe_scores(pe, j, i):
            r = slice(64 * (i % 2), 64 * (i % 2) + 64)
            nc.tensor.matmul(S[i][:, :], qT[r, i // 2, j * P:(j + 1) * P], kM[r, :, i // 2, j * P:(j + 1) * P],
                             start=True, stop=True).then_inc(M["scored"], 1)

        def bank_of(n):
            return SP[:, (n // 4) % 2, n % 4, :, :], S[n % 4][:, :].rearrange("p (s k) -> p s k", k=P)

        def cols_of(t, n):
            return t[:, (n // 4) % 2, 4 * (n % 4):4 * (n % 4) + 4]

        def spread(t, n):
            return cols_of(t, n).unsqueeze(2).to_broadcast([P, 4, P])

        TURN_LAG = 1
        COPY_LAG = 4 + TURN_LAG

        def dve_softmax(dve, N, pv_done, between=None):
            for n in range(N + COPY_LAG):
                if n < N:
                    dve.wait_ge(M["scored"], n + 1)
                    nc.vector.tensor_reduce(cols_of(mx, n), bank_of(n)[1], AX, ALU.max, negate=True)\
                        .then_inc(M["maxed"], 1)
                if 2 <= n < N + 2:
                    dve.wait_ge(M["probs"], n - 1)
                    nc.vector.reciprocal(cols_of(rden, n - 2), cols_of(psum, n - 2)).then_inc(M["divided"], 1)
                if n >= COPY_LAG:
                    m = n - COPY_LAG
                    dve.wait_ge(M["turned"], m + 1)
                    if m >= 8:
                        pv_done(m // 4 - 2)
                    nc.vector.tensor_copy(turned_tile(m), T[m % 2][:, :].rearrange("p (s q) -> p s q", q=P))\
                        .then_inc(M["pt_ok"], 1)
                if between:
                    between(n)

        def turned_tile(m):
            return PT[:, (m // 4) % 2, 4 * (m % 4):4 * (m % 4) + 4, :]

        def pool_scale(pool, m):
            pool.wait_ge(M["divided"], m + 1)
            v = bank_of(m)[0]
            nc.gpsimd.tensor_tensor(v, v, spread(rden, m), ALU.mult).then_inc(M["scaled"], 1)

        def act_exp(act, n, source):
            act.wait_ge(M["maxed"], n + 1)
            if n >= 8:
                act.wait_ge(M["turned"], n - 7)
            for a in range(4):
                ins = nc.scalar.activation(bank_of(n)[0][:, a, :], source[:, a, :], ACT.Exp,
                                           bias=cols_of(mx, n)[:, a:a + 1], accum_out=cols_of(psum, n)[:, a:a + 1])
            ins.then_inc(M["probs"], 1)

        def pe_turn(pe, n):
            pe.wait_ge(M["scaled"], n + 1)
            if n >= 2:
                pe.wait_ge(M["pt_ok"], n - 1)
            for s in range(4):
                ins = nc.tensor.transpose(T[n % 2][:, s * P:(s + 1) * P], bank_of(n)[0][:, s, :], ident[:])
            ins.then_inc(M["turned"], 1)

        def pe_products(pe, bank, j, out_cols, in_cols, half):
            for m in range(C):
                for par in range(2):
                    for x in range(4):
                        h = 8 * m + 2 * x + par
                        ins = nc.tensor.matmul(bank[32 * x:32 * x + 32, m * P + out_cols.start:m * P + out_cols.stop],
                                               VA[:, j, h, :], PT[:, half, h, in_cols],
                                               start=(par == 0), stop=(par == 1))
            return ins

        def act_products(act, J, name, bv, dst_cols):
            bank = await_full(act, J, name)
            for c in range(C):
                ins = nc.scalar.activation(oT[:, c, dst_cols], bank[:, c * P:(c + 1) * P], ACT.Identity, bias=col(bv, c))
            ins.then_inc(q_free[J[name][0]], 1)

        def attention(q_norm, kv, w, bq, bk, bv, ob, loads, store=False):
            turn = ["hx0", "hx1"] + ([] if kv == "self" else ["hc0", "hc1"])
            J_first = Jobs(turn)
            J = Jobs(["k0", "k1", "q0", "q1", "v0", "v1", "pv0", "pv1", "pv2"] + turn + ["y0", "pv3", "y1"])
            kvT = hT if kv == "self" else cT

            def pe_turn_group(pe, J):
                pe_turn_rows(pe, J, ["hx0", "hx1"], xn, M["xn_ok"])
                if kv != "self":
                    pe_turn_rows(pe, J, ["hc0", "hc1"], cn, M["cn_ok"])

            def act_norm_group(act, J):
                act_affine(act, J, ["hx0", "hx1"], hT, *q_norm)
                if kv == "norm":
                    act_affine(act, J, ["hc0", "hc1"], cT, "ck_g", "ck_b")
                elif kv == "raw":
                    act_affine(act, J, ["hc0", "hc1"], cT, None, None)

            def pool_norm_group(pool, link, g):
                pool_rstd(pool, link, 0, GB, LN_EPS)
                if kv == "norm":
                    pool_rstd(pool, link, 1, 2 * GB, LN_EPS)
                if kv == "raw":
                    pool_copy(pool, g)

            def dve_stats_group(dve, link, g):
                dve_stats(dve, link, xres, g, 0)
                if kv == "norm":
                    dve_stats(dve, link, ctxr, g, 1)

            def dve_centre_group(dve, g):
                dve.wait_ge(M["rstd_ok"], 1)
                dve_centre(dve, xres, xn, g, 0, M["xn_ok"])
                if kv == "norm":
                    dve.wait_ge(M["rstd_ok"], 2)
                    dve_centre(dve, ctxr, cn, g, 1, M["cn_ok"])

            with nc.Block(no_gpsimd_drain=True) as block:
                @block.tensor
                def _(pe):
                    pe_turn_group(pe, J_first)

                @block.scalar
                def _(act):
                    act_norm_group(act, J_first)

                @block.gpsimd
                def _(pool):
                    if kv == "raw":
                        pool.wait_ge(ld["ctx"], 16)
                    nc.gpsimd.memset(VA[:, :, :, :], 0.0)
                    pool_norm_group(pool, chained(pool, M["pchain"]), 0)

                @block.vector
                def _(dve):
                    dve.wait_ge(ld["x"], 16)
                    if kv == "norm":
                        dve.wait_ge(ld["ctx"], 16)
                    dve_stats_group(dve, chained(dve, M["chain"]), 0)
                    dve_centre_group(dve, 0)

                @block.sync
                def _(sp):
                    if kv == "self":
                        load_the_rest(sp)
            end_turn()

            N = 4 * GB
            with nc.Fori(0, G) as g:
                g_next = (g + 1) & (G - 1)
                with nc.Block(no_gpsimd_drain=True) as block:
                    @block.tensor
                    def _(pe):
                        for s in loads:
                            pe.wait_ge(ld[s], 16)
                        for m in range(C):
                            pe_project(pe, J, f"k{m}", w, D + m * P, kvT)
                        for m in range(C):
                            pe_project(pe, J, f"q{m}", w, m * P, hT)
                        pe_values(pe, J, ["v0", "v1"], w, 2 * D, kvT)
                        for n in ("q0", "q1", "k0", "k1"):
                            await_read(pe, J, n)
                        for i in range(4):
                            pe_scores(pe, 0, i)

                        def products(j):
                            pe.wait_ge(M["pt_ok"], 4 * j + 4)
                            if j == 0:
                                await_read(pe, J, "v0")
                                await_read(pe, J, "v1")
                            bank = claim(pe, J, f"pv{j}")
                            pe_products(pe, bank, j, slice(0, P), slice(0, P), j % 2).then_inc(q_full[J[f"pv{j}"][0]], 1)

                        def out_rows(y):
                            await_read(pe, J, f"pv{2 * y}")
                            await_read(pe, J, f"pv{2 * y + 1}")
                            bank = claim(pe, J, f"y{y}")
                            for jj in range(2):
                                j = 2 * y + jj
                                for c in range(C):
                                    ins = nc.tensor.matmul(bank[:, jj * D:(jj + 1) * D], oT[:, c, j * P:(j + 1) * P],
                                                           w[:, c, 3 * D:4 * D], start=(c == 0), stop=(c == C - 1))
                            ins.then_inc(q_full[J[f"y{y}"][0]], 1)

                        for n in range(N + TURN_LAG):
                            if n + 4 < N:
                                pe.wait_ge(M["probs"], n + 1)
                                pe_scores(pe, n // 4 + 1, n % 4)
                            m = n - TURN_LAG
                            if m >= 0:
                                pe_turn(pe, m)
                            if m % 4 == 2 and m > 4:
                                products(m // 4 - 1)
                        pe_turn_group(pe, J)
                        out_rows(0)
                        products(GB - 1)
                        out_rows(1)

                    @block.scalar
                    def _(act):
                        for m in range(C):
                            bank = await_full(act, J, f"q{m}")
                            nc.scalar.activation(qT[:, m, :], bank[:, :], ACT.Identity, bias=col(bq, m))\
                                .then_inc(q_free[J[f"q{m}"][0]], 1)

                        act_values(act, J, ["v0", "v1"])
                        for n in range(N):
                            act_exp(act, n, bank_of(n)[1])
                            j = (n - 10 - TURN_LAG) // 4
                            if j >= 0 and n == 4 * j + 10 + TURN_LAG:
                                act_products(act, J, f"pv{j}", bv, slice(j * P, (j + 1) * P))
                        act_products(act, J, "pv2", bv, slice(2 * P, 3 * P))
                        act_norm_group(act, J)
                        act_products(act, J, "pv3", bv, slice(3 * P, 4 * P))

                    @block.gpsimd
                    def _(pool):
                        link = chained(pool, M["pchain"])
                        for j in range(GB):
                            nc.gpsimd.tensor_tensor(at(xres, g * GB + j), at(xres, g * GB + j), row(ob), ALU.add)\
                                .then_inc(M["biased"], 1)
                        for n in range(N):
                            pool_scale(pool, n)
                            if n == 6:
                                pool_rstd(pool, link, 0, GB, LN_EPS)
                            if n == 7 and kv == "norm":
                                pool_rstd(pool, link, 1, 2 * GB, LN_EPS)
                            if 7 <= n < 7 + GB and kv == "raw":
                                pool_copy(pool, g_next, [n - 7])

                    @block.vector
                    def _(dve):
                        link = chained(dve, M["chain"])
                        for m in range(C):
                            dve_keys(dve, J, m, bk)

                        def row_stats(j):
                            nc.vector.bn_stats(st[:, 0, j, :], at(xres, g_next * GB + j)).then_inc(M["measured"], 1)
                            if kv == "norm":
                                nc.vector.bn_stats(st[:, 1, j, :], at(ctxr, g_next * GB + j)).then_inc(M["measured"], 1)

                        def aggregate(k):
                            dve.wait_ge(M["measured"], 2 * GB if kv == "norm" else GB)
                            for j in range(GB):
                                nc.vector.bn_aggr(mv[:, k, j, :], st[:, k, j, :]).then_inc(M["stats"], 1)

                        def between(n):
                            if 1 <= n <= GB:
                                row_stats(n - 1)
                            if n == GB + 2:
                                aggregate(0)
                            if n == GB + 3 and kv == "norm":
                                aggregate(1)
                            j = n - 11
                            if j == 0:
                                dve.wait_ge(M["rstd_ok"], 2 if kv == "norm" else 1)
                            if 0 <= j < GB:
                                dve_centre(dve, xres, xn, g_next, 0, M["xn_ok"], [j])
                                if kv == "norm":
                                    dve_centre(dve, ctxr, cn, g_next, 1, M["cn_ok"], [j])
                        dve_softmax(dve, N, lambda j: await_full(dve, J, f"pv{j}"), between)
                        dve.wait_ge(M["biased"], GB)
                        for y in range(2):
                            bank = await_full(dve, J, f"y{y}")
                            x2 = at(xres, g * GB + 2 * y, 2)
                            nc.vector.tensor_tensor(x2, bank[:, :].rearrange("p (j d) -> p j d", j=2), x2, ALU.add)\
                                .then_inc(q_free[J[f"y{y}"][0]], 1)

                    @block.sync
                    def _(sp):
                        if store:
                            await_read(sp, J, "y0")
                            await_read(sp, J, "y1")
                            sp.dma_start(out.rearrange("b p d -> p b d")[:, bass.ds(g * GB, GB), :],
                                         at(xres, g * GB, GB)).then_inc(stored, 16)
                end_turn()

        attention(("sa_g", "sa_b"), "self", w_sa, "sa_bq", "sa_bk", "sa_bv", "sa_ob", ["sa"])
        attention(("cq_g", "cq_b"), "norm", w_ca, "ca_bq", "ca_bk", "ca_bv", "ca_ob", ["ca"])

        with nc.Block(no_gpsimd_drain=True) as block:
            @block.sync
            def _(sp):
                sp.wait_ge(ld["zeros"], 16 * ZEROS)
                sp.dma_start(mask2, A["mask"].rearrange("b q k -> q b k")).then_inc(ld["mask"], 16)

        def expert_of(eng, k):
            return eng.value_load(block_expert[0:1, bass.ds(k, 1)], min_val=0, max_val=E - 1)

        def load_up(sp, block_k, k, s):
            e = expert_of(sp, block_k)
            sp.dma_start(up_w8[k], A["fc1"][bass.ds(e * D, D), :].rearrange("(c p) f -> p c f", p=P)).then_inc(s, 16)

        def load_down(sp, block_k, k, s):
            e = expert_of(sp, block_k)
            sp.dma_start(down_w8[k], A["fc2"][bass.ds(e * FF, FF), :].rearrange("(f p) d -> p f d", p=P)).then_inc(s, 16)

        def load_rows(sp, block_k, k):
            sp.dma_start(xb[:, k, :, :], xs_dram[bass.ds(block_k * BR, BR), :].rearrange("(t p) d -> p t d", p=P))\
                .then_inc(M[f"rows_in{k}"], 16)

        def pe_block_rows(pe, k):
            pe.wait_ge(M[f"rows_in{k}"], 16)
            for c in range(C):
                for t in range(BT):
                    ins = nc.tensor.transpose(S[2 * k + c][:, t * P:(t + 1) * P], xb[:, k, t, c * P:(c + 1) * P], ident[:])
            ins.then_inc(M["turned_in"], 1)

        def act_block_rows(act, k):
            act.wait_ge(M["turned_in"], k + 1)
            for c in range(C):
                nc.scalar.activation(xbT[:, k, c, :], S[2 * k + c][:, 0:BR], ACT.Identity, scale=col("me_g", c),
                                     bias=col("me_b", c))

        J_route = Jobs(["hx0", "hx1", "logits"])
        with nc.Fori(0, G) as g:
            with nc.Block(no_gpsimd_drain=True) as block:
                @block.tensor
                def _(pe):
                    J = J_route
                    pe_turn_rows(pe, J, ["hx0", "hx1"], xn, M["xn_ok"])
                    await_read(pe, J, "hx0")
                    await_read(pe, J, "hx1")
                    bank = claim(pe, J, "logits")
                    for j in range(GB):
                        for c in range(C):
                            ins = nc.tensor.matmul(bank[:, j * E:(j + 1) * E], hT[:, c, j * P:(j + 1) * P], rw[:, c, :],
                                                   start=(c == 0), stop=(c == C - 1))
                    ins.then_inc(q_full[J["logits"][0]], 1)

                @block.scalar
                def _(act):
                    J = J_route
                    for c in range(C):
                        bank = await_full(act, J, f"hx{c}")
                        nc.scalar.activation(hT[:, c, :], bank[:, :], ACT.Identity,
                                             scale=col("me_g", c), bias=col("me_b", c)).then_inc(q_free[J[f"hx{c}"][0]], 1)

                @block.gpsimd
                def _(pool):
                    pool_rstd(pool, chained(pool, M["pchain"]), 0, GB, LN_EPS)
                    for j in range(GB):
                        pool.wait_ge(M["xn_ok"], j + 1)
                        nc.gpsimd.tensor_copy(at(xnall, g * GB + j), xn[:, j, :])

                @block.vector
                def _(dve):
                    J = J_route
                    dve_stats(dve, chained(dve, M["chain"]), xres, g, 0)
                    dve.wait_ge(M["rstd_ok"], 1)
                    dve_centre(dve, xres, xn, g, 0, M["xn_ok"])
                    bank = await_full(dve, J, "logits")
                    nc.vector.tensor_tensor(logit[:, bass.ds(g * GB, GB), :],
                                            bank[:, 0:GB * E].rearrange("p (j e) -> p j e", e=E),
                                            rb[:, :].unsqueeze(1).to_broadcast([P, GB, E]), ALU.add)\
                        .then_inc(q_free[J["logits"][0]], 1)
            end_turn()

        above = view(17408, [B, E, E])
        tied = view(17408 + B * E * E, [B, E, E])
        at_be = [view(19456 + k * B * E, [B, E]) for k in range(6)]
        rank, chosen, first, second, row_of, part_be = at_be
        per_expert = view(19456 + 6 * B * E, [6, E])
        n_chosen, n_rows, n_blocks, start, end = [per_expert[:, k, :] for k in range(5)]
        over = view(20480, [E, NSTEP])
        earlier = view(20608, [E, E])
        ended = view(20736, [NBLK, E])
        block_at = view(20992, [NBLK])
        later = view(21056, [P])
        top = small[:, 0:B]
        total = small[:, B:2 * B]
        inverse = small[:, 2 * B:3 * B]
        gateT = view(11264, [B * P])
        J_gate = Jobs([f"t{k}" for k in range(G)] + [f"b{k}" for k in range(B // 2)])
        with nc.Block(no_gpsimd_drain=True) as block:
            @block.vector
            def _(dve):
                J = J_gate
                link = chained(dve, M["chain"])
                others = logit[:, :, :].unsqueeze(2).to_broadcast([P, B, E, E])
                own = logit[:, :, :].unsqueeze(3).to_broadcast([P, B, E, E])
                nc.vector.tensor_tensor(above, others, own, ALU.is_gt)
                nc.vector.tensor_reduce(top, logit[:, :, :], AX, ALU.max)
                link(nc.vector.tensor_tensor(tied, others, own, ALU.is_equal))
                nc.vector.tensor_tensor(gl1[:, :, :], logit[:, :, :], top.unsqueeze(2).to_broadcast([P, B, E]),
                                        ALU.subtract).then_inc(M["shifted"], 1)
                nc.vector.tensor_tensor(later, ones[:, :], before, ALU.subtract)
                link(nc.vector.tensor_tensor(tied, tied, ebefore.unsqueeze(1).to_broadcast([P, B, E, E]), ALU.mult))
                nc.vector.tensor_tensor(later, later, ident[:, :], ALU.subtract)
                link(nc.vector.tensor_tensor(above, above, tied, ALU.add))
                link(nc.vector.tensor_reduce(rank, above, AX, ALU.add))
                nc.vector.tensor_scalar(chosen, rank, 1.5, None, ALU.is_lt)
                nc.vector.tensor_scalar(first, rank, 0.0, None, ALU.is_equal)
                link(nc.vector.tensor_scalar(second, rank, 1.0, None, ALU.is_equal))
                nc.vector.tensor_reduce(n_chosen, chosen.rearrange("p b e -> p e b"), AX, ALU.add)\
                    .then_inc(M["routed"], 1)
                dve.wait_ge(M["counted"], 1)
                link(nc.vector.tensor_copy(n_rows, T[1][:, 0:E]))
                link(nc.vector.tensor_tensor(over, n_rows.unsqueeze(2).to_broadcast([P, E, NSTEP]),
                                             steps.unsqueeze(1).to_broadcast([P, E, NSTEP]), ALU.is_gt))
                link(nc.vector.tensor_reduce(n_blocks, over, AX, ALU.add))
                link(nc.vector.tensor_tensor(earlier, n_blocks.unsqueeze(1).to_broadcast([P, E, E]), ebefore, ALU.mult))
                link(nc.vector.tensor_reduce(start, earlier, AX, ALU.add))
                link(nc.vector.tensor_tensor(end, start, n_blocks, ALU.add))
                link(nc.vector.tensor_tensor(ended, end.unsqueeze(1).to_broadcast([P, NBLK, E]),
                                             block_ids.unsqueeze(2).to_broadcast([P, NBLK, E]), ALU.is_le))
                link(nc.vector.tensor_reduce(block_at, ended, AX, ALU.add))
                nc.vector.tensor_scalar(block_expert[:, :], block_at, E - 1.0, None, ALU.min).then_inc(M["routed"], 1)
                link(nc.vector.tensor_scalar(start, start, float(BR), None, ALU.mult))
                link(nc.vector.tensor_tensor(row_of, T[0][:, 0:B * E].rearrange("p (b e) -> p b e", e=E),
                                             start.unsqueeze(1).to_broadcast([P, B, E]), ALU.add))
                for k, mask in enumerate((first, second)):
                    link(nc.vector.tensor_tensor(part_be, row_of, mask, ALU.mult))
                    link(nc.vector.tensor_reduce(total, part_be, AX, ALU.add))
                    nc.vector.tensor_copy(pick_row[:, k, :], total).then_inc(M["routed"], 1)
                dve.wait_ge(M["exp_ok"], 1)
                link(nc.vector.tensor_tensor(gl1[:, :, :], gl1[:, :, :], chosen, ALU.mult))
                link(nc.vector.tensor_reduce(total, gl1[:, :, :], AX, ALU.add))
                link(nc.vector.reciprocal(inverse, total))
                nc.vector.tensor_tensor(gates[:, :, :], gl1[:, :, :], inverse.unsqueeze(2).to_broadcast([P, B, E]),
                                        ALU.mult).then_inc(M["gates_ok"], 1)
                dve.wait_ge(M["gates_ok"], 1)
                for k, mask in enumerate((first, second)):
                    link(nc.vector.tensor_tensor(part_be, gates[:, :, :], mask, ALU.mult))
                    link(nc.vector.tensor_reduce(pick_gate[:, k, :], part_be, AX, ALU.add))
                for k in range(B // 2):
                    bank = await_full(dve, J, f"b{k}")
                    x2 = xres[:, 2 * k:2 * k + 2, :]
                    nc.vector.tensor_tensor(x2, bank[:, :].rearrange("p (j d) -> p j d", j=2), x2, ALU.add)\
                        .then_inc(q_free[J[f"b{k}"][0]], 1)

            @block.gpsimd
            def _(pool):
                for k in range(2):
                    pool.wait_ge(M["routed"], 3 + k)
                    for b in range(B):
                        nc.gpsimd.indirect_dma_start(xs_dram, bass.IndirectOffsetOnAxis(pick_row[:, k, b:b + 1], 0),
                                                     xnall[:, b, :], None).then_inc(M["scattered"], 16)
                pool.wait_ge(M["scattered"], 16 * 2 * B)

            @block.sync
            def _(sp):
                sp.wait_ge(M["routed"], 2)
                for k in range(2):
                    load_up(sp, k, k, M[f"up_in{k}"])
                load_down(sp, 0, 0, M["down_in0"])
                sp.wait_ge(M["scattered"], 16 * 2 * B)
                for k in range(2):
                    load_rows(sp, k, k)
                for n in ("up_in0", "up_in1"):
                    sp.wait_ge(M[n], 16)
                sp.wait_ge(M["down_in0"], 16)
                sp.sem_inc(y_stored, 32)

            @block.scalar
            def _(act):
                J = J_gate
                act.wait_ge(M["shifted"], 1)
                nc.scalar.activation(gl1[:, :, :], gl1[:, :, :], ACT.Exp).then_inc(M["exp_ok"], 1)
                for k in range(G):
                    bank = await_full(act, J, f"t{k}")
                    nc.scalar.activation(gateT[0:E, k * NT:(k + 1) * NT], bank[0:E, :], ACT.Copy)\
                        .then_inc(q_free[J[f"t{k}"][0]], 1)
                for k in range(2):
                    act_block_rows(act, k)

            @block.tensor
            def _(pe):
                J = J_gate
                pe.wait_ge(M["routed"], 1)
                nc.tensor.matmul(T[0][:, 0:B * E], later, chosen.rearrange("p b e -> p (b e)"), start=True, stop=False)
                for b in range(B - 1):
                    nc.tensor.matmul(T[0][:, (b + 1) * E:B * E].rearrange("p (b e) -> p b e", e=E), ones[:, :],
                                     chosen[:, b:b + 1, :].to_broadcast([P, B - 1 - b, E]), start=False,
                                     stop=(b == B - 2))
                nc.tensor.matmul(T[1][:, 0:E], ones[:, :], n_chosen, start=True, stop=True).then_inc(M["counted"], 1)
                pe.wait_ge(M["gates_ok"], 1)
                for k in range(G):
                    bank = claim(pe, J, f"t{k}")
                    for j in range(GB):
                        ins = nc.tensor.transpose(bank[0:E, j * P:(j + 1) * P], gates[:, k * GB + j, :], ident[:])
                    ins.then_inc(q_full[J[f"t{k}"][0]], 1)
                for k in range(G):
                    await_read(pe, J, f"t{k}")
                for k in range(B // 2):
                    bank = claim(pe, J, f"b{k}")
                    for j in range(2):
                        b = 2 * k + j
                        ins = nc.tensor.matmul(bank[:, j * D:(j + 1) * D], gateT[0:E, b * P:(b + 1) * P], fc2b[:, :],
                                               start=True, stop=True)
                    ins.then_inc(q_full[J[f"b{k}"][0]], 1)
                for k in range(2):
                    pe_block_rows(pe, k)
        end_turn()

        sums = small[:, 32:36]
        gamma, half_step, minus = small[:, 36:40], small[:, 40:44], small[:, 44:48]
        up_w, down_w = view(0, [C, D]), view(512, [C, D])
        sums_bank = banks[5][:, 2 * D - 4:2 * D]

        def dve_ternary(dve):
            link = chained(dve, M["chain"])
            dve.wait_ge(ld["l3"], 16)
            W4 = [w_l3[:, :, k * D:(k + 1) * D] for k in range(4)]
            for k in range(4):
                nc.vector.tensor_reduce(sums[:, k:k + 1], W4[k], mybir.AxisListType.XY, ALU.add,
                                        apply_absolute_value=True).then_inc(M["maxed"], 1)
            dve.wait_ge(M["scored"], 1)
            nc.vector.tensor_scalar(gamma, sums_bank, 1.0 / (D * D), None, ALU.mult).then_inc(M["summed"], 1)
            dve.wait_ge(M["summed"], 1)
            link(nc.vector.tensor_scalar(half_step, gamma, Q_EPS, 0.5, ALU.add, ALU.mult))
            link(nc.vector.tensor_scalar(minus, half_step, -1.0, None, ALU.mult))
            for k in range(4):
                link(nc.vector.tensor_scalar(up_w, W4[k], half_step[:, k:k + 1], gamma[:, k:k + 1], ALU.is_gt, ALU.mult))
                link(nc.vector.tensor_scalar(down_w, W4[k], minus[:, k:k + 1], gamma[:, k:k + 1], ALU.is_lt, ALU.mult))
                link(nc.vector.tensor_tensor(up_w, up_w, down_w, ALU.subtract))
                link(nc.vector.tensor_tensor(up_w, up_w, W4[k], ALU.subtract))
                link(nc.vector.tensor_tensor(W4[k], W4[k], up_w, ALU.add))

        def experts(p, last):
            with nc.Block(no_gpsimd_drain=True) as block:
                @block.sync
                def _(sp):
                    load_down(sp, p * 2 + 1, 1, M["down_in1"])
                    sp.wait_ge(y_stored, (p + 1) * 32)
                    sp.sem_inc(M["y_free"], 1)
                    if not last:
                        for k in range(2):
                            load_rows(sp, p * 2 + 2 + k, k)
                        for k in range(2):
                            sp.wait_ge(M["fc1_full"], FC * (k + 1))
                            load_up(sp, p * 2 + 2 + k, k, M[f"up_in{k}"])
                        sp.wait_ge(M["fc2_full"], len(PAIRS))
                        load_down(sp, p * 2 + 2, 0, M["down_in0"])
                    for k in range(2):
                        sp.wait_ge(M["y_ok"], len(PAIRS) * (k + 1))
                        sp.dma_start(ys_dram[bass.ds((p * 2 + k) * BR, BR), :].rearrange("(t p) d -> p t d", p=P),
                                     yb[:, k, :, :]).then_inc(y_stored, 16)
                    if not last:
                        for n in ("up_in0", "up_in1"):
                            sp.wait_ge(M[n], 16)
                        sp.wait_ge(M["down_in0"], 16)
                    else:
                        sp.wait_ge(y_stored, (NBLK // 2 + 1) * 32)

                @block.tensor
                def _(pe):
                    for k in range(2):
                        for f in range(FC):
                            n = FC * k + f
                            if n >= 4:
                                pe.wait_ge(M["fc1_free"], n - 3)
                            for c in range(C):
                                ins = nc.tensor.matmul(S[n % 4][:, 0:BR], up_w8[k][:, c, f * P:(f + 1) * P],
                                                       xbT[:, k, c, :], start=(c == 0), stop=(c == C - 1))
                            ins.then_inc(M["fc1_full"], 1)
                    if last:
                        pe.wait_ge(M["maxed"], 4)
                        nc.tensor.matmul(sums_bank, ones[:, :], sums, start=True, stop=True).then_inc(M["scored"], 1)
                        pe.wait_ge(M["summed"], 1)
                    for k in range(2):
                        pe.wait_ge(M["fc1_free"], FC * (k + 1))
                        if k == 1:
                            if not last:
                                for b in range(2):
                                    pe_block_rows(pe, b)
                            pe.wait_ge(M["down_in1"], 16)
                        for m, tiles in enumerate(PAIRS):
                            for t in tiles:
                                for f in range(FC):
                                    ins = nc.tensor.matmul(banks[4 + 2 * k + m][:, (t - 2 * m) * D:(t - 2 * m + 1) * D],
                                                           h1[:, k, f, t * P:(t + 1) * P], down_w8[k][:, f, :],
                                                           start=(f == 0), stop=(f == FC - 1))
                            ins.then_inc(M["fc2_full"], 1)

                @block.scalar
                def _(act):
                    for k in range(2):
                        e = expert_of(act, p * 2 + k)
                        for f in range(FC):
                            n = FC * k + f
                            act.wait_ge(M["fc1_full"], n + 1)
                            nc.scalar.activation(h1[:, k, f, :], S[n % 4][:, 0:BR], ACT.Gelu,
                                                 bias=fc1b[:, bass.ds(e * FC + f, 1)]).then_inc(M["fc1_free"], 1)
                    if not last:
                        for k in range(2):
                            act_block_rows(act, k)

                @block.vector
                def _(dve):
                    if last:
                        dve_ternary(dve)
                    dve.wait_ge(M["y_free"], 1)
                    for k in range(2):
                        for m, tiles in enumerate(PAIRS):
                            n = len(tiles)
                            dve.wait_ge(M["fc2_full"], len(PAIRS) * k + m + 1)
                            nc.vector.tensor_copy(yb[:, k, tiles.start:tiles.stop, :], banks[4 + 2 * k + m][:, 0:n * D]
                                                  .rearrange("p (t d) -> p t d", d=D)).then_inc(M["y_ok"], 1)

                @block.gpsimd
                def _(pool):
                    if last:
                        nc.gpsimd.memset(VA[:, :, :, :], 0.0)
                        pool_copy(pool, 0)
            end_turn()

        with nc.Fori(0, NBLK // 2 - 1) as p:
            experts(p, False)
        experts(NBLK // 2 - 1, True)

        score, scoreb = small[:, 0:GB], small[:, 4:4 + GB]
        n_above, n_tied = small[:, 8:8 + GB], small[:, 12:12 + GB]
        place, keep = small[:, 16:16 + GB], small[:, 20:20 + GB]
        TAIL = ["pv", "y"] + [f"s{j}" for j in range(GB)]
        HEAD = ["hc0", "hc1", "k0", "k1", "v0", "v1", "xs", "gt", "q0", "q1"]

        def pool_pick(pool, link, g):
            link(nc.gpsimd.tensor_copy(pick_now[:, :, :], pick_row[:, :, bass.ds(g * GB, GB)]))
            for k in range(2):
                for j in range(GB):
                    nc.gpsimd.indirect_dma_start(picked[:, k, j, :], None, ys_dram,
                                                 bass.IndirectOffsetOnAxis(pick_now[:, k, j:j + 1], 0))\
                        .then_inc(ld_picked, 16)

        def pool_picked(pool, g):
            pool.wait_ge(ld_picked, (g + 1) * (16 * 2 * GB))
            pool.sem_inc(M["picked_in"], 1)

        def pool_rows(pool, g):
            for j in range(GB):
                pool.wait_ge(M["taken"], 2 * GB)
                nc.gpsimd.tensor_copy(xs[:, j, :], at(xres, g * GB + j)).then_inc(M["xs_ok"], 1)

        def dve_take(dve, g):
            dve.wait_ge(M["picked_in"], 1)
            for k in range(2):
                for j in range(GB):
                    if k == 1:
                        dve.wait_ge(M["taken"], j + 1)
                    x = at(xres, g * GB + j)
                    nc.vector.scalar_tensor_tensor(out=x, in0=picked[:, k, j, :],
                                                   scalar=pick_gate[:, k, bass.ds(g * GB + j, 1)], in1=x,
                                                   op0=ALU.mult, op1=ALU.add).then_inc(M["taken"], 1)

        def dve_score(dve, link, g):
            for j in range(GB):
                dve.wait_ge(M["taken"], GB + j + 1)
                ins = nc.vector.scalar_tensor_tensor(out=junk, in0=at(xres, g * GB + j), scalar=1.0, in1=row("l1_sw"),
                                                     op0=ALU.mult, op1=ALU.mult, accum_out=score[:, j:j + 1])
                link(ins)
            link(nc.vector.tensor_scalar(scoreb, score, sbias[:, 0:1], None, ALU.add))
            for j in range(GB):
                nc.vector.tensor_scalar(colb[:, j, :], ones[:, :], scoreb[:, j:j + 1], None, ALU.mult)\
                    .then_inc(M["colb_ok"], 1)

        def pe_score_row(pe, J):
            bank = claim(pe, J, "row")
            pe.wait_ge(M["colb_ok"], GB)
            for j in range(GB):
                ins = nc.tensor.transpose(bank[:, j * P:(j + 1) * P], colb[:, j, :], ident[:])
            ins.then_inc(q_full[J["row"][0]], 1)

        def dve_choose(dve, link, J):
            bank = await_full(dve, J, "row")
            for j in range(GB):
                each = bank[:, j * P:(j + 1) * P]
                link(nc.vector.tensor_scalar(junk[:, 0:P], each, scoreb[:, j:j + 1], None, ALU.is_gt, ALU.add,
                                             accum_out=n_above[:, j:j + 1]))
                link(nc.vector.scalar_tensor_tensor(out=junk[:, 0:P], in0=each, scalar=scoreb[:, j:j + 1],
                                                    in1=before, op0=ALU.is_equal, op1=ALU.mult,
                                                    accum_out=n_tied[:, j:j + 1]))
            dve.sem_inc(q_free[J["row"][0]], 1)
            link(nc.vector.tensor_tensor(place, n_above, n_tied, ALU.add))
            for j in range(GB):
                nc.vector.tensor_scalar(gat[:, j, :], ranks, place[:, j:j + 1], None, ALU.is_equal)

        J_choose = Jobs(["row"])
        with nc.Block(no_gpsimd_drain=True) as block:
            @block.gpsimd
            def _(pool):
                pool_pick(pool, chained(pool, M["pchain"]), 0)
                pool_picked(pool, 0)
                pool_rows(pool, 0)

            @block.vector
            def _(dve):
                link = chained(dve, M["chain"])
                dve_take(dve, 0)
                dve_score(dve, link, 0)
                dve_choose(dve, link, J_choose)

            @block.tensor
            def _(pe):
                pe_score_row(pe, J_choose)
        end_turn()

        def best_tokens(g, last):
            J = Jobs(HEAD + ([] if last else ["row"]) + TAIL)
            with nc.Block(no_gpsimd_drain=True) as block:
                @block.tensor
                def _(pe):
                    pe.wait_ge(ld["l1"], 16)
                    pe_turn_rows(pe, J, ["hc0", "hc1"], cn, None)
                    await_read(pe, J, "hc0")
                    await_read(pe, J, "hc1")
                    for m in range(C):
                        pe_project(pe, J, f"k{m}", w_l1, D + m * P, cT)
                    pe_values(pe, J, ["v0", "v1"], w_l1, 2 * D, cT)
                    bank = claim(pe, J, "xs")
                    for c in range(C):
                        for j in range(GB):
                            ins = nc.tensor.matmul(bank[:, c * P + j * R:c * P + (j + 1) * R], xs[:, j, c * P:(c + 1) * P],
                                                   gat[:, j, :], start=True, stop=True)
                    ins.then_inc(q_full[J["xs"][0]], 1)
                    bank = claim(pe, J, "gt")
                    nc.tensor.transpose(bank[:, 0:P], gat[:, :, :].rearrange("p j r -> p (j r)"), ident[:])\
                        .then_inc(q_full[J["gt"][0]], 1)
                    await_read(pe, J, "xs")
                    for m in range(C):
                        pe_project(pe, J, f"q{m}", w_l1, m * P, xsT, P)
                    for n in ("k0", "k1", "q0", "q1"):
                        await_read(pe, J, n)
                    for i in range(4):
                        r = slice(64 * (i % 2), 64 * (i % 2) + 64)
                        for j in range(GB):
                            ins = nc.tensor.matmul(S[i][j * R:(j + 1) * R, :], q1T[r, i // 2, j * R:(j + 1) * R],
                                                   kM[r, :, i // 2, j * P:(j + 1) * P], start=True, stop=True)
                        ins.then_inc(M["scored"], 1)
                    for n in range(4):
                        pe_turn(pe, n)
                    if not last:
                        pe_score_row(pe, J)
                    pe.wait_ge(M["pt_ok"], 4)
                    await_read(pe, J, "v0")
                    await_read(pe, J, "v1")
                    bank = claim(pe, J, "pv")
                    for j in range(GB):
                        r = slice(j * R, (j + 1) * R)
                        ins = pe_products(pe, bank, j, r, r, 0)
                    ins.then_inc(q_full[J["pv"][0]], 1)
                    await_read(pe, J, "pv")
                    bank = claim(pe, J, "y")
                    for c in range(C):
                        ins = nc.tensor.matmul(bank[:, 0:D], oT[:, c, 0:P], w_l1[:, c, 3 * D:4 * D],
                                               start=(c == 0), stop=(c == C - 1))
                    ins.then_inc(q_full[J["y"][0]], 1)
                    await_read(pe, J, "y")
                    await_read(pe, J, "gt")
                    for j in range(GB):
                        bank = claim(pe, J, f"s{j}")
                        r = slice(j * R, (j + 1) * R)
                        nc.tensor.matmul(bank[:, 0:D], gatT[r, :], yo[r, :], start=True, stop=True)\
                            .then_inc(q_full[J[f"s{j}"][0]], 1)

                @block.scalar
                def _(act):
                    act_affine(act, J, ["hc0", "hc1"], cT, None, None)
                    act_values(act, J, ["v0", "v1"])
                    bank = await_full(act, J, "xs")
                    nc.scalar.activation(xsT[:, :, :], bank[:, 0:C * P].rearrange("p (c n) -> p c n", c=C), ACT.Copy)\
                        .then_inc(q_free[J["xs"][0]], 1)
                    bank = await_full(act, J, "gt")
                    nc.scalar.activation(gatT, bank[:, 0:P], ACT.Copy).then_inc(q_free[J["gt"][0]], 1)
                    for m in range(C):
                        bank = await_full(act, J, f"q{m}")
                        nc.scalar.activation(q1T[:, m, :], bank[:, 0:P], ACT.Identity, bias=col("l1_bq", m))\
                            .then_inc(q_free[J[f"q{m}"][0]], 1)
                    for n in range(4):
                        act_exp(act, n, bank_of(n)[1])
                    act_products(act, J, "pv", "l1_bv", slice(0, P))

                @block.gpsimd
                def _(pool):
                    link = chained(pool, M["pchain"])
                    if not last:
                        pool_pick(pool, link, g + 1)
                        await_full(pool, J, "hc1")
                        pool_copy(pool, g + 1)
                        pool_picked(pool, g + 1)
                    for n in range(4):
                        pool_scale(pool, n)
                    if not last:
                        await_full(pool, J, "xs")
                        pool_rows(pool, g + 1)

                @block.vector
                def _(dve):
                    link = chained(dve, M["chain"])
                    nc.vector.tensor_scalar(keep, place, TOPK - 0.5, None, ALU.is_gt)
                    for m in range(C):
                        dve_keys(dve, J, m, "l1_bk")
                    if not last:
                        dve_take(dve, g + 1)
                        dve_score(dve, link, g + 1)
                    dve_softmax(dve, 4, None)
                    if not last:
                        await_full(dve, J, "gt")
                        dve_choose(dve, link, J)
                    bank = await_full(dve, J, "y")
                    nc.vector.tensor_tensor(yo, bank[:, 0:D], row("l1_ob"), ALU.add).then_inc(q_free[J["y"][0]], 1)
                    for j in range(GB):
                        bank = await_full(dve, J, f"s{j}")
                        nc.vector.scalar_tensor_tensor(out=at(xres, g * GB + j), in0=at(xres, g * GB + j),
                                                       scalar=keep[:, j:j + 1], in1=bank[:, 0:D],
                                                       op0=ALU.mult, op1=ALU.add).then_inc(q_free[J[f"s{j}"][0]], 1)
            end_turn()

        with nc.Fori(0, G - 1) as g:
            best_tokens(g, False)
        best_tokens(G - 1, True)

        A4 = H // NKV
        turn2 = ["hx0", "hx1", "hc0", "hc1"]
        jobs = ["kA", "kB"] + [f"q{a}{h}" for a in range(A4) for h in "AB"] + ["v0", "v1"]
        jobs += [f"pv{j}_{q}" for j in range(GB) for q in range(2)]
        jobs += ["w0", "w1", "n0", "n1"] + [f"{x}{f}" for f in range(FC) for x in "gu"] + turn2 + ["d0", "d1"]
        J_l2, J_l2_first = Jobs(jobs), Jobs(turn2)
        scratch = [w_ca, w_l1]

        def products4(k, r):
            return scratch[r % 2][:, :, :].rearrange("p c n -> p (c n)")[:, k * NT:(k + 1) * NT]\
                .rearrange("p (j n) -> p j n", j=GB)

        def rms(pool, link, k, n_stats, js=slice(0, GB)):
            pool.wait_ge(M["stats"], n_stats)
            v = ve[:, k, js]
            link(nc.gpsimd.tensor_tensor(v, mv[:, k, js, 0], mv[:, k, js, 0], ALU.mult))
            link(nc.gpsimd.tensor_tensor(v, v, mv[:, k, js, 1], ALU.add))
            link(nc.gpsimd.tensor_scalar(v, v, RMS_EPS, 1.0, ALU.add, ALU.mult))
            nc.gpsimd.tensor_tensor(rstd[:, k, js], v, nhalf[:, js], ALU.pow).then_inc(M["rstd_ok"], 1)

        def scale_rows(dve, src, dst, g, k, ok, batches=range(GB)):
            for j in batches:
                nc.vector.tensor_scalar(dst[:, j, :], at(src, g * GB + j), rstd[:, k, j:j + 1], None,
                                        ALU.mult).then_inc(ok, 1)

        def dve_rms_group(dve, link, g, n_before):
            dve_stats(dve, link, xres, g, 0)
            dve_stats(dve, link, ctxr, g, 1)
            dve.wait_ge(M["rstd_ok"], n_before + 1)
            scale_rows(dve, xres, xn, g, 0, M["xn_ok"])
            dve.wait_ge(M["rstd_ok"], n_before + 2)
            scale_rows(dve, ctxr, cn, g, 1, M["cn_ok"])

        def act_rms_group(act, J):
            act_affine(act, J, ["hx0", "hx1"], hT, "ln1", None)
            act_affine(act, J, ["hc0", "hc1"], cT, "ln1", None)

        with nc.Block(no_gpsimd_drain=True) as block:
            @block.tensor
            def _(pe):
                pe_turn_rows(pe, J_l2_first, ["hx0", "hx1"], xn, M["xn_ok"])
                pe_turn_rows(pe, J_l2_first, ["hc0", "hc1"], cn, M["cn_ok"])

            @block.scalar
            def _(act):
                act_rms_group(act, J_l2_first)

            @block.gpsimd
            def _(pool):
                link = chained(pool, M["pchain"])
                rms(pool, link, 0, GB)
                rms(pool, link, 1, 2 * GB)

            @block.vector
            def _(dve):
                dve_rms_group(dve, chained(dve, M["chain"]), 0, 0)
        end_turn()

        with nc.Fori(0, G) as g:
            g_next = (g + 1) & (G - 1)
            with nc.Block(no_gpsimd_drain=True) as block:
                @block.tensor
                def _(pe):
                    J = J_l2
                    pe.wait_ge(ld["l2"], 16 * 6)
                    for h in range(2):
                        pe_project(pe, J, "k" + "AB"[h], wkv2, h * P, cT)
                    for a in range(A4):
                        for h in range(2):
                            pe_project(pe, J, f"q{a}" + "AB"[h], wq2, (2 * a + h) * P, hT)
                    def scores(j, a):
                        for h in range(2):
                            ins = nc.tensor.matmul(S[a][:, :], qr[:, a, h, j * P:(j + 1) * P],
                                                   kM2[:, :, h, j * P:(j + 1) * P], start=(h == 0), stop=(h == 1))
                        ins.then_inc(M["scored"], 1)

                    def products(j):
                        pe.wait_ge(M["pt_ok"], 4 * j + 4)
                        for q in range(2):
                            bank = claim(pe, J, f"pv{j}_{q}")
                            for half in range(2):
                                i = 2 * q + half
                                ins = nc.tensor.matmul(bank[half * HD:(half + 1) * HD, :], V2[:, j, i, :],
                                                       PT[:, j % 2, i::NKV, :],
                                                       start=True, stop=True)
                            ins.then_inc(q_full[J[f"pv{j}_{q}"][0]], 1)

                    pe_values(pe, J, ["v0", "v1"], wkv2, D, cT)
                    pe.wait_ge(M["keys_ok"], 2)
                    for a in range(A4):
                        pe.wait_ge(M["roped"], 2 * (a + 2))
                        scores(0, a)
                    for n in range(4 * GB + TURN_LAG):
                        if n + 4 < 4 * GB:
                            pe.wait_ge(M["masked"], n + 1)
                            scores(n // 4 + 1, n % 4)
                        m = n - TURN_LAG
                        if m >= 0:
                            pe_turn(pe, m)
                        if m == 4:
                            await_read(pe, J, "v0")
                            await_read(pe, J, "v1")
                        if m % 4 == 2 and m > 4:
                            products(m // 4 - 1)
                    products(GB - 1)
                    for j in range(GB):
                        await_read(pe, J, f"pv{j}_0")
                        await_read(pe, J, f"pv{j}_1")

                    def rows_out(names, w, src):
                        for y, name in enumerate(names):
                            bank = claim(pe, J, name)
                            for jj in range(2):
                                j = 2 * y + jj
                                for f in range(FC):
                                    ins = nc.tensor.matmul(bank[:, jj * D:(jj + 1) * D], src[:, f, j * P:(j + 1) * P],
                                                           w[:, f, :], start=(f == 0), stop=(f == FC - 1))
                            ins.then_inc(q_full[J[name][0]], 1)

                    rows_out(["w0", "w1"], wo2, o2T)
                    for c in range(C):
                        bank = claim(pe, J, f"n{c}")
                        for j in range(GB):
                            if c == 0:
                                pe.wait_ge(M["xn_ok"], j + 1)
                            ins = nc.tensor.transpose(bank[:, j * P:(j + 1) * P], xn2[:, j, c * P:(c + 1) * P], ident[:])
                        ins.then_inc(q_full[J[f"n{c}"][0]], 1)
                    await_read(pe, J, "n0")
                    await_read(pe, J, "n1")
                    for f in range(FC):
                        pe_project(pe, J, f"g{f}", wg2, f * P, hT)
                        pe_project(pe, J, f"u{f}", wu2, f * P, hT)
                    for src, ok, names, seen in ((xn, M["xn_ok"], ["hx0", "hx1"], GB), (cn, M["cn_ok"], ["hc0", "hc1"], 0)):
                        for c in range(C):
                            bank = claim(pe, J, names[c])
                            pe.wait_ge(ok, seen + GB)
                            for j in range(GB):
                                ins = nc.tensor.transpose(bank[:, j * P:(j + 1) * P], src[:, j, c * P:(c + 1) * P], ident[:])
                            ins.then_inc(q_full[J[names[c]][0]], 1)
                    for f in range(FC):
                        await_read(pe, J, f"u{f}")
                    rows_out(["d0", "d1"], wd2, act2)

                @block.scalar
                def _(act):
                    J = J_l2
                    def values():
                        for v in range(2):
                            bank = await_full(act, J, f"v{v}")
                            nc.scalar.activation(V2[:, 2 * v:2 * v + 2, :, :],
                                                 bank[:, :].rearrange("p (j h d) -> p j h d", j=2, d=HD), ACT.Copy)\
                                .then_inc(q_free[J[f"v{v}"][0]], 1)

                    def out_copies(j):
                        for q in range(2):
                            name = f"pv{j}_{q}"
                            bank = await_full(act, J, name)
                            nc.scalar.activation(o2T[:, 4 * q:4 * q + 4, j * P:(j + 1) * P],
                                                 bank[:, :].rearrange("p (f n) -> p f n", f=4), ACT.Copy)\
                                .then_inc(q_free[J[name][0]], 1)

                    for h in range(2):
                        act.wait_ge(M["roped"], h + 1)
                        for i in range(NKV):
                            ins = nc.scalar.activation(kM2[:, i, h, :], kr[:, h, :], ACT.Copy, scale=of_key_head[:, i:i + 1])
                        ins.then_inc(M["keys_ok"], 1)
                    values()
                    N, LAG = 4 * GB, COPY_LAG
                    for n in range(N + LAG):
                        if n < N:
                            act_exp(act, n, bank_of(n)[0])
                        if n >= LAG:
                            m = n - LAG
                            act.wait_ge(M["turned"], m + 1)
                            if m >= 8:
                                await_full(act, J, f"pv{m // 4 - 2}_1")
                            nc.scalar.activation(turned_tile(m), T[m % 2][:, :].rearrange("p (s q) -> p s q", q=P),
                                                 ACT.Copy).then_inc(M["pt_ok"], 1)
                        j = (n - 7 - LAG) // 4
                        if 0 <= j < GB - 1 and n == 4 * j + 7 + LAG:
                            out_copies(j)
                    out_copies(GB - 1)
                    for c in range(C):
                        bank = await_full(act, J, f"n{c}")
                        nc.scalar.activation(hT[:, c, :], bank[:, :], ACT.Identity, scale=col("ln2", c))\
                            .then_inc(q_free[J[f"n{c}"][0]], 1)
                    for f in range(FC):
                        bank = await_full(act, J, f"g{f}")
                        nc.scalar.activation(act2[:, f, :], bank[:, :], ACT.Silu).then_inc(q_free[J[f"g{f}"][0]], 1)
                    act_rms_group(act, J)

                @block.gpsimd
                def _(pool):
                    link = chained(pool, M["pchain"])
                    for r in range(1 + A4):
                        pool.wait_ge(M["multiplied"], 4 * (r + 1))
                        first, second = (kr[:, 0, :], kr[:, 1, :]) if r == 0 else (qr[:, r - 1, 0, :], qr[:, r - 1, 1, :])
                        for dst, k1, k2, op in ((first, 0, 1, ALU.subtract), (second, 2, 3, ALU.add)):
                            nc.gpsimd.tensor_tensor(dst.rearrange("p (j n) -> p j n", j=GB), products4(k1, r),
                                                    products4(k2, r), op).then_inc(M["roped"], 1)
                    for n in range(4 * GB):
                        pool_scale(pool, n)
                    for y in range(2):
                        rms(pool, link, 0, 2 * y + 2, slice(2 * y, 2 * y + 2))
                    rms(pool, link, 0, 2 * GB)
                    rms(pool, link, 1, 3 * GB)

                @block.vector
                def _(dve):
                    J = J_l2
                    link = chained(dve, M["chain"])

                    cos = rope[:, 0, :].unsqueeze(1).to_broadcast([P, GB, P])
                    sin = rope[:, 1, :].unsqueeze(1).to_broadcast([P, GB, P])
                    for r in range(1 + A4):
                        n = "k" if r == 0 else f"q{r - 1}"
                        if r >= 2:
                            dve.wait_ge(M["roped"], 2 * (r - 1))
                        for half, table in ((0, ((0, cos), (3, sin))), (1, ((1, sin), (2, cos)))):
                            bank = await_full(dve, J, n + "AB"[half])
                            for k, t in table:
                                nc.vector.tensor_tensor(products4(k, r), bank[:, :].rearrange("p (j n) -> p j n", j=GB),
                                                        t, ALU.mult).then_inc(M["multiplied"], 1)
                            dve.wait_ge(M["multiplied"], 4 * r + 2 * half + 2)
                            dve.sem_inc(q_free[J[n + "AB"[half]][0]], 1)

                    dve.wait_ge(ld["mask"], 16)
                    N = 4 * GB
                    for n in range(N + 2):
                        if n < N:
                            j = n // 4
                            dve.wait_ge(M["scored"], n + 1)
                            if n >= 8:
                                dve.wait_ge(M["turned"], n - 7)
                            nc.vector.scalar_tensor_tensor(
                                out=bank_of(n)[0], in0=bank_of(n)[1], scalar=HD ** -0.5,
                                in1=mask2[:, bass.ds(g * GB + j, 1), :].to_broadcast([P, A4, P]),
                                op0=ALU.mult, op1=ALU.add).then_inc(M["masked"], 1)
                            dve.wait_ge(M["masked"], n + 1)
                            nc.vector.tensor_reduce(cols_of(mx, n), bank_of(n)[0], AX, ALU.max, negate=True)\
                                .then_inc(M["maxed"], 1)
                        if n >= 2:
                            dve.wait_ge(M["probs"], n - 1)
                            nc.vector.reciprocal(cols_of(rden, n - 2), cols_of(psum, n - 2)).then_inc(M["divided"], 1)

                    def add_rows(names, y0=0):
                        for y, name in enumerate(names, y0):
                            bank = await_full(dve, J, name)
                            x2 = at(xres, g * GB + 2 * y, 2)
                            link(nc.vector.tensor_tensor(x2, bank[:, :].rearrange("p (j d) -> p j d", j=2), x2, ALU.add))
                            dve.sem_inc(q_free[J[name][0]], 1)

                    for y in range(2):
                        pair = range(2 * y, 2 * y + 2)
                        add_rows([f"w{y}"], y)
                        dve_stats(dve, link, xres, g, 0, pair)
                        dve.wait_ge(M["rstd_ok"], y + 1)
                        scale_rows(dve, xres, xn2, g, 0, M["xn_ok"], pair)
                    for f in range(FC):
                        await_read(dve, J, f"g{f}")
                        bank = await_full(dve, J, f"u{f}")
                        nc.vector.tensor_tensor(act2[:, f, :], bank[:, :], act2[:, f, :], ALU.mult)\
                            .then_inc(q_free[J[f"u{f}"][0]], 1)
                        if f == 1:
                            dve_stats(dve, link, xres, g_next, 0)
                        if f == 2:
                            dve_stats(dve, link, ctxr, g_next, 1)
                        if f == 4:
                            dve.wait_ge(M["rstd_ok"], 3)
                            scale_rows(dve, xres, xn, g_next, 0, M["xn_ok"])
                        if f == 5:
                            dve.wait_ge(M["rstd_ok"], 4)
                            scale_rows(dve, ctxr, cn, g_next, 1, M["cn_ok"])
                    add_rows(["d0", "d1"])
            end_turn()

        attention(("l3_g", "l3_b"), "raw", w_l3, "l3_bq", "l3_bk", "l3_bv", "l3_ob", ["l3"], store=True)
        with nc.Block(no_gpsimd_drain=True) as block:
            @block.sync
            def _(sp):
                sp.wait_ge(stored, 16 * G)


def shape_tables():
    d = np.arange(P) % HALF
    inv = (1.0 / np.float32(10000.0) ** (np.arange(0, HD, 2, dtype=np.float32) / np.float32(HD))).astype(np.float32)
    angle = np.arange(P, dtype=np.float32)[None, :] * inv[d][:, None]
    rope = np.stack([np.cos(angle), np.sin(angle)], axis=1).astype(np.float32)
    p = np.arange(P)
    of_four = ((p // DH) % 4)[:, None] == np.arange(4)[None]
    of_key_head = (p // HALF)[:, None] == np.arange(NKV)[None]
    before = p[None, :] < p[:, None]
    ranks = np.broadcast_to(np.where(np.arange(R) < TOPK, np.arange(R), -1)[None], (P, R))
    e = np.arange(E)
    ebefore = np.broadcast_to((e[None, :] < e[:, None]).reshape(1, E * E), (P, E * E))
    steps = np.broadcast_to(np.arange(NSTEP)[None] * BR, (P, NSTEP))
    block_ids = np.broadcast_to(np.arange(NBLK)[None], (P, NBLK))
    table = np.concatenate([of_four * DH ** -0.5, of_key_head, before, ranks, ebefore, steps, block_ids], axis=1).astype(np.float32)
    return rope, table


def lay_out(i):
    def chunks(v):
        return v.reshape(C, P).T

    def thirds(name, v):
        return [v[k * D:(k + 1) * D] for k in range(3)]

    L0, L1, L2, L3 = "L0_xattn_", "L1_xattn_", "L2_xattn_", "L3_xattn_"
    sq, sk, sv = thirds("sa", i[L0 + "sa_in_b"])
    cq, ck, cv = thirds("ca", i[L0 + "ca_in_b"])
    oq, ok, ov = thirds("l1", i[L1 + "in_proj_b"])
    vec = {"sa_g": i[L0 + "sa_ln_g"], "sa_b": i[L0 + "sa_ln_b"], "sa_bq": sq, "sa_bk": sk, "sa_bv": sv,
           "cq_g": i[L0 + "ca_q_ln_g"], "cq_b": i[L0 + "ca_q_ln_b"], "ck_g": i[L0 + "ca_kv_ln_g"],
           "ck_b": i[L0 + "ca_kv_ln_b"], "ca_bq": cq, "ca_bk": ck, "ca_bv": cv,
           "me_g": i[L0 + "moe_ln_g"], "me_b": i[L0 + "moe_ln_b"], "l1_bq": oq, "l1_bk": ok, "l1_bv": ov,
           "ln1": i[L2 + "ln1_w"], "ln2": i[L2 + "ln2_w"], "l3_g": i[L3 + "ln_gamma"], "l3_b": i[L3 + "ln_beta"],
           "l3_bq": i[L3 + "bq"], "l3_bk": i[L3 + "bk"], "l3_bv": i[L3 + "bv"]}
    rows = {"sa_ob": i[L0 + "sa_out_b"], "ca_ob": i[L0 + "ca_out_b"], "l1_ob": i[L1 + "out_b"], "l3_ob": i[L3 + "bo"],
            "l1_sw": i[L1 + "score_w"].reshape(D)}
    rope, table = shape_tables()
    cat = np.concatenate
    out = {
        "x": i["x"], "ctx": i["ctx_1024"], "mask": i["mask_Bx1xSxS2_ff0"].reshape(B, P, P),
        "cols": cat([chunks(vec[n]) for n in COLS], axis=1),
        "rows": np.broadcast_to(np.stack([rows[n] for n in ROWS])[None], (P, len(ROWS), D)),
        "fc1b": i[L0 + "e_fc1_b"].reshape(E * FC, P).T, "fc2b": i[L0 + "e_fc2_b"],
        "rw": i[L0 + "router_w"].T, "rb": np.broadcast_to(i[L0 + "router_b"].reshape(1, E), (P, E)),
        "sbias": np.broadcast_to(i[L1 + "score_b"].reshape(1, 1), (P, 1)),
        "rope": rope, "shape_c": table,
        "w_sa": cat([i[L0 + "sa_in_w"].T, i[L0 + "sa_out_w"].T], axis=1),
        "w_ca": cat([i[L0 + "ca_in_w"].T, i[L0 + "ca_out_w"].T], axis=1),
        "w_l1": cat([i[L1 + "in_proj_w"].T, i[L1 + "out_w"].T], axis=1),
        "w_l3": cat([i[L3 + n].T for n in ("Wq", "Wk", "Wv", "Wo")], axis=1),
        "fc1": i[L0 + "e_fc1_w"].transpose(0, 2, 1).reshape(E * D, FF),
        "fc2": i[L0 + "e_fc2_w"].transpose(0, 2, 1).reshape(E * FF, D),
        "wq2": i[L2 + "Wq"].reshape(D, NKV, H // NKV, 2, HALF).transpose(0, 2, 3, 1, 4).reshape(D, FF),
        "wkv2": cat([i[L2 + "Wk"].reshape(D, NKV, 2, HALF).transpose(0, 2, 1, 3).reshape(D, D), i[L2 + "Wv"]], axis=1),
        "wo2": i[L2 + "Wo"].reshape(2, 2, H // NKV, HD, D).transpose(0, 2, 1, 3, 4).reshape(FF, D),
        "wg2": i[L2 + "Wgate"], "wu2": i[L2 + "Wup"], "wd2": i[L2 + "Wdown"],
    }
    return {n: np.ascontiguousarray(a) for n, a in out.items()}


def kernel(**inputs):
    import concourse.bacc as bacc
    from concourse.bass_utils import run_bass_kernel_spmd

    arrays = lay_out({n: np.asarray(a) for n, a in inputs.items()})
    nc = bacc.Bacc("TRN2", target_bir_lowering=False, num_devices=1)
    aps = {n: nc.dram_tensor("in_" + n, a.shape, mybir.dt.from_np(a.dtype), kind="ExternalInput").ap()
           for n, a in arrays.items()}
    out = nc.dram_tensor("out", (B, P, D), F32, kind="ExternalOutput").ap()
    build(nc, aps, out)
    r = run_bass_kernel_spmd(nc, [{"in_" + n: a for n, a in arrays.items()}], core_ids=[0])
    return r.results[0]["out"]
```
